# Optimizing a Trainium2 kernel written in Bass

```python
import numpy as np
import jax
import jax.numpy as jnp

def _softmax(x, axis=-1):
    return jax.nn.softmax(x, axis=axis)

def _gelu(x):
    return jax.nn.gelu(x, approximate=True)

def _silu(x):
    return jax.nn.silu(x)

def _sigmoid(x):
    return jax.nn.sigmoid(x)

def _layernorm(x, axis=-1, eps=1e-05):
    m = jnp.mean(x, axis=axis, keepdims=True)
    v = jnp.var(x, axis=axis, keepdims=True)
    return (x - m) / jnp.sqrt(v + eps)

def _scatter_add(tgt, idx, src, axis=0):
    return tgt.at[idx].add(src)

def _segment_sum(src, seg, n):
    return jax.ops.segment_sum(src, seg, n)
kernel_name = 'mk_recurrent_d2_jaxref_r8_2ba5a2'

def setup_inputs(seed: int=0):
    np.random.seed(seed)
    _w = jnp.asarray

    def _L0_attn_setup():
        import jax, jax.numpy as jnp
        import numpy as np
        EMB = 128
        HEADS = 16
        HEAD_DIM = EMB // HEADS
        MAX_LEN = 125
        key = jax.random.key(seed)
        ks = jax.random.split(key, 11)
        s = 0.02
        x = jax.random.normal(ks[0], (4, 128, EMB), dtype=jnp.float32)
        Wq = jax.random.normal(ks[1], (EMB, EMB), dtype=jnp.float32) * s
        bq = jnp.zeros((EMB,), dtype=jnp.float32)
        Wk = jax.random.normal(ks[2], (EMB, EMB), dtype=jnp.float32) * s
        bk = jnp.zeros((EMB,), dtype=jnp.float32)
        Wv = jax.random.normal(ks[3], (EMB, EMB), dtype=jnp.float32) * s
        bv = jnp.zeros((EMB,), dtype=jnp.float32)
        Wp = jax.random.normal(ks[4], (EMB, EMB), dtype=jnp.float32) * s
        bp = jnp.zeros((EMB,), dtype=jnp.float32)
        bias_table = jax.random.normal(ks[5], (2 * MAX_LEN - 1, HEADS), dtype=jnp.float32) * 0.02
        temperature = jnp.ones((1,), dtype=jnp.float32)
        return {'x': x, 'Wq': Wq, 'bq': bq, 'Wk': Wk, 'bk': bk, 'Wv': Wv, 'bv': bv, 'Wp': Wp, 'bp': bp, 'bias_table': bias_table, 'temperature': temperature}
    _L0_attn_in = _L0_attn_setup()

    def _L0_ffn_setup():
        import jax, jax.numpy as jnp
        import numpy as np
        B, S, DIM = (2, 256, 128)
        HID = 256
        E, NSH, TOPK = (8, 2, 2)

        def _ffn(x, w1, w2, w3):
            return jax.nn.silu(x @ w1.T) * (x @ w3.T) @ w2.T
        key = jax.random.key(seed)
        ks = jax.random.split(key, 8)
        sc = 0.02
        return {'x': jax.random.normal(ks[0], (B, S, DIM), jnp.float32), 'router_w': jax.random.normal(ks[1], (E, DIM), jnp.float32) * sc, 'expert_bias': jnp.zeros((E,), jnp.float32), 'w1': jax.random.normal(ks[2], (E, HID, DIM), jnp.float32) * sc, 'w3': jax.random.normal(ks[3], (E, HID, DIM), jnp.float32) * sc, 'w2': jax.random.normal(ks[4], (E, DIM, HID), jnp.float32) * sc, 'sw1': jax.random.normal(ks[5], (NSH, HID, DIM), jnp.float32) * sc, 'sw3': jax.random.normal(ks[6], (NSH, HID, DIM), jnp.float32) * sc, 'sw2': jax.random.normal(ks[7], (NSH, DIM, HID), jnp.float32) * sc}
    _L0_ffn_in = _L0_ffn_setup()

    def _L1_attn_setup():
        import jax, jax.numpy as jnp
        import numpy as np
        D_MODEL = 128
        NUM_HEADS = 16
        B, S = (1, 512)
        key = jax.random.key(seed)
        kx, kq, kk, kv, ko = jax.random.split(key, 5)
        std = (1.0 / D_MODEL) ** 0.5

        def trunc(k):
            return std * jax.random.truncated_normal(k, -3.0, 3.0, (D_MODEL, D_MODEL), dtype=jnp.float32)
        return {'x': jax.random.normal(kx, (B, S, D_MODEL), dtype=jnp.float32), 'W_Q': trunc(kq), 'W_K': trunc(kk), 'W_V': trunc(kv), 'W_O': trunc(ko)}
    _L1_attn_in = _L1_attn_setup()

    def _L1_ffn_setup():
        import jax, jax.numpy as jnp
        import numpy as np
        B, T, C = (4, 256, 128)
        H = 128
        E_ATT = 8
        E_MOE = 8
        I = 128
        MIN_ATT = 2
        MIN_MOE = 2
        EPS_LN = 1e-05

        def _normalize(x, axis):
            n = jnp.linalg.norm(x, axis=axis, keepdims=True)
            return x / jnp.maximum(n, 1e-12)

        def _layernorm(x, w, b):
            m = jnp.mean(x, axis=-1, keepdims=True)
            v = jnp.mean(jnp.square(x - m), axis=-1, keepdims=True)
            return (x - m) / jnp.sqrt(v + EPS_LN) * w + b

        def _gating(flat_hs, sim, gates, min_experts):
            logits = _normalize(flat_hs, -1) @ _normalize(sim, 0) - jax.nn.sigmoid(gates)
            gated = jax.nn.relu(logits)
            mask = (gated > 0).astype(gated.dtype)
            inactive = jnp.sum(mask, axis=1) == 0
            _, idx = jax.lax.top_k(logits, min_experts)
            onehot = jnp.sum(jax.nn.one_hot(idx, logits.shape[-1], dtype=gated.dtype), axis=1)
            put = inactive[:, None] & (onehot > 0)
            mask = jnp.where(put, 1.0, mask)
            masked = jnp.where(mask > 0, gated, -jnp.inf)
            return jax.nn.softmax(masked, axis=-1)
        key = jax.random.key(seed)
        ks = jax.random.split(key, 12)
        d = {}
        d['x'] = jax.random.normal(ks[0], (B, T, C), dtype=jnp.float32)
        d['ln1_w'] = jnp.ones((C,), jnp.float32)
        d['ln1_b'] = jnp.zeros((C,), jnp.float32)
        d['ln2_w'] = jnp.ones((C,), jnp.float32)
        d['ln2_b'] = jnp.zeros((C,), jnp.float32)
        d['smha_sim'] = jax.random.normal(ks[1], (C, E_ATT), dtype=jnp.float32)
        d['smha_gates'] = jnp.zeros((E_ATT,), jnp.float32)
        sq = 1.0 / np.sqrt(C + H)
        d['q_proj'] = jax.random.normal(ks[2], (E_ATT, C, H), dtype=jnp.float32) * sq
        d['k_proj'] = jax.random.normal(ks[3], (E_ATT, C, H), dtype=jnp.float32) * sq
        d['v_proj'] = jax.random.normal(ks[4], (E_ATT, C, H), dtype=jnp.float32) * sq
        d['o_proj'] = jax.random.normal(ks[5], (E_ATT, H, C), dtype=jnp.float32) * sq
        d['moe_sim'] = jax.random.normal(ks[6], (C, E_MOE), dtype=jnp.float32)
        d['moe_gates'] = jnp.zeros((E_MOE,), jnp.float32)
        d['w1'] = jax.random.normal(ks[7], (E_MOE, C, I), dtype=jnp.float32) * (1.0 / np.sqrt(C))
        d['w2'] = jax.random.normal(ks[8], (E_MOE, I, C), dtype=jnp.float32) * (1.0 / np.sqrt(I))
        return d
    _L1_ffn_in = _L1_ffn_setup()
    _d = {'L0_attn_x': _L0_attn_in['x'], 'L0_attn_Wq': _L0_attn_in['Wq'], 'L0_attn_bq': _L0_attn_in['bq'], 'L0_attn_Wk': _L0_attn_in['Wk'], 'L0_attn_bk': _L0_attn_in['bk'], 'L0_attn_Wv': _L0_attn_in['Wv'], 'L0_attn_bv': _L0_attn_in['bv'], 'L0_attn_Wp': _L0_attn_in['Wp'], 'L0_attn_bp': _L0_attn_in['bp'], 'L0_attn_bias_table': _L0_attn_in['bias_table'], 'L0_attn_temperature': _L0_attn_in['temperature'], 'L0_ffn_router_w': _L0_ffn_in['router_w'], 'L0_ffn_expert_bias': _L0_ffn_in['expert_bias'], 'L0_ffn_w1': _L0_ffn_in['w1'], 'L0_ffn_w3': _L0_ffn_in['w3'], 'L0_ffn_w2': _L0_ffn_in['w2'], 'L0_ffn_sw1': _L0_ffn_in['sw1'], 'L0_ffn_sw3': _L0_ffn_in['sw3'], 'L0_ffn_sw2': _L0_ffn_in['sw2'], 'L1_attn_W_Q': _L1_attn_in['W_Q'], 'L1_attn_W_K': _L1_attn_in['W_K'], 'L1_attn_W_V': _L1_attn_in['W_V'], 'L1_attn_W_O': _L1_attn_in['W_O'], 'L1_ffn_ln1_w': _L1_ffn_in['ln1_w'], 'L1_ffn_ln1_b': _L1_ffn_in['ln1_b'], 'L1_ffn_ln2_w': _L1_ffn_in['ln2_w'], 'L1_ffn_ln2_b': _L1_ffn_in['ln2_b'], 'L1_ffn_smha_sim': _L1_ffn_in['smha_sim'], 'L1_ffn_smha_gates': _L1_ffn_in['smha_gates'], 'L1_ffn_q_proj': _L1_ffn_in['q_proj'], 'L1_ffn_k_proj': _L1_ffn_in['k_proj'], 'L1_ffn_v_proj': _L1_ffn_in['v_proj'], 'L1_ffn_o_proj': _L1_ffn_in['o_proj'], 'L1_ffn_moe_sim': _L1_ffn_in['moe_sim'], 'L1_ffn_moe_gates': _L1_ffn_in['moe_gates'], 'L1_ffn_w1': _L1_ffn_in['w1'], 'L1_ffn_w2': _L1_ffn_in['w2']}
    _x0 = _d['L0_attn_x']
    _d['L0_attn_x'] = jax.random.normal(jax.random.fold_in(jax.random.key(seed), 1), (2, 1024, 128), dtype=_x0.dtype)
    del _x0
    return _d

def reference(L0_attn_x, L0_attn_Wq, L0_attn_bq, L0_attn_Wk, L0_attn_bk, L0_attn_Wv, L0_attn_bv, L0_attn_Wp, L0_attn_bp, L0_attn_bias_table, L0_attn_temperature, L0_ffn_router_w, L0_ffn_expert_bias, L0_ffn_w1, L0_ffn_w3, L0_ffn_w2, L0_ffn_sw1, L0_ffn_sw3, L0_ffn_sw2, L1_attn_W_Q, L1_attn_W_K, L1_attn_W_V, L1_attn_W_O, L1_ffn_ln1_w, L1_ffn_ln1_b, L1_ffn_ln2_w, L1_ffn_ln2_b, L1_ffn_smha_sim, L1_ffn_smha_gates, L1_ffn_q_proj, L1_ffn_k_proj, L1_ffn_v_proj, L1_ffn_o_proj, L1_ffn_moe_sim, L1_ffn_moe_gates, L1_ffn_w1, L1_ffn_w2):

    def _L0_attn_ref(x, Wq, bq, Wk, bk, Wv, bv, Wp, bp, bias_table, temperature):
        import jax, jax.numpy as jnp
        import numpy as np
        EMB = 128
        HEADS = 16
        HEAD_DIM = EMB // HEADS
        MAX_LEN = 125
        B, N, C = x.shape
        H, D = (HEADS, C // HEADS)

        def split_heads(t):
            return t.reshape(B, N, H, D).transpose(0, 2, 1, 3)
        q = split_heads(x @ Wq + bq)
        k = split_heads(x @ Wk + bk)
        v = split_heads(x @ Wv + bv)
        energy = jnp.einsum('bhqd,bhkd->bhqk', q, k)
        pos = jnp.arange(N)
        rel = pos[:, None] - pos[None, :] + (N - 1)
        rel = jnp.clip(rel, 0, bias_table.shape[0] - 1)
        bias = bias_table[rel].transpose(2, 0, 1)
        energy = energy + bias[None]
        scaling = jnp.sqrt(jnp.float32(C))
        temp = jnp.clip(temperature[0], 0.1, 10.0)
        att = jax.nn.softmax(energy / (scaling * temp), axis=-1)
        out = jnp.einsum('bhqk,bhkd->bhqd', att, v)
        out = out.transpose(0, 2, 1, 3).reshape(B, N, C)
        return out @ Wp + bp

    def _L0_ffn_ref(x, router_w, expert_bias, w1, w3, w2, sw1, sw3, sw2):
        import jax, jax.numpy as jnp
        import numpy as np
        B, S, DIM = (2, 256, 128)
        HID = 256
        E, NSH, TOPK = (8, 2, 2)

        def _ffn(x, w1, w2, w3):
            return jax.nn.silu(x @ w1.T) * (x @ w3.T) @ w2.T
        bs, sl, d = x.shape
        xf = x.reshape(-1, d)
        shared = jnp.zeros_like(xf)
        for i in range(sw1.shape[0]):
            shared = shared + _ffn(xf, sw1[i], sw2[i], sw3[i])
        logits = xf @ router_w.T + expert_bias
        rw, sel = jax.lax.top_k(logits, TOPK)
        rw = jax.nn.softmax(rw.astype(jnp.float32), axis=-1).astype(x.dtype)
        onehot = jax.nn.one_hot(sel, E, dtype=x.dtype)
        combine = jnp.einsum('tk,tke->te', rw, onehot)

        def body(acc, ew):
            e1, e3, e2, cw = ew
            acc = acc + cw[:, None] * _ffn(xf, e1, e2, e3)
            return (acc, None)
        out, _ = jax.lax.scan(body, jnp.zeros_like(xf), (w1, w3, w2, combine.T))
        out = out + shared
        return out.reshape(bs, sl, -1)

    def _L1_attn_ref(x, W_Q, W_K, W_V, W_O):
        import jax, jax.numpy as jnp
        import numpy as np
        D_MODEL = 128
        NUM_HEADS = 16
        B, S = (1, 512)
        Bx, Sx, Dm = x.shape
        H = NUM_HEADS
        d_attn = Dm // H
        Q = x @ W_Q.T
        K = x @ W_K.T
        V = x @ W_V.T
        Q = Q.reshape(Bx, Sx, H, d_attn).transpose(0, 2, 1, 3)
        K = K.reshape(Bx, Sx, H, d_attn).transpose(0, 2, 1, 3)
        V = V.reshape(Bx, Sx, H, d_attn).transpose(0, 2, 1, 3)
        scale = 1.0 / jnp.sqrt(jnp.asarray(d_attn, dtype=x.dtype))
        attn = jnp.einsum('bhqd,bhkd->bhqk', Q, K) * scale
        causal = jnp.tril(jnp.ones((Sx, Sx), dtype=bool))
        attn = jnp.where(causal, attn, jnp.asarray(-jnp.inf, dtype=attn.dtype))
        probs = jax.nn.softmax(attn, axis=-1)
        y = jnp.einsum('bhqk,bhkd->bhqd', probs, V)
        y = y.transpose(0, 2, 1, 3).reshape(Bx, Sx, Dm)
        return y @ W_O.T

    def _L1_ffn_ref(x, ln1_w, ln1_b, ln2_w, ln2_b, smha_sim, smha_gates, q_proj, k_proj, v_proj, o_proj, moe_sim, moe_gates, w1, w2):
        import jax, jax.numpy as jnp
        import numpy as np
        B, T, C = (4, 256, 128)
        H = 128
        E_ATT = 8
        E_MOE = 8
        I = 128
        MIN_ATT = 2
        MIN_MOE = 2
        EPS_LN = 1e-05

        def _normalize(x, axis):
            n = jnp.linalg.norm(x, axis=axis, keepdims=True)
            return x / jnp.maximum(n, 1e-12)

        def _layernorm(x, w, b):
            m = jnp.mean(x, axis=-1, keepdims=True)
            v = jnp.mean(jnp.square(x - m), axis=-1, keepdims=True)
            return (x - m) / jnp.sqrt(v + EPS_LN) * w + b

        def _gating(flat_hs, sim, gates, min_experts):
            logits = _normalize(flat_hs, -1) @ _normalize(sim, 0) - jax.nn.sigmoid(gates)
            gated = jax.nn.relu(logits)
            mask = (gated > 0).astype(gated.dtype)
            inactive = jnp.sum(mask, axis=1) == 0
            _, idx = jax.lax.top_k(logits, min_experts)
            onehot = jnp.sum(jax.nn.one_hot(idx, logits.shape[-1], dtype=gated.dtype), axis=1)
            put = inactive[:, None] & (onehot > 0)
            mask = jnp.where(put, 1.0, mask)
            masked = jnp.where(mask > 0, gated, -jnp.inf)
            return jax.nn.softmax(masked, axis=-1)
        b, t, c = x.shape
        n1 = _layernorm(x, ln1_w, ln1_b)
        rw = _gating(n1.reshape(b * t, c), smha_sim, smha_gates, MIN_ATT).reshape(b, t, -1)
        q = jnp.einsum('btc,ech,bte->bth', n1, q_proj, rw)
        k = jnp.einsum('btc,ech,bte->bth', n1, k_proj, rw)
        v = jnp.einsum('btc,ech,bte->bth', n1, v_proj, rw)
        scale = 1.0 / jnp.sqrt(jnp.asarray(q.shape[-1], q.dtype))
        scores = jnp.einsum('bth,bsh->bts', q, k) * scale
        causal = jnp.tril(jnp.ones((t, t), dtype=bool))
        scores = jnp.where(causal, scores, -jnp.inf)
        attn = jnp.einsum('bts,bsh->bth', jax.nn.softmax(scores, axis=-1), v)
        attn_out = jnp.einsum('bth,ehc,bte->btc', attn, o_proj, rw)
        hs = x + attn_out
        n2 = _layernorm(hs, ln2_w, ln2_b)
        rw2 = _gating(n2.reshape(b * t, c), moe_sim, moe_gates, MIN_MOE).reshape(b, t, -1)
        inter = jax.nn.gelu(jnp.einsum('btc,eci->btei', n2, w1), approximate=False)
        moe_out = jnp.einsum('btei,eic,bte->btc', inter, w2, rw2)
        return hs + moe_out
    x = L0_attn_x
    xn = _layernorm(x, axis=-1)
    s = _L0_attn_ref(xn, L0_attn_Wq, L0_attn_bq, L0_attn_Wk, L0_attn_bk, L0_attn_Wv, L0_attn_bv, L0_attn_Wp, L0_attn_bp, L0_attn_bias_table, L0_attn_temperature)
    g = _silu(_L0_ffn_ref(xn, L0_ffn_router_w, L0_ffn_expert_bias, L0_ffn_w1, L0_ffn_w3, L0_ffn_w2, L0_ffn_sw1, L0_ffn_sw3, L0_ffn_sw2))
    x = x + s * g
    xn = _layernorm(x, axis=-1)
    s = _L1_attn_ref(xn, L1_attn_W_Q, L1_attn_W_K, L1_attn_W_V, L1_attn_W_O)
    g = _silu(_L1_ffn_ref(xn, L1_ffn_ln1_w, L1_ffn_ln1_b, L1_ffn_ln2_w, L1_ffn_ln2_b, L1_ffn_smha_sim, L1_ffn_smha_gates, L1_ffn_q_proj, L1_ffn_k_proj, L1_ffn_v_proj, L1_ffn_o_proj, L1_ffn_moe_sim, L1_ffn_moe_gates, L1_ffn_w1, L1_ffn_w2))
    x = x + s * g
    return x

_drawn_inputs = setup_inputs


def setup_inputs(seed=0):
    import zlib

    import numpy as np

    out = dict(_drawn_inputs(seed))
    spreads = {'L0_attn_bq': (0.0, 0.8),
     'L0_attn_bk': (0.0, 2.0),
     'L0_attn_bv': (0.0, 0.8),
     'L0_attn_bp': (0.0, 0.8),
     'L0_ffn_expert_bias': (0.0, 0.8),
     'L1_ffn_ln1_w': (1.0, 0.6),
     'L1_ffn_ln1_b': (0.0, 0.632),
     'L1_ffn_ln2_w': (1.0, 0.6),
     'L1_ffn_ln2_b': (0.0, 2.0),
     'L1_ffn_smha_gates': (0.0, 0.8),
     'L1_ffn_moe_gates': (0.0, 1.008)}
    factors = {'L0_attn_Wq': 8.0,
     'L0_attn_Wk': 8.0,
     'L0_attn_Wv': 8.0,
     'L0_attn_Wp': 8.0,
     'L0_attn_bias_table': 200.0,
     'L0_ffn_router_w': 8.0,
     'L0_ffn_w1': 8.0,
     'L0_ffn_w3': 8.0,
     'L0_ffn_w2': 8.0,
     'L0_ffn_sw1': 8.0,
     'L0_ffn_sw3': 8.0,
     'L0_ffn_sw2': 8.0,
     'L1_ffn_smha_sim': 3.901,
     'L1_ffn_q_proj': 8.0,
     'L1_ffn_k_proj': 8.0,
     'L1_ffn_v_proj': 3.978,
     'L1_ffn_o_proj': 4.038}
    for name, (base, spread) in spreads.items():
        noise = np.random.default_rng([zlib.crc32(name.encode()), seed]).standard_normal(out[name].shape)
        drawn = base * np.exp(spread * noise) if base else spread * noise
        out[name] = jnp.asarray(drawn.astype(out[name].dtype))
    for name, factor in factors.items():
        out[name] = (out[name] * factor).astype(out[name].dtype)
    return out
```

```python
import math
from contextlib import ExitStack

import concourse.bass as bass
from concourse import mybir

F32 = mybir.dt.float32
BF16 = mybir.dt.bfloat16
ALU = mybir.AluOpType
ACT = mybir.ActivationFunctionType
AX = mybir.AxisListType

P = 128
C = 128
BATCH, SEQ = 2, 1024
TOK = BATCH * SEQ
NT = TOK // P
NC = TOK // 512
HEADS, HD = 16, 8
HG = 4
NG = HEADS // HG
GROUPS = BATCH * NG
KT = SEQ // P
PARTS = 3
STACK = PARTS * PARTS * HD
HID = 256
EXP = 8
FFN_SEQ = EXP + 2
REL = 249
DREV = 384
NEG = -1.0e30
LN_EPS = 1e-5


class Chain:

    def __init__(self, eng, sem):
        self.eng, self.sem, self.n, self.term = eng, sem, 0, 0

    def link(self, ins):
        self.n += 1
        ins.then_inc(self.sem, 1)
        self.eng.wait_ge(self.sem, self.term + self.n)

    def enter(self, it, per):
        self.start, self.per, self.term = self.n, per, it * per

    def leave(self, iters):
        assert self.n - self.start == self.per, (self.n - self.start, self.per)
        self.n, self.term = self.start + self.per * iters, 0


def t_steps(layer):
    if layer == 0:
        return [(h, k, 0) for h in range(2) for k in range(KT)]
    return [(h, k, max(0, k - 4 * h) * P) for h in range(2) for k in range(4 * h + 4)]


def s_units(layer):
    order = list(range(2, KT)) + [0, 1]
    return [(j, q, SEQ if layer == 0 else (q + 1) * P) for q in order for j in range(HG)]


def ring_plan(layer, carry, s_phase, t_phase):
    steps = t_steps(layer)
    n = len(steps)
    plan = [[] for _ in range(n)]
    first_of_half1 = next(i for i, s in enumerate(steps) if s[0] == 1)
    if carry:
        plan[3].append(("Q", 1))
        plan[5].append(("R", 1))
    if t_phase:
        plan[first_of_half1 + 3].append(("Q", 0))
        plan[first_of_half1 + 5].append(("R", 0))
    if s_phase:
        units = s_units(layer)
        span = n - 2 if t_phase else n
        total, done, at = sum(u[2] for u in units), 0, 0
        for u in units:
            while at < span - 1 and done >= total * (at + 1) / span:
                at += 1
            plan[at].append(("S", u))
            done += u[2]
        plan[span if t_phase else span - 1].append(("M",))
    return plan


def block_net(nc, a, out):
    ctx = ExitStack()
    with ctx:
        def sb(name, shape, dt=F32):
            return ctx.enter_context(nc.sbuf_tensor(name, shape, dt))

        def sem(name):
            return ctx.enter_context(nc.semaphore(name))

        def dram(name, shape, dt):
            return nc.dram_tensor(name, shape, dt).ap()

        q_dram = [dram(f"q_dram{l}", (GROUPS, HG, PARTS + 2, HD, SEQ), BF16) for l in range(2)]
        k_dram = [dram(f"k_dram{l}", (GROUPS, HG, PARTS, HD, SEQ), BF16) for l in range(2)]
        drev_dram = dram("drev_dram", (GROUPS, HG, PARTS, DREV), BF16)
        comb_dram = [dram(f"comb_dram{n}", (P, P), F32) for n in range(3)]

        PS = ctx.enter_context(nc.psum_tensor("PS", [P, 8 * 512], F32))

        def bank(n, lo=0, hi=512):
            return PS[:, n * 512 + lo:n * 512 + hi]

        xT = sb("xT", [P, TOK])
        xnT = sb("xnT", [P, TOK])
        n1T = sb("n1T", [P, TOK])
        ident = sb("ident", [P, P])
        ones = sb("ones", [P, P])
        sel = sb("sel", [P, P])
        identb = sb("identb", [P, P], BF16)
        flip = sb("flip", [P, P], BF16)
        mask_kq = sb("mask_kq", [P, P], BF16)
        mask_qk = sb("mask_qk", [P, P], BF16)
        tri = sb("tri", [P, EXP, EXP])
        wq = sb("wq", [P, 2, C])
        wk = sb("wk", [P, 2, C])
        wv = sb("wv", [P, 2, C])
        wo = sb("wo", [P, 2, NG, C])
        router = sb("router", [P, 3, EXP])
        simsq = sb("simsq", [P, 2, EXP])
        cols = sb("cols", [P, 10])
        bvb = sb("bvb", [P, C])
        erow = sb("erow", [P, 3, EXP])
        small = sb("small", [P, 10, NT])
        gl = sb("gl", [P, 3, 160])
        combT = sb("combT", [P, P])
        mx = sb("mx", [P, HG * KT])
        sums = sb("sums", [P, 2, 16])
        rsums = sb("rsums", [P, 2, 16])
        mres = sb("mres", [HG * KT, P])
        mrow = sb("mrow", [HG * KT, PARTS, P], BF16)
        fw = sb("fw", [P, 6 * 1024])
        arena = sb("arena", [P, 144 * 256])

        def at(kib, size):
            return arena[:, kib * 256:(kib + size) * 256]

        def bf(kib, size):
            return at(kib, size).bitcast(BF16)

        stack = {n: bf(k, 16).rearrange("p (s j t) -> p s j t", s=2, j=HG)
                 for n, k in (("Sq", 0), ("Sk", 16), ("Tq", 32), ("Tk", 48))}
        V = at(64, 8).rearrange("p (g k c) -> p g k c", g=GROUPS, k=KT)
        sT1 = at(64, 8)
        Vst = at(72, 8).rearrange("p (s k j c) -> p s k j c", s=2, k=KT, j=HG)
        Pr = at(80, 16).rearrange("p (s q) -> p s q", s=8)
        Osb = at(96, 4).rearrange("p (s q) -> p s q", s=2)
        OT = at(100, 32).rearrange("p (g q) -> p g q", g=GROUPS)
        Hst = bf(132, 12).rearrange("p (s j a c) -> p s j a c", s=2, j=HG, a=PARTS)
        xtok = at(32, 8).rearrange("p (t c) -> p t c", t=NT)
        ztok = at(40, 8).rearrange("p (t c) -> p t c", t=NT)
        zz = at(48, 8).rearrange("p (t c) -> p t c", t=NT)
        cmp_a = at(56, 4).rearrange("p (t e f) -> p t e f", t=NT, e=EXP)
        cmp_b = at(60, 4).rearrange("p (t e f) -> p t e f", t=NT, e=EXP)
        q32, k32 = at(80, 8), at(88, 8)
        qsp = bf(100, 12).rearrange("p (a t) -> p a t", a=PARTS)
        ksp = bf(112, 12).rearrange("p (a t) -> p a t", a=PARTS)
        gate_tmp = at(129, 3)
        lg, top2, act_mask, gated = (gate_tmp[:, n * 128:(n + 1) * 128].rearrange("p (t e) -> p t e", e=EXP) for n in range(4))
        comb = gate_tmp[:, 512:640].rearrange("p (e t) -> p e t", e=EXP)
        stats = gate_tmp[:, 640:736].rearrange("p (t n) -> p t n", t=NT)
        tblr = at(124, 5)[0:HEADS, 0:REL]
        dfull = at(124, 5)[0:HEADS, 256:256 + DREV]
        dpart = at(124, 5)[0:HEADS, 640:1216].bitcast(BF16).rearrange("h (a n) -> h a n", a=PARTS)
        cwb = at(100, 16).rearrange("p (s t) -> p s t", s=2)
        fw0 = fw[:, 0:1536].rearrange("p (s n) -> p s n", s=2)
        fa = fw[:, 2048:3072].rearrange("p (s n) -> p s n", s=2)
        fg = fw[:, 3072:5120].rearrange("p (s n) -> p s n", s=4)
        fwq, fwk, fwv, fwo, fw1, fw2 = (fw[:, n * 1024:(n + 1) * 1024].rearrange("p (e c) -> p e c", e=EXP)
                                        for n in range(6))
        rwb = at(0, 64).rearrange("p (e t) -> p e t", e=EXP)
        Xe = at(80, 8).rearrange("p (s t) -> p s t", s=2)
        P1 = at(88, 8).rearrange("p (s t) -> p s t", s=2)
        vtok = at(72, 4).rearrange("p (k c) -> p k c", k=KT)
        qT, kT, vT = at(100, 4), at(104, 4), at(108, 4)
        attnT = at(112, 8)
        hsT = at(120, 8)
        PT = at(128, 16).rearrange("p (k q) -> p k q", k=KT)
        ga = at(80, 8).rearrange("p (s t) -> p s t", s=4)
        gg = at(88, 8).rearrange("p (s t) -> p s t", s=4)
        otok = at(100, 8).rearrange("p (t c) -> p t c", t=NT)

        bq, bk, bp = cols[:, 0:1], cols[:, 1:2], cols[:, 2:3]
        ln_w = [cols[:, 3:4], cols[:, 5:6]]
        ln_b = [cols[:, 4:5], cols[:, 6:7]]
        temp, qscale = cols[:, 7:8], cols[:, 8:9]

        x_in = [sem(f"x_in{c}") for c in range(NC)]
        w_in, fw_in, tbl_in = sem("w_in"), sem("fw_in"), sem("tbl_in")
        zero_done, const_done = sem("zero_done"), sem("const_done")
        dve_own, act_own, pool_own = sem("dve_own"), sem("act_own"), sem("pool_own")
        var_ready, rstd_ready = sem("var_ready"), sem("rstd_ready")
        z_ready = sem("z_ready")
        ss_ready, norm_ready = sem("ss_ready"), sem("norm_ready")
        tr_ps, tr_ev = sem("tr_ps"), sem("tr_ev")
        q_ps, k_ps, v_ps = sem("q_ps"), sem("k_ps"), sem("v_ps")
        q_ev, k_ev, v_ev = sem("q_ev"), sem("k_ev"), sem("v_ev")
        hi_done, rest_done, mid_done, split_done = sem("hi_done"), sem("rest_done"), sem("mid_done"), sem("split_done")
        qk_stored = [sem(f"qk_stored{l}") for l in range(2)]
        drev_ready, drev_stored = sem("drev_ready"), sem("drev_stored")
        lg_ps, gx_ready, ge_ready, comb_ready, cb_ps, cb_ev = (sem(n) for n in (
            "lg_ps", "gx_ready", "ge_ready", "comb_ready", "cb_ps", "cb_ev"))
        comb_stored = sem("comb_stored")
        sq_ready, gate_exp, gneg = sem("sq_ready"), sem("gate_exp"), sem("gneg")
        f_w = [sem(f"f_w{s}") for s in range(2)]
        f_c = [sem(f"f_c{s}") for s in range(2)]
        h_ps, a_made, g_made, y_done, y_ev = (sem(n) for n in ("h_ps", "a_made", "g_made", "y_done", "y_ev"))
        att = [{n: sem(f"{n}{l}") for n in (
            "ones_set", "s_ld0", "s_ld1", "t_ld0", "t_ld1", "h_ld0", "h_ld1", "m_ld",
            "ring_full", "ring_free", "st_ps", "e_done", "av_done", "o_ev", "m_ready", "v_staged", "sum_in0", "sum_in1", "sum_inv", "rrow_in", "pj_ps", "pj_ev")}
            for l in range(2)]
        rw_in, rw2_in = sem("rw_in"), sem("rw2_in")
        x_made, x_used, x_ev, vt_ps, vt_ev = (sem(n) for n in ("x_made", "x_used", "x_ev", "vt_ps", "vt_ev"))
        s1_ps, s1_max, s1_exp, s1_p, pt_ps, pt_ev, o1_ps, o1_ev = (sem(n) for n in (
            "s1_ps", "s1_max", "s1_exp", "s1_p", "pt_ps", "pt_ev", "o1_ps", "o1_ev"))
        ox_made, ox_used, hs_ev = sem("ox_made"), sem("ox_used"), sem("hs_ev")
        i_ps, i_gelu, i_g, i_used, moe_ps, moe_ev = (sem(n) for n in ("i_ps", "i_gelu", "i_g", "i_used", "moe_ps", "moe_ev"))
        fin_silu, fin_x, fin_ps, fin_ev, stored = (sem(n) for n in ("fin_silu", "fin_x", "fin_ps", "fin_ev", "stored"))

        W_LOADS = 28
        NS = [len(t_steps(l)) for l in range(2)]

        UNITS = len(s_units(0)) + 1

        def ring_base(G):
            return UNITS if isinstance(G, int) and G == 0 else (G - 1) * (UNITS + 2) + (2 * UNITS + 1)

        def ring_after_s(G):
            return UNITS if isinstance(G, int) and G == 0 else (G - 1) * (UNITS + 2) + (2 * UNITS + 1)

        def groups(eng, body, chain=None, per=0):
            body(0, 0, False, True)
            with eng.Fori(0, 3) as it:
                if chain:
                    chain.enter(it, per)
                body(it * 2 + 1, 1, True, True)
                body(it * 2 + 2, 0, True, True)
            if chain:
                chain.leave(3)
            body(GROUPS - 1, 1, True, False)

        block = ctx.enter_context(nc.Block())

        @block.sync
        def _(sp):
            x_v = a["L0_attn_x"].rearrange("b (t p) c -> p (b t) c", p=P)
            for c in range(NC):
                sp.dma_start(xtok[:, 4 * c:4 * c + 4, :], x_v[:, 4 * c:4 * c + 4, :]).then_inc(x_in[c], 16)
            n = 0
            sp.wait_ge(zero_done, 1)
            for l in range(2):
                for dst, src in ((wq, ("L0_attn_Wq", "L1_WQT")), (wk, ("L0_attn_Wk", "L1_WKT")), (wv, ("L0_attn_Wv", "L1_WVT"))):
                    sp.dma_start(dst[:, l, :], a[src[l]]).then_inc(w_in, 16)
                    n += 1
                w_v = a[("L0_attn_Wp", "L1_WOT")[l]].rearrange("(g j d) c -> j d g c", g=NG, j=HG)
                for j in range(HG):
                    sp.dma_start(wo[32 * j:32 * j + HD, l, :, :], w_v[j]).then_inc(w_in, 16)
                    n += 1
            for k, name in enumerate(("router_T", "L1_ffn_smha_sim", "L1_ffn_moe_sim")):
                sp.dma_start(router[:, k, :], a[name]).then_inc(w_in, 16)
                n += 1
            for k, name in enumerate(("L0_ffn_expert_bias", "L1_ffn_smha_gates", "L1_ffn_moe_gates")):
                sp.dma_start(erow[:, k, :], a[name].partition_broadcast(P)).then_inc(w_in, 16)
                n += 1
            for k, name in enumerate(("L0_attn_bq", "L0_attn_bk", "L0_attn_bp", "L1_ffn_ln1_w", "L1_ffn_ln1_b",
                                      "L1_ffn_ln2_w", "L1_ffn_ln2_b")):
                sp.dma_start(cols[:, k:k + 1], a[name].rearrange("(p a) -> p a", a=1)).then_inc(w_in, 16)
                n += 1
            sp.dma_start(temp, a["L0_attn_temperature"].partition_broadcast(P)).then_inc(w_in, 16)
            sp.dma_start(bvb[:, :], a["L0_attn_bv"].partition_broadcast(P)).then_inc(w_in, 16)
            n += 2
            assert n == W_LOADS + 1, n
            sp.dma_start(tblr[:, :], a["bias_rev_T"]).then_inc(tbl_in, 16)
            for s in range(2):
                sp.dma_start(fw0[:, s, 0:768], a["ffn_w"][s]).then_inc(f_w[s], 16)

            def store_qk(l):
                for which, sp32, dr, order in ((0, qsp, q_dram[l], (0, 1, 2, 0, 1)), (1, ksp, k_dram[l], (0, 1, 2))):
                    sp.wait_ge(split_done, 2 * l + which + 1)
                    for n_, part in enumerate(order):
                        for b in range(BATCH):
                            dst = dr[b * NG:(b + 1) * NG, :, n_, :, :].rearrange("g j d t -> (g j) d t")
                            sp.dma_start(dst, sp32[:, part, b * SEQ:(b + 1) * SEQ]).then_inc(qk_stored[l], 16)

            def load_stack(l, which, G, parity):
                ld = att[l][f"{which.lower()}_ld{parity}"]
                for j in range(HG):
                    for name, dr, np_, step in (("q", q_dram[l], PARTS + 2, 1), ("k", k_dram[l], PARTS, 0)):
                        src = bass.AP(tensor=dr.tensor, offset=G * (HG * np_ * HD * SEQ) + j * np_ * HD * SEQ,
                                      ap=[[step * HD * SEQ, PARTS], [SEQ, PARTS * HD], [1, SEQ]])
                        sp.dma_start(stack[which + name][0:STACK, parity, j, :], src).then_inc(ld, 16)

            def load_bias(G, parity):
                for j in range(HG):
                    src = bass.AP(tensor=drev_dram.tensor, offset=G * (HG * PARTS * DREV) + j * PARTS * DREV,
                                  ap=[[1, P], [DREV, PARTS], [1, 256]])
                    sp.dma_start(Hst[:, parity, j, :, :], src).then_inc(att[0][f"h_ld{parity}"], 16)

            def load_max(l, G, parity):
                A = att[l]
                sp.wait_ge(A["m_ready"], G + 1)
                for part in range(PARTS):
                    dst = stack["Tq"][STACK + part:STACK + part + 1, parity, :, :].rearrange("p j (q t) -> p (j q) t", t=P)
                    sp.dma_start(dst, mrow[:, part, :]).then_inc(A["m_ld"], 16)

            def attention_loads(l):
                A = att[l]
                sp.wait_ge(A["ones_set"], 1)
                sp.wait_ge(qk_stored[l], 16 * 16)
                if l == 0:
                    sp.wait_ge(drev_stored, 16 * PARTS * BATCH)
                load_stack(l, "S", 0, 0)
                if l == 0:
                    load_bias(0, 0)
                load_stack(l, "T", 0, 0)
                load_stack(l, "S", 1, 1)
                if l == 0:
                    load_bias(1, 1)
                load_stack(l, "T", 1, 1)

            def attention_feed(l):
                A = att[l]
                NSJ = NS[l] * HG

                def sums_back(G, half):
                    sp.wait_ge(A["sum_inv"], G * 2 + (half + 1))
                    sp.dma_start(Osb[HD:P:32, half, :].rearrange("j (c e) -> j c e", e=16), rsums[:, half, :]).then_inc(A["rrow_in"], 16)

                def feed(G, parity, first, s_next, t_next):
                    load_max(l, G, parity)
                    if l == 0 and not first and t_next:
                        sp.wait_ge(A["st_ps"], G * NSJ)
                        load_bias(G + 1, 1 - parity)
                    if not first:
                        sums_back(G - 1, 1)
                    if l == 1 and not first and t_next:
                        sp.wait_ge(A["st_ps"], G * NSJ)
                    if s_next:
                        sp.wait_ge(A["ring_full"], ring_after_s(G))
                        load_stack(l, "S", G + 2, parity)
                    if not first and t_next:
                        load_stack(l, "T", G + 1, 1 - parity)
                    sums_back(G, 0)

                feed(0, 0, True, True, False)
                with sp.Fori(0, 2) as it:
                    feed(it * 2 + 1, 1, False, True, True)
                    feed(it * 2 + 2, 0, False, True, True)
                feed(5, 1, False, True, True)
                feed(6, 0, False, False, True)
                feed(7, 1, False, False, False)
                sums_back(GROUPS - 1, 1)

            store_qk(0)
            sp.wait_ge(drev_ready, 1)
            for part in range(PARTS):
                for b in range(BATCH):
                    dst = drev_dram[b * NG:(b + 1) * NG, :, part, :].rearrange("g j n -> (g j) n")
                    sp.dma_start(dst, dpart[:, part, :]).then_inc(drev_stored, 16)
            sp.wait_ge(cb_ev, 1)
            sp.dma_start(comb_dram[0], combT[:, :]).then_inc(comb_stored, 16)
            sp.wait_ge(comb_stored, 16)
            sp.wait_ge(qk_stored[0], 16 * 16)
            comb_rows = comb_dram[0].rearrange("(e t) k -> e (t k)", e=EXP)

            def load_gate(e, slot):
                sp.dma_start(cwb[:, slot, :], comb_rows[e].partition_broadcast(P)).then_inc(f_c[slot], 16)

            load_gate(0, 1)

            def next_expert(n, slot, routed):
                sp.wait_ge(y_done, n * 8 + 8)
                sp.dma_start(fw0[:, slot, 0:768], a["ffn_w"][n + 2]).then_inc(f_w[slot], 16)
                if routed:
                    load_gate(n + 1, slot)

            with sp.Fori(0, 3) as it:
                next_expert(it * 2, 0, True)
                next_expert(it * 2 + 1, 1, True)
            next_expert(6, 0, True)
            next_expert(7, 1, False)
            attention_loads(0)
            attention_feed(0)
            sp.wait_ge(y_ev, NC)
            for n_, name in enumerate(("q_proj", "k_proj", "v_proj", "o_proj", "w1", "w2")):
                sp.dma_start(fw[:, n_ * 1024:(n_ + 1) * 1024].rearrange("p (e c) -> p e c", e=EXP),
                             a["L1_ffn_" + name].rearrange("e c h -> c e h")).then_inc(fw_in, 16)
            store_qk(1)
            sp.wait_ge(cb_ev, 2)
            sp.dma_start(comb_dram[1], combT[:, :]).then_inc(comb_stored, 16)
            attention_loads(1)
            attention_feed(1)
            sp.wait_ge(comb_stored, 32)
            sp.wait_ge(att[1]["pj_ev"], NC)
            rows = comb_dram[1].rearrange("(e t) k -> e (t k)", e=EXP)
            for e in range(EXP):
                sp.dma_start(rwb[:, e, :], rows[e].partition_broadcast(P)).then_inc(rw_in, 16)
            sp.wait_ge(cb_ev, 3)
            sp.dma_start(comb_dram[2], combT[:, :]).then_inc(comb_stored, 16)
            sp.wait_ge(comb_stored, 48)
            rows = comb_dram[2].rearrange("(e t) k -> e (t k)", e=EXP)
            for e in range(EXP):
                sp.dma_start(rwb[:, e, :], rows[e].partition_broadcast(P)).then_inc(rw2_in, 16)
            o_v = out.rearrange("b (t p) c -> p (b t) c", p=P)
            for c in range(NC):
                sp.wait_ge(fin_ev, c + 1)
                sp.dma_start(o_v[:, 4 * c:4 * c + 4, :], otok[:, 4 * c:4 * c + 4, :]).then_inc(stored, 16)
            sp.wait_ge(stored, 16 * NC)

        @block.gpsimd
        def _(pool):
            own = Chain(pool, pool_own)
            g = nc.gpsimd
            g.memset(wo[:, :, :, :], 0.0).then_inc(zero_done, 1)
            for t_ in (ident, sel, identb, flip, mask_kq, mask_qk):
                g.memset(t_[:, :], 0.0)
            g.memset(ones[:, :], 1.0)
            own.link(g.memset(tri[:, :, :], 1.0))
            for t_, pattern, base, mult, op, fill in (
                    (ident, [[-1, P]], 0, 1, ALU.not_equal, 1.0),
                    (identb, [[-1, P]], 0, 1, ALU.not_equal, 1.0),
                    (flip, [[1, P]], -(P - 1), 1, ALU.not_equal, 1.0),
                    (mask_kq, [[1, P]], 0, -1, ALU.is_ge, NEG),
                    (mask_qk, [[-1, P]], 0, 1, ALU.is_ge, NEG)):
                g.affine_select(out=t_[:, :], in_=t_[:, :], compare_op=op, fill=fill, base=base,
                                pattern=pattern, channel_multiplier=mult)
            sel_v = sel[:, :].rearrange("p (j d) -> p j d", j=HG)
            g.affine_select(out=sel_v, in_=sel_v, compare_op=ALU.not_equal, fill=1.0, base=-HD,
                            pattern=[[-32, HG], [0, 32]], channel_multiplier=1)
            g.affine_select(out=tri[:, :, :], in_=tri[:, :, :], compare_op=ALU.is_gt, fill=0.0, base=0,
                            pattern=[[1, EXP], [-1, EXP]], channel_multiplier=0).then_inc(const_done, 1)

            def attention(l):
                A = att[l]
                if l == 0:
                    pool.wait_ge(split_done, 2)
                    pool.wait_ge(cb_ev, 1)
                else:
                    pool.wait_ge(cb_ev, 2)
                pool.wait_ge(v_ev, 4 * (l + 1))
                own.link(g.memset(Vst[:, :, :, :, :], 0.0))
                own.link(g.memset(Vst[:, :, :, :, HD:HD + 1], 1.0))
                g.memset(stack["Tk"][64:96, :, :, :], 1.0).then_inc(A["ones_set"], 1)
                pool.wait_ge(A["ones_set"], 1)

                def stage(G, parity):
                    src = V[:, G, :, :].rearrange("p k (j c) -> p k j c", j=HG)
                    g.tensor_copy(Vst[:, parity, :, :, 0:HD], src).then_inc(A["v_staged"], 1)

                def body(G, parity, carry, s_phase):
                    if s_phase:
                        if carry:
                            pool.wait_ge(A["av_done"], G * NS[l])
                        stage(G + 1, 1 - parity)

                stage(0, 0)
                groups(pool, body)

            attention(0)
            attention(1)

        @block.scalar
        def _(act):
            s = nc.scalar

            def copies(first, dst, count_from):
                for c in range(NC):
                    act.wait_ge(tr_ps, count_from + c + 1)
                    s.activation(dst(c), bank(first + c), ACT.Copy).then_inc(tr_ev, 1)

            def split_hi(l):
                for n, (src, dst) in enumerate(((q32, qsp), (k32, ksp))):
                    act.wait_ge(q_ev if n == 0 else k_ev, 4 * (l + 1))
                    s.activation(dst[:, 0, :], src, ACT.Copy).then_inc(hi_done, 1)
                for n, (src, dst) in enumerate(((q32, qsp), (k32, ksp))):
                    act.wait_ge(rest_done, 2 * l + n + 1)
                    s.activation(dst[:, 1, :], src, ACT.Copy).then_inc(mid_done, 1)

            def gate_exps(n):
                act.wait_ge(gx_ready, n)
                s.activation(gated[:, :, :], gated[:, :, :], ACT.Exp).then_inc(ge_ready, 1)

            def attention(l):
                A = att[l]
                steps = t_steps(l)
                n_exp = len(steps) * HG

                def evac(G, half):
                    if half == 0:
                        act.wait_ge(A["av_done"], G * len(steps) + sum(1 for x in steps if x[0] == 0))
                    else:
                        act.wait_ge(A["av_done"], (G + 1) * len(steps))
                    s.activation(Osb[:, half, :], bank(7), ACT.Copy).then_inc(A["o_ev"], 1)
                    act.wait_ge(A["o_ev"], G * 2 + (half + 1))
                    act.dma_start(sums[:, half, :], Osb[HD:P:32, half, :].rearrange("j (c e) -> j c e", e=16)).then_inc(A[f"sum_in{half}"], 16)

                def body(G, parity, carry, s_phase):
                    first_of_half1 = next(i for i, x in enumerate(steps) if x[0] == 1)
                    for i, (h, kt, off) in enumerate(steps):
                        for j in range(HG):
                            m = HG * i + j
                            act.wait_ge(A["st_ps"], G * n_exp + m + 1)
                            if i >= 2:
                                act.wait_ge(A["av_done"], G * len(steps) + i - 1)
                            elif carry:
                                act.wait_ge(A["av_done"], G * len(steps) + i - 1)
                            w = 512 - off
                            s.activation(Pr[:, m % 8, 0:w], bank(4 + m % 3, 0, w), ACT.Exp).then_inc(A["e_done"], 1)
                        if i == 0 and carry:
                            act.wait_ge(A["ring_free"], ring_base(G))
                            evac(G - 1, 1)
                        if i == first_of_half1:
                            if carry:
                                act.wait_ge(A["ring_free"], ring_base(G))
                            evac(G, 0)

                groups(act, body)
                act.wait_ge(A["ring_free"], ring_base(GROUPS - 1) + 2)
                evac(GROUPS - 1, 1)

            def root_var(n):
                act.wait_ge(var_ready, n)
                s.activation(small[:, 2, :], small[:, 1, :], ACT.Sqrt).then_inc(rstd_ready, 1)

            def root_squares(n):
                act.wait_ge(ss_ready, n)
                s.activation(gl[:, n, 128:152], gl[:, n, 128:152], ACT.Sqrt).then_inc(norm_ready, 1)

            act.wait_ge(const_done, 1)
            copies(4, lambda c: xT[:, 512 * c:512 * (c + 1)], 0)
            root_var(1)
            copies(0, lambda c: xnT[:, 512 * c:512 * (c + 1)], 4)
            act.wait_ge(w_in, 16 * (W_LOADS + 1))
            for c in range(NC):
                act.wait_ge(k_ps, c + 1)
                s.activation(k32[:, 512 * c:512 * (c + 1)], bank(c), ACT.Identity, bias=bk).then_inc(k_ev, 1)
            split_hi(0)
            gate_exps(1)
            s.activation(gl[:, 0, 0:2 * EXP], erow[:, 1:3, :].rearrange("p a e -> p (a e)"), ACT.Exp, scale=-1.0).then_inc(gate_exp, 1)

            def silu_units(n_term, base):
                for u in range(8):
                    act.wait_ge(h_ps, n_term + base + u + 1)
                    if not (isinstance(n_term, int) and base + u < 2):
                        act.wait_ge(g_made, n_term + base + u - 1)
                    s.activation(fa[:, u % 2, :], bank(2 * (u % 2)), ACT.Silu).then_inc(a_made, 1)

            silu_units(0, 0)
            with act.Fori(0, 4) as it:
                silu_units(it * 16, 8)
                silu_units(it * 16, 16)
            silu_units(0, 72)
            act.wait_ge(y_done, 8 * FFN_SEQ)
            for c in range(NC):
                s.activation(n1T[:, 512 * c:512 * (c + 1)], bank(4 + c), ACT.Silu).then_inc(y_ev, 1)
            attention(0)

            copies(4, lambda c: xtok[:, 4 * c:4 * c + 4, :].rearrange("p t c -> p (t c)"), 8)
            root_var(2)
            copies(0, lambda c: xnT[:, 512 * c:512 * (c + 1)], 12)
            root_var(3)
            for c in range(NC):
                act.wait_ge(tr_ps, 16 + c + 1)
                s.activation(n1T[:, 512 * c:512 * (c + 1)], bank(4 + c), ACT.Identity, bias=ln_b[0], scale=ln_w[0]).then_inc(tr_ev, 1)
            for c in range(NC):
                act.wait_ge(k_ps, 4 + c + 1)
                s.activation(k32[:, 512 * c:512 * (c + 1)], bank(4 + c), ACT.Copy).then_inc(k_ev, 1)
            split_hi(1)
            act.wait_ge(tr_ev, 20)
            s.activation(zz.rearrange("p t c -> p (t c)"), n1T[:, :], ACT.Square).then_inc(sq_ready, 1)
            root_squares(1)
            gate_exps(2)
            attention(1)
            for c in range(NC):
                act.wait_ge(att[1]["pj_ps"], c + 1)
                if c == 0:
                    act.wait_ge(att[1]["v_staged"], GROUPS)
                s.activation(sT1[:, 512 * c:512 * (c + 1)], bank(c), ACT.Copy).then_inc(att[1]["pj_ev"], 1)

            with act.Fori(0, BATCH) as b:
                act.wait_ge(x_used, b * EXP + EXP)
                for c in range(2):
                    s.activation(qT[:, 512 * c:512 * (c + 1)], bank(c), ACT.Copy, scale=1.0 / math.sqrt(C)).then_inc(x_ev, 1)
                for c in range(2):
                    s.activation(vT[:, 512 * c:512 * (c + 1)], bank(4 + c), ACT.Copy).then_inc(x_ev, 1)
                for qt in range(KT):
                    act.wait_ge(s1_max, b * KT + qt + 1)
                    if qt >= 2:
                        act.wait_ge(pt_ps, b * KT + qt - 1)
                    w = (qt + 1) * P
                    s.activation(P1[:, qt % 2, 0:w], PS[:, 1024 * (qt % 2):1024 * (qt % 2) + w], ACT.Exp,
                                 bias=small[:, 4, qt:qt + 1], accum_out=small[:, 5, qt:qt + 1]).then_inc(s1_exp, 1)
                    if qt in (4, 7):
                        half = 0 if qt == 4 else 1
                        act.wait_ge(o1_ps, b * 2 + half + 1)
                        s.activation(attnT[:, bass.ds(b * SEQ + 512 * half, 512)], bank(6 + half), ACT.Copy).then_inc(o1_ev, 1)
            copies(4, lambda c: xtok[:, 4 * c:4 * c + 4, :].rearrange("p t c -> p (t c)"), 20)
            root_var(4)
            for c in range(NC):
                act.wait_ge(tr_ps, 24 + c + 1)
                s.activation(xnT[:, 512 * c:512 * (c + 1)], bank(c), ACT.Identity, bias=ln_b[1], scale=ln_w[1]).then_inc(tr_ev, 1)
            act.wait_ge(tr_ev, 28)
            s.activation(zz.rearrange("p t c -> p (t c)"), xnT[:, :], ACT.Square).then_inc(sq_ready, 1)
            root_squares(2)
            gate_exps(3)
            with act.Fori(0, BATCH) as b:
                for u in range(2 * EXP):
                    act.wait_ge(i_ps, b * 16 + u + 1)
                    s.activation(ga[:, u % 4, :], bank(u % 4), ACT.Gelu).then_inc(i_gelu, 1)
            for c in range(NC):
                act.wait_ge(moe_ev, c + 1)
                s.activation(hsT[:, 512 * c:512 * (c + 1)], hsT[:, 512 * c:512 * (c + 1)], ACT.Silu).then_inc(fin_silu, 1)
            for c in range(NC):
                act.wait_ge(fin_ps, c + 1)
                s.activation(otok[:, 4 * c:4 * c + 4, :].rearrange("p t c -> p (t c)"), bank(c), ACT.Copy).then_inc(fin_ev, 1)

        @block.vector
        def _(dve):
            own = Chain(dve, dve_own)
            v = nc.vector
            mean, var, rs, dd = small[:, 0, :], small[:, 1, :], small[:, 2, :], small[:, 3, :]

            def layer_norm(n, src, dst, ready=None):
                for t in range(NT):
                    if ready and t % 4 == 0:
                        ready(t // 4)
                    ins = v.bn_stats(stats[:, t, :], src[:, t, :])
                own.link(ins)
                own.link(v.tensor_tensor(dd, stats[:, :, 1], stats[:, :, 4], ALU.add))
                own.link(v.tensor_scalar(mean, dd, 0.5, None, ALU.mult))
                own.link(v.tensor_tensor(dd, stats[:, :, 1], stats[:, :, 4], ALU.subtract))
                own.link(v.scalar_tensor_tensor(dd, dd, 0.25, dd, ALU.mult, ALU.mult))
                own.link(v.tensor_tensor(var, stats[:, :, 2], stats[:, :, 5], ALU.add))
                own.link(v.scalar_tensor_tensor(var, var, 1.0 / C, dd, ALU.mult, ALU.add))
                v.tensor_scalar(var, var, LN_EPS, None, ALU.add).then_inc(var_ready, 1)
                dve.wait_ge(rstd_ready, n)
                own.link(v.reciprocal(rs, rs))
                for t in range(NT):
                    ins = v.tensor_scalar(dst[:, t, :], src[:, t, :], mean[:, t:t + 1], rs[:, t:t + 1], ALU.subtract, ALU.mult)
                    if t % 4 == 3:
                        ins.then_inc(z_ready, 1)

            def split_rest(l):
                for n, (src, dst) in enumerate(((q32, qsp), (k32, ksp))):
                    dve.wait_ge(hi_done, 2 * l + n + 1)
                    v.tensor_tensor(src, src, dst[:, 0, :], ALU.subtract).then_inc(rest_done, 1)
                for n, (src, dst) in enumerate(((q32, qsp), (k32, ksp))):
                    dve.wait_ge(mid_done, 2 * l + n + 1)
                    v.tensor_tensor(dst[:, 2, :], src, dst[:, 1, :], ALU.subtract).then_inc(split_done, 1)

            def per_token(x):
                return x.unsqueeze(2).to_broadcast([P, NT, EXP])

            def per_expert(x):
                return x.unsqueeze(1).to_broadcast([P, NT, EXP])

            def gate(n):
                own.link(v.tensor_tensor(cmp_a, lg[:, :, :].unsqueeze(2).to_broadcast([P, NT, EXP, EXP]),
                                         lg[:, :, :].unsqueeze(3).to_broadcast([P, NT, EXP, EXP]), ALU.is_gt))
                own.link(v.tensor_tensor(cmp_b, lg[:, :, :].unsqueeze(2).to_broadcast([P, NT, EXP, EXP]),
                                         lg[:, :, :].unsqueeze(3).to_broadcast([P, NT, EXP, EXP]), ALU.is_equal))
                own.link(v.tensor_tensor(cmp_b, cmp_b, tri[:, :, :].unsqueeze(1).to_broadcast([P, NT, EXP, EXP]), ALU.mult))
                own.link(v.tensor_tensor(cmp_a, cmp_a, cmp_b, ALU.add))
                own.link(v.reduce_sum(top2[:, :, :], cmp_a, axis=AX.X))
                own.link(v.tensor_scalar(top2[:, :, :], top2[:, :, :], 1.5, None, ALU.is_lt))
                src = lg
                if n:
                    own.link(v.tensor_scalar(act_mask[:, :, :], lg[:, :, :], 0.0, None, ALU.is_gt))
                    own.link(v.reduce_max(small[:, 6, :], act_mask[:, :, :], axis=AX.X))
                    own.link(v.tensor_scalar(small[:, 6, :], small[:, 6, :], 0.5, None, ALU.is_lt))
                    own.link(v.tensor_tensor(top2[:, :, :], top2[:, :, :], per_token(small[:, 6, :]), ALU.mult))
                    own.link(v.tensor_tensor(top2[:, :, :], top2[:, :, :], act_mask[:, :, :], ALU.max))
                    own.link(v.tensor_scalar(lg[:, :, :], lg[:, :, :], 0.0, None, ALU.max))
                own.link(v.reduce_max(small[:, 7, :], src[:, :, :], axis=AX.X))
                v.tensor_tensor(gated[:, :, :], src[:, :, :], per_token(small[:, 7, :]), ALU.subtract).then_inc(gx_ready, 1)
                dve.wait_ge(ge_ready, n + 1)
                own.link(v.tensor_tensor(gated[:, :, :], gated[:, :, :], top2[:, :, :], ALU.mult))
                own.link(v.reduce_sum(small[:, 8, :], gated[:, :, :], axis=AX.X))
                own.link(v.reciprocal(small[:, 9, :], small[:, 8, :]))
                if n:
                    dve.wait_ge(comb_stored, 16 * n)
                v.tensor_tensor(comb[:, :, :].rearrange("p e t -> p t e"), gated[:, :, :], per_token(small[:, 9, :]),
                                ALU.mult).then_inc(comb_ready, 1)
                dve.wait_ge(cb_ps, n + 1)
                v.tensor_copy(combT[:, :], bank((1, 5, 5)[n], 0, P)).then_inc(cb_ev, 1)

            def gate_logits(n):
                dve.wait_ge(lg_ps, n + 1)
                v.tensor_copy(gl[:, n, 0:152], bank(4, 0, 152)).then_inc(ss_ready, 1)
                dve.wait_ge(norm_ready, n)
                own.link(v.tensor_scalar(gl[:, n, 128:152], gl[:, n, 128:152], 1e-12, None, ALU.max))
                own.link(v.reciprocal(gl[:, n, 128:152], gl[:, n, 128:152]))
                raw = gl[:, n, 0:128].rearrange("p (t e) -> p t e", e=EXP)
                own.link(v.tensor_tensor(lg[:, :, :], raw, per_token(gl[:, n, 128:144]), ALU.mult))
                own.link(v.tensor_tensor(lg[:, :, :], lg[:, :, :], per_expert(gl[:, n, 144:152]), ALU.mult))
                own.link(v.tensor_tensor(lg[:, :, :], lg[:, :, :], per_expert(erow[:, n, :]), ALU.subtract))

            def attention(l):
                A = att[l]

                def unit(U, parity, what):
                    dve.wait_ge(A["ring_full"], U + 1)
                    lo = 1024 * parity
                    if what[0] == "S":
                        j, q, w = what[1]
                        v.reduce_max(mx[:, j * KT + q:j * KT + q + 1], PS[:, lo:lo + w], axis=AX.X).then_inc(A["ring_free"], 1)
                    elif what[0] == "R":
                        G, half = what[1]
                        dst = OT[:, G, 512 * half:512 * (half + 1)]
                        v.tensor_tensor(dst, Osb[:, half, :], PS[:, lo:lo + 512], ALU.mult).then_inc(A["ring_free"], 1)
                    else:
                        G = what[1]
                        n = HG * KT
                        src = PS[0:n, lo:lo + P]
                        if not (isinstance(G, int) and G == 0):
                            dve.wait_ge(A["m_ld"], G * 48)
                        own.link(v.tensor_scalar(mrow[:, 0, :], src, -1.0, None, ALU.mult))
                        v.scalar_tensor_tensor(mres[:, :], src, -1.0, mrow[:, 0, :], ALU.mult, ALU.subtract).then_inc(A["ring_free"], 1)
                        dve.wait_ge(A["ring_free"], U + 1)
                        own.link(v.tensor_copy(mrow[:, 1, :], mres[:, :]))
                        v.tensor_tensor(mrow[:, 2, :], mres[:, :], mrow[:, 1, :], ALU.subtract).then_inc(A["m_ready"], 1)

                def invert(G, half):
                    dve.wait_ge(A[f"sum_in{half}"], G * 16 + 16)
                    v.reciprocal(rsums[:, half, :], sums[:, half, :]).then_inc(A["sum_inv"], 1)

                def units(G, U, parity, plan):
                    n = 0
                    for step in plan:
                        for what in step:
                            if what[0] == "Q":
                                invert(G - 1 if what[1] else G, what[1])
                                continue
                            if what[0] == "R":
                                what = ("R", (G - 1 if what[1] else G, what[1]))
                            if what[0] == "M":
                                what = ("M", G + 1)
                            unit(U + n, (parity + n) % 2, what)
                            n += 1

                def body(G, parity, carry, s_phase):
                    base = ring_base(G)
                    base_parity = ring_base(2 - parity if carry else 0) % 2
                    units(G, base, base_parity, ring_plan(l, carry, s_phase, True))

                units(-1, 0, 0, ring_plan(l, False, True, False))
                groups(dve, body, own, 4)
                invert(GROUPS - 1, 1)
                last = ring_base(GROUPS - 1) + 2
                unit(last, last % 2, ("R", (GROUPS - 1, 1)))

            def x_ready(c):
                dve.wait_ge(x_in[c], 16)

            layer_norm(1, xtok, ztok, x_ready)
            dve.wait_ge(w_in, 16 * (W_LOADS + 1))
            own.link(v.tensor_scalar(qscale, temp, 0.1, 10.0, ALU.max, ALU.min))
            own.link(v.tensor_scalar(qscale, qscale, math.sqrt(C), None, ALU.mult))
            own.link(v.reciprocal(qscale, qscale))
            for c in range(NC):
                dve.wait_ge(q_ps, c + 1)
                v.tensor_scalar(q32[:, 512 * c:512 * (c + 1)], bank(4 + c), bq, qscale, ALU.add, ALU.mult).then_inc(q_ev, 1)

            def values(l, first):
                for c in range(NC):
                    dve.wait_ge(v_ps, 4 * l + c + 1)
                    b, k0 = c // 2, 4 * (c % 2)
                    dst = V[:, b * NG:(b + 1) * NG, k0:k0 + 4, :].rearrange("p g k c -> p k g c")
                    src = bank(first + c).rearrange("p (k g c) -> p k g c", k=4, g=NG)
                    if l == 0:
                        bias = bvb[:, :].rearrange("p (g c) -> p g c", g=NG).unsqueeze(1).to_broadcast([P, 4, NG, 32])
                        v.tensor_tensor(dst, src, bias, ALU.add).then_inc(v_ev, 1)
                    else:
                        v.tensor_copy(dst, src).then_inc(v_ev, 1)

            values(0, 4)
            split_rest(0)
            dve.wait_ge(tbl_in, 16)
            own.link(v.memset(dfull[:, :], 0.0))
            own.link(v.tensor_scalar(dfull[:, DREV - 1 - REL:DREV - 1], tblr[:, :], tblr[:, 0:1], qscale[0:HEADS, :],
                                     ALU.subtract, ALU.mult))
            own.link(v.tensor_copy(dpart[:, 0, :], dfull[:, :]))
            own.link(v.tensor_tensor(dfull[:, :], dfull[:, :], dpart[:, 0, :], ALU.subtract))
            own.link(v.tensor_copy(dpart[:, 1, :], dfull[:, :]))
            v.tensor_tensor(dpart[:, 2, :], dfull[:, :], dpart[:, 1, :], ALU.subtract).then_inc(drev_ready, 1)
            dve.wait_ge(lg_ps, 1)
            dve.wait_ge(const_done, 1)
            own.link(v.tensor_tensor(lg[:, :, :], bank(0, 0, 128).rearrange("p (t e) -> p t e", e=EXP),
                                     per_expert(erow[:, 0, :]), ALU.add))
            gate(0)
            dve.wait_ge(gate_exp, 1)
            own.link(v.tensor_scalar(gl[:, 0, 0:2 * EXP], gl[:, 0, 0:2 * EXP], 1.0, None, ALU.add))
            own.link(v.reciprocal(erow[:, 1:3, :].rearrange("p a e -> p (a e)"), gl[:, 0, 0:2 * EXP]))
            v.tensor_tensor(simsq[:, :, :], router[:, 1:3, :], router[:, 1:3, :], ALU.mult).then_inc(gneg, 1)

            def ffn_units(n_term, base, slot, routed):
                for u in range(8):
                    U = base + u
                    dve.wait_ge(a_made, n_term + U + 1)
                    if not (isinstance(n_term, int) and U < 4):
                        dve.wait_ge(y_done, n_term + U - 3)
                    g_ = fg[:, u % 4, :]
                    ins = v.tensor_tensor(g_, bank(2 * (u % 2) + 1), fa[:, u % 2, :], ALU.mult)
                    if routed is not None:
                        own.link(ins)
                        if u == 0:
                            dve.wait_ge(f_c[slot], routed)
                        ins = v.tensor_tensor(g_, g_, cwb[:, slot, 512 * (u // 2):512 * (u // 2 + 1)], ALU.mult)
                    ins.then_inc(g_made, 1)

            ffn_units(0, 0, 0, None)
            with dve.Fori(0, 4) as it:
                own.enter(it, 16)
                ffn_units(it * 16, 8, 1, it * 16 + 16)
                ffn_units(it * 16, 16, 0, it * 16 + 16)
            own.leave(4)
            ffn_units(0, 72, 1, None)
            attention(0)
            for c in range(NC):
                dve.wait_ge(att[0]["pj_ps"], c + 1)
                part = slice(512 * c, 512 * (c + 1))
                dve.wait_ge(y_ev, c + 1)
                own.link(v.scalar_tensor_tensor(n1T[:, part], bank(c), bp, n1T[:, part], ALU.add, ALU.mult))
                v.tensor_tensor(xT[:, part], xT[:, part], n1T[:, part], ALU.add).then_inc(att[0]["pj_ev"], 1)

            layer_norm(2, xtok, ztok, lambda c: dve.wait_ge(tr_ev, 8 + c + 1))
            dve.wait_ge(z_ready, 8)
            layer_norm(3, ztok, zz)
            for c in range(NC):
                dve.wait_ge(q_ps, 4 + c + 1)
                v.tensor_scalar(q32[:, 512 * c:512 * (c + 1)], bank(c), 1.0 / math.sqrt(HD), None, ALU.mult).then_inc(q_ev, 1)
            values(1, 0)
            split_rest(1)
            gate_logits(1)
            gate(1)
            attention(1)

            dve.wait_ge(att[1]["pj_ev"], NC)
            dve.wait_ge(rw_in, 16 * EXP)
            with dve.Fori(0, BATCH) as b:
                own.enter(b, 16)
                tok = bass.ds(b * SEQ, SEQ)
                for e in range(EXP):
                    if e >= 2:
                        dve.wait_ge(x_used, b * EXP + e - 1)
                    v.tensor_tensor(Xe[:, e % 2, :], n1T[:, tok], rwb[:, e, tok], ALU.mult).then_inc(x_made, 1)
                dve.wait_ge(x_used, b * EXP + EXP)
                for c in range(2):
                    v.tensor_copy(kT[:, 512 * c:512 * (c + 1)], bank(2 + c)).then_inc(vt_ev, 1)
                for c in range(2):
                    dve.wait_ge(vt_ps, b * 2 + c + 1)
                    v.tensor_copy(vtok[:, 4 * c:4 * c + 4, :].rearrange("p k c -> p (k c)"), bank(6 + c)).then_inc(vt_ev, 1)
                for i in range(KT + 1):
                    if i < KT:
                        w = (i + 1) * P
                        dve.wait_ge(s1_ps, b * KT + i + 1)
                        own.link(v.reduce_max(small[:, 3, i:i + 1], PS[:, 1024 * (i % 2):1024 * (i % 2) + w], axis=AX.X))
                        v.tensor_scalar(small[:, 4, i:i + 1], small[:, 3, i:i + 1], -1.0, None, ALU.mult).then_inc(s1_max, 1)
                        dve.wait_ge(s1_exp, b * KT + i + 1)
                        own.link(v.reciprocal(small[:, 6, i:i + 1], small[:, 5, i:i + 1]))
                        v.tensor_scalar(P1[:, i % 2, 0:w], P1[:, i % 2, 0:w], small[:, 6, i:i + 1], None, ALU.mult).then_inc(s1_p, 1)
                    if i >= 1:
                        q = i - 1
                        dve.wait_ge(pt_ps, b * KT + q + 1)
                        if q == 4:
                            dve.wait_ge(o1_ps, b * 2 + 1)
                        src = PS[:, 2048:2048 + (q + 1) * P].rearrange("p (k q) -> p k q", q=P)
                        v.tensor_copy(PT[:, 0:q + 1, (q % 4) * P:(q % 4 + 1) * P], src).then_inc(pt_ev, 1)
                for e in range(EXP):
                    if e == 0:
                        dve.wait_ge(o1_ev, b * 2 + 2)
                    if e >= 2:
                        dve.wait_ge(ox_used, b * EXP + e - 1)
                    v.tensor_tensor(Xe[:, e % 2, :], attnT[:, tok], rwb[:, e, tok], ALU.mult).then_inc(ox_made, 1)
                dve.wait_ge(ox_used, b * EXP + EXP)
                for c in range(2):
                    sl = bass.ds(b * SEQ + 512 * c, 512)
                    v.tensor_tensor(hsT[:, sl], bank(c), xnT[:, sl], ALU.add).then_inc(hs_ev, 1)
            own.leave(2)
            layer_norm(4, xtok, ztok, lambda c: dve.wait_ge(tr_ev, 20 + c + 1))
            gate_logits(2)
            gate(2)
            dve.wait_ge(rw2_in, 16 * EXP)
            with dve.Fori(0, BATCH) as b:
                for u in range(2 * EXP):
                    e, c = u // 2, u % 2
                    dve.wait_ge(i_gelu, b * 16 + u + 1)
                    if u >= 4:
                        dve.wait_ge(i_used, b * 16 + u - 3)
                    v.tensor_tensor(gg[:, u % 4, :], ga[:, u % 4, :], rwb[:, e, bass.ds(b * SEQ + 512 * c, 512)], ALU.mult).then_inc(i_g, 1)
                dve.wait_ge(i_used, b * 16 + 16)
                for c in range(2):
                    sl = bass.ds(b * SEQ + 512 * c, 512)
                    v.tensor_tensor(hsT[:, sl], bank(4 + c), hsT[:, sl], ALU.add).then_inc(moe_ev, 1)
            for c in range(NC):
                part = slice(512 * c, 512 * (c + 1))
                dve.wait_ge(fin_silu, c + 1)
                own.link(v.tensor_tensor(hsT[:, part], hsT[:, part], sT1[:, part], ALU.mult))
                v.tensor_tensor(hsT[:, part], hsT[:, part], xT[:, part], ALU.add).then_inc(fin_x, 1)

        @block.tensor
        def _(pe):
            def mm(out_, lhsT, rhs, start=True, stop=True):
                return nc.tensor.matmul(out_, lhsT, rhs, start=start, stop=stop)

            def transposes(src, first, ready):
                for c in range(NC):
                    ready(c)
                    for k in range(4):
                        ins = nc.tensor.transpose(bank(first + c, P * k, P * (k + 1)), src(4 * c + k), ident[:, :])
                    ins.then_inc(tr_ps, 1)

            def project(l, w, first, done, ready):
                for c in range(NC):
                    ready(c)
                    mm(bank(first + c), w[:, l, :], xnT[:, 512 * c:512 * (c + 1)]).then_inc(done, 1)

            def project_v(l, first, ready):
                for c in range(NC):
                    ready(c)
                    for k in range(4):
                        t = 4 * c + k
                        ins = mm(bank(first + c, P * k, P * (k + 1)), xnT[:, t * P:(t + 1) * P], wv[:, l, :])
                    ins.then_inc(v_ps, 1)

            def comb_T(n, b_):
                pe.wait_ge(comb_ready, n + 1)
                nc.tensor.transpose(bank(b_, 0, P), comb[:, :, :].rearrange("p e t -> p (e t)"), ident[:, :]).then_inc(cb_ps, 1)

            def gate_products(n, srcT):
                pe.wait_ge(sq_ready, n)
                pe.wait_ge(gneg, 1)
                sq = zz.rearrange("p t c -> p (t c)")
                for t in range(NT):
                    mm(bank(4, 8 * t, 8 * t + 8), srcT[:, t * P:(t + 1) * P], router[:, n, :])
                    mm(bank(4, 128 + t, 129 + t), sq[:, t * P:(t + 1) * P], ones[:, 0:1])
                mm(bank(4, 144, 152), ones[:, :], simsq[:, n - 1, :]).then_inc(lg_ps, 1)

            def attention(l):
                A = att[l]
                steps = t_steps(l)
                n_st = len(steps) * HG
                half0 = sum(1 for x in steps if x[0] == 0)

                def s_unit(U, parity, j, q, w, slot):
                    lo = 1024 * parity
                    queries = stack["Sq"][0:STACK, slot, j, q * P:(q + 1) * P]
                    for k0 in range(0, w, 512):
                        k1 = min(w, k0 + 512)
                        extra = []
                        if l == 0 and q < 2 and k0 == 512:
                            h0 = 256 if q == 0 else 384
                            extra = [(h0, flip[:, :], Hst[:, slot, j, part, 0:512 - h0]) for part in range(PARTS)]
                        if l == 1 and k1 == w:
                            extra = [(k1 - k0 - P, identb[:, :], mask_qk[:, :])]
                        ins = mm(PS[:, lo + k0:lo + k1], queries, stack["Sk"][0:STACK, slot, j, k0:k1], stop=not extra)
                        for n, (c0, lhsT, rhs) in enumerate(extra):
                            ins = mm(PS[:, lo + k0 + c0:lo + k1], lhsT, rhs, start=False, stop=n == len(extra) - 1)
                    ins.then_inc(A["ring_full"], 1)

                def unit(U, parity, what, slot):
                    if not (isinstance(U, int) and U < 2):
                        pe.wait_ge(A["ring_free"], U - 1)
                    if what[0] == "S":
                        s_unit(U, parity, *what[1], slot)
                    elif what[0] == "R":
                        G, half = what[1]
                        pe.wait_ge(A["rrow_in"], G * 32 + 16 * half + 16)
                        mm(PS[:, 1024 * parity:1024 * parity + 512], sel[:, :], Osb[:, half, :]).then_inc(A["ring_full"], 1)
                    else:
                        pe.wait_ge(A["ring_free"], U)
                        nc.tensor.transpose(PS[0:HG * KT, 1024 * parity:1024 * parity + P], mx[:, :], ident[:, :])\
                            .then_inc(A["ring_full"], 1)

                def st_step(G, i, parity, carry, heads):
                    h, kt, off = steps[i]
                    for j in heads:
                        m = HG * i + j
                        if m >= 3:
                            pe.wait_ge(A["e_done"], G * n_st + m - 2)
                        elif carry:
                            pe.wait_ge(A["e_done"], G * n_st)
                        w = 512 - off
                        q0 = 512 * h + off
                        dst = bank(4 + m % 3, 0, w)
                        extra = []
                        if l == 0 and h == 0 and kt == KT - 2:
                            extra = [(0, Hst[:, parity, j, part, 0:P], flip[:, :]) for part in range(PARTS)]
                        if l == 0 and h == 0 and kt == KT - 1:
                            extra = [(q * P, Hst[:, parity, j, part, P * (1 - q):P * (2 - q)], flip[:, :])
                                     for q in range(2) for part in range(PARTS)]
                        if l == 1 and kt * P == q0:
                            extra = [(0, identb[:, :], mask_kq[:, :])]
                        ins = mm(dst, stack["Tk"][0:STACK + PARTS, parity, j, kt * P:(kt + 1) * P],
                                 stack["Tq"][0:STACK + PARTS, parity, j, q0:q0 + w], stop=not extra)
                        for n, (c0, lhsT, rhs) in enumerate(extra):
                            ins = mm(bank(4 + m % 3, c0, c0 + P), lhsT, rhs, start=False, stop=n == len(extra) - 1)
                        ins.then_inc(A["st_ps"], 1)

                def av_step(G, i, parity):
                    h, kt, off = steps[i]
                    pe.wait_ge(A["e_done"], G * n_st + HG * (i + 1))
                    if i == 0:
                        pe.wait_ge(A["v_staged"], G + 1)
                        if not (isinstance(G, int) and G == 0):
                            pe.wait_ge(A["o_ev"], G * 2)
                    if i == half0:
                        pe.wait_ge(A["o_ev"], G * 2 + 1)
                    last = i + 1 == len(steps) or steps[i + 1][0] != h
                    for j in range(HG):
                        ins = mm(PS[32 * j:32 * (j + 1), 7 * 512 + off:8 * 512], Vst[:, parity, kt, j, :],
                                 Pr[:, (HG * i + j) % 8, 0:512 - off], start=kt == 0, stop=last)
                    ins.then_inc(A["av_done"], 1)

                def body(G, parity, carry, s_phase):
                    plan = ring_plan(l, carry, s_phase, True)
                    U = 0
                    base = ring_base(G)
                    base_parity = ring_base(2 - parity if carry else 0) % 2
                    for i in range(len(steps)):
                        if i == 0:
                            wait_loads("t", G, parity)
                            pe.wait_ge(A["m_ld"], G * 48 + 48)
                            if s_phase:
                                wait_loads("s", G + 1, 1 - parity)
                                if l == 0:
                                    wait_bias(G + 1, 1 - parity)
                        todo = [w for w in plan[i] if w[0] != "Q"]
                        for j in range(HG):
                            st_step(G, i, parity, carry, (j,))
                            if j == 1:
                                if i == 0 and carry:
                                    av_step(G - 1, len(steps) - 1, 1 - parity)
                                if i > 0:
                                    av_step(G, i - 1, parity)
                            now = len(todo) if j == HG - 1 else 0 if j == 1 and len(todo) < 3 else 1
                            for what in todo[:now]:
                                if what[0] == "R":
                                    what = ("R", (G - 1 if what[1] else G, what[1]))
                                unit(base + U, (base_parity + U) % 2, what, 1 - parity)
                                U += 1
                            todo = todo[now:]

                def wait_loads(which, G, parity):
                    pe.wait_ge(A[f"{which}_ld{parity}"], (G - parity) * 64 + 128)

                def wait_bias(G, parity):
                    pe.wait_ge(A[f"h_ld{parity}"], (G - parity) * 32 + 64)

                wait_loads("s", 0, 0)
                if l == 0:
                    wait_bias(0, 0)
                U = 0
                for step in ring_plan(l, False, True, False):
                    for what in step:
                        unit(U, U % 2, what, 0)
                        U += 1
                groups(pe, body)
                av_step(GROUPS - 1, len(steps) - 1, 1)
                last = ring_base(GROUPS - 1) + 2
                unit(last, last % 2, ("R", (GROUPS - 1, 1)), 0)
                pe.wait_ge(A["ring_free"], last + 1)
                for c in range(NC):
                    for g in range(NG):
                        ins = mm(bank(c), wo[:, l, g, :], OT[:, (c // 2) * NG + g, 512 * (c % 2):512 * (c % 2 + 1)],
                                 start=g == 0, stop=g == NG - 1)
                    ins.then_inc(A["pj_ps"], 1)

            pe.wait_ge(const_done, 1)
            transposes(lambda t: xtok[:, t, :], 4, lambda c: pe.wait_ge(x_in[c], 16))
            transposes(lambda t: ztok[:, t, :], 0, lambda c: pe.wait_ge(z_ready, c + 1))
            pe.wait_ge(w_in, 16 * (W_LOADS + 1))
            project(0, wq, 4, q_ps, lambda c: pe.wait_ge(tr_ev, 4 + c + 1))
            project(0, wk, 0, k_ps, lambda c: None)
            project_v(0, 4, lambda c: pe.wait_ge(q_ev, c + 1))
            pe.wait_ge(k_ev, 1)
            for t in range(NT):
                ins = mm(bank(0, 8 * t, 8 * t + 8), xnT[:, t * P:(t + 1) * P], router[:, 0, :])
            ins.then_inc(lg_ps, 1)
            pe.wait_ge(k_ev, 4)

            def up(n_term, U, u, slot, ready):
                if u == 0:
                    pe.wait_ge(f_w[slot], ready)
                if not (isinstance(n_term, int) and U < 2):
                    pe.wait_ge(g_made, n_term + U - 1)
                x = xnT[:, 512 * (u // 2):512 * (u // 2 + 1)]
                w0 = 128 * (u % 2)
                mm(bank(2 * (u % 2)), fw0[:, slot, w0:w0 + 128], x)
                mm(bank(2 * (u % 2) + 1), fw0[:, slot, 256 + w0:256 + w0 + 128], x).then_inc(h_ps, 1)

            def down(n_term, U, u, slot, first, last):
                pe.wait_ge(g_made, n_term + U + 1)
                w0 = 512 + 128 * (u % 2)
                mm(bank(4 + u // 2), fw0[:, slot, w0:w0 + 128], fg[:, u % 4, :], start=first and u % 2 == 0,
                   stop=last and u % 2 == 1).then_inc(y_done, 1)

            def expert(n_term, base, slot, ready, first=False, last=False, carry=False, flush=True):
                for u in range(8):
                    if u >= 2:
                        down(n_term, base + u - 2, u - 2, slot, first, last)
                    elif carry:
                        down(n_term, base + u - 2, 6 + u, 1 - slot, False, False)
                    up(n_term, base + u, u, slot, ready)
                if flush:
                    down(n_term, base + 6, 6, slot, first, last)
                    down(n_term, base + 7, 7, slot, first, last)

            comb_T(0, 1)
            pe.wait_ge(cb_ev, 1)
            pe.wait_ge(v_ev, 4)
            expert(0, 0, 0, 16, first=True)
            with pe.Fori(0, 4) as it:
                expert(it * 16, 8, 1, it * 16 + 16, flush=False)
                expert(it * 16, 16, 0, it * 16 + 32, carry=True)
            expert(0, 72, 1, 16 * 5, last=True)
            pe.wait_ge(y_ev, NC)
            attention(0)

            transposes(lambda t: xT[:, t * P:(t + 1) * P], 4, lambda c: pe.wait_ge(att[0]["pj_ev"], c + 1))
            transposes(lambda t: ztok[:, t, :], 0, lambda c: pe.wait_ge(z_ready, 4 + c + 1))
            transposes(lambda t: zz[:, t, :], 4, lambda c: pe.wait_ge(z_ready, 8 + c + 1))
            project(1, wq, 0, q_ps, lambda c: pe.wait_ge(tr_ev, 12 + c + 1))
            project(1, wk, 4, k_ps, lambda c: pe.wait_ge(tr_ev, 16 + c + 1))
            project_v(1, 0, lambda c: pe.wait_ge(q_ev, 4 + c + 1))
            pe.wait_ge(k_ev, 8)
            gate_products(1, n1T)
            comb_T(1, 5)
            pe.wait_ge(v_ev, 8)
            pe.wait_ge(cb_ev, 2)
            attention(1)

            pe.wait_ge(fw_in, 16 * 6)
            pe.wait_ge(att[1]["pj_ev"], NC)
            with pe.Fori(0, BATCH) as b:
                for e in range(EXP):
                    pe.wait_ge(x_made, b * EXP + e + 1)
                    for n, w in enumerate((fwq, fwk, fwv)):
                        for c in range(2):
                            ins = mm(bank(2 * n + c), w[:, e, :], Xe[:, e % 2, 512 * c:512 * (c + 1)], start=e == 0, stop=e == EXP - 1)
                    ins.then_inc(x_used, 1)
                pe.wait_ge(x_ev, b * 4 + 4)
                for c in range(2):
                    for k in range(4):
                        ins = nc.tensor.transpose(bank(6 + c, P * k, P * (k + 1)), vT[:, (4 * c + k) * P:(4 * c + k + 1) * P], ident[:, :])
                    ins.then_inc(vt_ps, 1)
                pe.wait_ge(vt_ev, b * 4 + 4)

                def scores(qt):
                    w = (qt + 1) * P
                    if qt >= 2:
                        pe.wait_ge(s1_p, b * KT + qt - 1)
                    lo = 1024 * (qt % 2)
                    for k0 in range(0, w, 512):
                        k1 = min(w, k0 + 512)
                        ins = mm(PS[:, lo + k0:lo + k1], qT[:, qt * P:(qt + 1) * P], kT[:, k0:k1], stop=k1 != w)
                    ins = mm(PS[:, lo + w - P:lo + w], identb[:, :], mask_qk[:, :], start=False)
                    ins.then_inc(s1_ps, 1)

                def p_transposes(qt):
                    pe.wait_ge(s1_p, b * KT + qt + 1)
                    if qt:
                        pe.wait_ge(pt_ev, b * KT + qt)
                    for k in range(qt + 1):
                        ins = nc.tensor.transpose(PS[:, 2048 + k * P:2048 + (k + 1) * P], P1[:, qt % 2, k * P:(k + 1) * P], ident[:, :])
                    ins.then_inc(pt_ps, 1)

                def values(half):
                    pe.wait_ge(pt_ev, b * KT + 4 * half + 4)
                    for kt in range(4 * half + 4):
                        off = max(0, kt - 4 * half) * P
                        ins = mm(bank(6 + half, off, 512), vtok[:, kt, :], PT[:, kt, off:512], start=kt == 0, stop=kt == 4 * half + 3)
                    ins.then_inc(o1_ps, 1)

                for qt in range(KT):
                    scores(qt)
                    if qt >= 1:
                        p_transposes(qt - 1)
                    if qt == 4:
                        values(0)
                p_transposes(KT - 1)
                values(1)
                for e in range(EXP):
                    pe.wait_ge(ox_made, b * EXP + e + 1)
                    for c in range(2):
                        ins = mm(bank(c), fwo[:, e, :], Xe[:, e % 2, 512 * c:512 * (c + 1)], start=e == 0, stop=e == EXP - 1)
                    ins.then_inc(ox_used, 1)
            pe.wait_ge(hs_ev, 4)
            transposes(lambda t: hsT[:, t * P:(t + 1) * P], 4, lambda c: None)
            transposes(lambda t: ztok[:, t, :], 0, lambda c: pe.wait_ge(z_ready, 12 + c + 1))
            pe.wait_ge(tr_ev, 28)
            gate_products(2, xnT)
            comb_T(2, 5)
            pe.wait_ge(cb_ev, 3)
            with pe.Fori(0, BATCH) as b:
                for u in range(2 * EXP + 2):
                    if u < 2 * EXP:
                        e, c = u // 2, u % 2
                        if u >= 4:
                            pe.wait_ge(i_gelu, b * 16 + u - 3)
                        mm(bank(u % 4), fw1[:, e, :], xnT[:, bass.ds(b * SEQ + 512 * c, 512)]).then_inc(i_ps, 1)
                    if u >= 2:
                        e, c = (u - 2) // 2, u % 2
                        pe.wait_ge(i_g, b * 16 + u - 1)
                        mm(bank(4 + c), fw2[:, e, :], gg[:, (u - 2) % 4, :], start=e == 0, stop=e == EXP - 1).then_inc(i_used, 1)
            for c in range(NC):
                pe.wait_ge(fin_x, c + 1)
                for k in range(4):
                    t = 4 * c + k
                    ins = nc.tensor.transpose(bank(c, P * k, P * (k + 1)), hsT[:, t * P:(t + 1) * P], ident[:, :])
                ins.then_inc(fin_ps, 1)


_NAMES = ["L0_attn_x", "L0_attn_Wq", "L0_attn_bq", "L0_attn_Wk", "L0_attn_bk", "L0_attn_Wv", "L0_attn_bv", "L0_attn_Wp",
          "L0_attn_bp", "L0_attn_temperature", "L0_ffn_expert_bias", "L1_ffn_ln1_w", "L1_ffn_ln1_b", "L1_ffn_ln2_w",
          "L1_ffn_ln2_b", "L1_ffn_smha_sim", "L1_ffn_smha_gates", "L1_ffn_q_proj", "L1_ffn_k_proj", "L1_ffn_v_proj",
          "L1_ffn_o_proj", "L1_ffn_moe_sim", "L1_ffn_moe_gates", "L1_ffn_w1", "L1_ffn_w2"]


def kernel(**inputs):
    import numpy as np
    import concourse.bacc as bacc
    from concourse.bass_utils import run_bass_kernel_spmd

    x = {k: np.asarray(v) for k, v in inputs.items()}
    laid = {n: x[n] for n in _NAMES}
    laid["L1_WQT"], laid["L1_WKT"] = x["L1_attn_W_Q"].T, x["L1_attn_W_K"].T
    laid["L1_WVT"], laid["L1_WOT"] = x["L1_attn_W_V"].T, x["L1_attn_W_O"].T
    laid["router_T"] = x["L0_ffn_router_w"].T
    laid["bias_rev_T"] = x["L0_attn_bias_table"][::-1].T

    def experts(w1, w3, w2):
        down = w2.transpose(0, 2, 1).reshape(w2.shape[0], 2, 128, 128).transpose(0, 2, 1, 3).reshape(w2.shape[0], 128, 256)
        return np.concatenate([w1.transpose(0, 2, 1), w3.transpose(0, 2, 1), down], axis=2)

    shared = experts(x["L0_ffn_sw1"], x["L0_ffn_sw3"], x["L0_ffn_sw2"])
    routed = experts(x["L0_ffn_w1"], x["L0_ffn_w3"], x["L0_ffn_w2"])
    laid["ffn_w"] = np.concatenate([shared[0:1], routed, shared[1:2]], axis=0)

    nc = bacc.Bacc("TRN2", target_bir_lowering=False, num_devices=1)
    arrays, args = {}, {}
    for name, value in laid.items():
        value = np.ascontiguousarray(value)
        arrays["in_" + name] = value
        args[name] = nc.dram_tensor("in_" + name, value.shape, mybir.dt.from_np(value.dtype), kind="ExternalInput").ap()
    out = nc.dram_tensor("out_x", (BATCH, SEQ, C), F32, kind="ExternalOutput").ap()
    block_net(nc, args, out)
    r = run_bass_kernel_spmd(nc, [arrays], core_ids=[0])
    return r.results[0]["out_x"]
```

```python
import math
from contextlib import ExitStack

import concourse.bass as bass
from concourse import mybir

F32 = mybir.dt.float32
BF16 = mybir.dt.bfloat16
ALU = mybir.AluOpType
ACT = mybir.ActivationFunctionType
AX = mybir.AxisListType

P = 128
C = 128
BATCH, SEQ = 2, 1024
TOK = BATCH * SEQ
NT = TOK // P
NC = TOK // 512
HEADS, HD = 16, 8
HG = 4
NG = HEADS // HG
GROUPS = BATCH * NG
KT = SEQ // P
PARTS = 3
STACK = PARTS * PARTS * HD
HID = 256
EXP = 8
FFN_SEQ = EXP + 2
REL = 249
DREV = 384
NEG = -1.0e30
LN_EPS = 1e-5


class Chain:

    def __init__(self, eng, sem):
        self.eng, self.sem, self.n, self.term = eng, sem, 0, 0

    def link(self, ins):
        self.n += 1
        ins.then_inc(self.sem, 1)
        self.eng.wait_ge(self.sem, self.term + self.n)

    def enter(self, it, per):
        self.start, self.per, self.term = self.n, per, it * per

    def leave(self, iters):
        assert self.n - self.start == self.per, (self.n - self.start, self.per)
        self.n, self.term = self.start + self.per * iters, 0


def t_steps(layer):
    if layer == 0:
        return [(h, k, 0) for h in range(2) for k in range(KT)]
    return [(h, k, max(0, k - 4 * h) * P) for h in range(2) for k in range(4 * h + 4)]


def s_units(layer):
    order = list(range(2, KT)) + [0, 1]
    return [(j, q, SEQ if layer == 0 else (q + 1) * P) for q in order for j in range(HG)]


AHEAD = (8, 12)


def s_sequence(layer, first, rest):
    units = s_units(layer)
    seq = [("S", 0, u) for u in units[(0 if first else AHEAD[layer]):]]
    if rest:
        seq += [("S", 1, u) for u in units[:2]]
    seq.append(("M",))
    if rest:
        seq += [("S", 1, u) for u in units[2:AHEAD[layer]]]
    return seq


def ring_plan(layer, carry, s_phase):
    steps = t_steps(layer)
    n = len(steps)
    plan = [[] for _ in range(n)]
    first_of_half1 = next(i for i, s in enumerate(steps) if s[0] == 1)
    if carry:
        plan[3].append(("Q", 1))
        plan[5].append(("R", 1))
    plan[first_of_half1 + 3].append(("Q", 0))
    plan[first_of_half1 + 5].append(("R", 0))
    if s_phase:
        seq = s_sequence(layer, False, True)
        total, done, at = sum(w[2][2] for w in seq if w[0] == "S"), 0, 0
        for what in seq:
            while at < n - 1 and done >= total * (at + 1) / n:
                at += 1
            if what[0] == "M":
                plan[at].append(what)
                continue
            done += what[2][2]
            if what[1] == 0 or s_phase == 2:
                plan[at].append(what)
    return plan


def block_net(nc, a, out):
    ctx = ExitStack()
    with ctx:
        def sb(name, shape, dt=F32):
            return ctx.enter_context(nc.sbuf_tensor(name, shape, dt))

        def sem(name):
            return ctx.enter_context(nc.semaphore(name))

        def dram(name, shape, dt):
            return nc.dram_tensor(name, shape, dt).ap()

        q_dram = [dram(f"q_dram{l}", (GROUPS, HG, PARTS + 2, HD, SEQ), BF16) for l in range(2)]
        k_dram = [dram(f"k_dram{l}", (GROUPS, HG, PARTS, HD, SEQ), BF16) for l in range(2)]
        drev_dram = dram("drev_dram", (GROUPS, HG, PARTS, DREV), BF16)
        comb_dram = [dram(f"comb_dram{n}", (P, P), F32) for n in range(3)]

        PS = ctx.enter_context(nc.psum_tensor("PS", [P, 8 * 512], F32))

        def bank(n, lo=0, hi=512):
            return PS[:, n * 512 + lo:n * 512 + hi]

        xT = sb("xT", [P, TOK])
        xnT = sb("xnT", [P, TOK])
        n1T = sb("n1T", [P, TOK])
        ident = sb("ident", [P, P])
        ones = sb("ones", [P, P])
        sel = sb("sel", [P, P])
        identb = sb("identb", [P, P], BF16)
        flip = sb("flip", [P, P], BF16)
        mask_kq = sb("mask_kq", [P, P], BF16)
        mask_qk = sb("mask_qk", [P, P], BF16)
        tri = sb("tri", [P, EXP, EXP])
        wq = sb("wq", [P, 2, C])
        wk = sb("wk", [P, 2, C])
        wv = sb("wv", [P, 2, C])
        wo = sb("wo", [P, 2, NG, C])
        router = sb("router", [P, 3, EXP])
        simsq = sb("simsq", [P, 2, EXP])
        cols = sb("cols", [P, 10])
        bvb = sb("bvb", [P, C])
        erow = sb("erow", [P, 3, EXP])
        small = sb("small", [P, 10, NT])
        gl = sb("gl", [P, 3, 160])
        combT = sb("combT", [P, P])
        mx = sb("mx", [P, 2, HG * KT])
        sums = sb("sums", [P, 2, 16])
        rsums = sb("rsums", [P, 2, 16])
        mres = sb("mres", [HG * KT, P])
        mrow = sb("mrow", [HG * KT, PARTS, P], BF16)
        fw = sb("fw", [P, 6 * 1024])
        arena = sb("arena", [P, 144 * 256])

        def at(kib, size):
            return arena[:, kib * 256:(kib + size) * 256]

        def bf(kib, size):
            return at(kib, size).bitcast(BF16)

        stack = {n: bf(k, 16).rearrange("p (s j t) -> p s j t", s=2, j=HG)
                 for n, k in (("Sq", 0), ("Sk", 16), ("Tq", 32), ("Tk", 48))}
        V = at(64, 8).rearrange("p (g k c) -> p g k c", g=GROUPS, k=KT)
        sT1 = at(64, 8)
        Vst = at(72, 8).rearrange("p (s k j c) -> p s k j c", s=2, k=KT, j=HG)
        Pr = at(80, 16).rearrange("p (s q) -> p s q", s=8)
        Osb = at(96, 4).rearrange("p (s q) -> p s q", s=2)
        OT = at(100, 32).rearrange("p (g q) -> p g q", g=GROUPS)
        Hst = bf(132, 12).rearrange("p (s j a c) -> p s j a c", s=2, j=HG, a=PARTS)
        xtok = at(32, 8).rearrange("p (t c) -> p t c", t=NT)
        ztok = at(40, 8).rearrange("p (t c) -> p t c", t=NT)
        zz = at(132, 8).rearrange("p (t c) -> p t c", t=NT)
        cmp_a = at(140, 4).rearrange("p (t e f) -> p t e f", t=NT, e=EXP)
        cmp_b = at(96, 4).rearrange("p (t e f) -> p t e f", t=NT, e=EXP)
        q32, k32 = at(80, 8), at(88, 8)
        qsp = bf(100, 12).rearrange("p (a t) -> p a t", a=PARTS)
        ksp = bf(112, 12).rearrange("p (a t) -> p a t", a=PARTS)
        gate_tmp = at(129, 3)
        lg, top2, act_mask, gated = (gate_tmp[:, n * 128:(n + 1) * 128].rearrange("p (t e) -> p t e", e=EXP) for n in range(4))
        comb = gate_tmp[:, 512:640].rearrange("p (e t) -> p e t", e=EXP)
        stats = gate_tmp[:, 640:736].rearrange("p (t n) -> p t n", t=NT)
        tblr = at(124, 5)[0:HEADS, 0:REL]
        dfull = at(124, 5)[0:HEADS, 256:256 + DREV]
        dpart = at(124, 5)[0:HEADS, 640:1216].bitcast(BF16).rearrange("h (a n) -> h a n", a=PARTS)
        cwb = at(100, 16).rearrange("p (s t) -> p s t", s=2)
        fw0 = fw[:, 0:1536].rearrange("p (s n) -> p s n", s=2)
        fa = fw[:, 2048:3072].rearrange("p (s n) -> p s n", s=2)
        fg = fw[:, 3072:5120].rearrange("p (s n) -> p s n", s=4)
        fwq, fwk, fwv, fwo, fw1, fw2 = (fw[:, n * 1024:(n + 1) * 1024].rearrange("p (e c) -> p e c", e=EXP)
                                        for n in range(6))
        rwb = at(0, 64).rearrange("p (e t) -> p e t", e=EXP)
        Xe = at(80, 8).rearrange("p (s t) -> p s t", s=2)
        P1 = at(88, 8).rearrange("p (s t) -> p s t", s=2)
        vtok = at(72, 4).rearrange("p (k c) -> p k c", k=KT)
        qT, kT, vT = at(100, 4), at(104, 4), at(108, 4)
        attnT = at(112, 8)
        hsT = at(120, 8)
        PT = at(128, 16).rearrange("p (k q) -> p k q", k=KT)
        ga = at(80, 8).rearrange("p (s t) -> p s t", s=4)
        gg = at(88, 8).rearrange("p (s t) -> p s t", s=4)
        otok = at(100, 8).rearrange("p (t c) -> p t c", t=NT)

        bq, bk, bp = cols[:, 0:1], cols[:, 1:2], cols[:, 2:3]
        ln_w = [cols[:, 3:4], cols[:, 5:6]]
        ln_b = [cols[:, 4:5], cols[:, 6:7]]
        temp, qscale = cols[:, 7:8], cols[:, 8:9]

        x_in = [sem(f"x_in{c}") for c in range(NC)]
        w_in, fw_in, tbl_in = sem("w_in"), sem("fw_in"), sem("tbl_in")
        zero_done, const_done, ones_set = sem("zero_done"), sem("const_done"), sem("ones_set")
        dve_own, act_own, pool_own = sem("dve_own"), sem("act_own"), sem("pool_own")
        var_ready, rstd_ready = sem("var_ready"), sem("rstd_ready")
        z_ready = sem("z_ready")
        ss_ready, norm_ready = sem("ss_ready"), sem("norm_ready")
        tr_ps, tr_ev = sem("tr_ps"), sem("tr_ev")
        q_ps, k_ps, v_ps = sem("q_ps"), sem("k_ps"), sem("v_ps")
        q_ev, k_ev, v_ev = sem("q_ev"), sem("k_ev"), sem("v_ev")
        hi_done, rest_done, mid_done, split_done = sem("hi_done"), sem("rest_done"), sem("mid_done"), sem("split_done")
        qk_stored = [[sem(f"qk_stored{l}{b}") for b in range(BATCH)] for l in range(2)]
        drev_ready, drev_stored = sem("drev_ready"), sem("drev_stored")
        lg_ps, gx_ready, ge_ready, comb_ready, cb_ps, cb_ev = (sem(n) for n in (
            "lg_ps", "gx_ready", "ge_ready", "comb_ready", "cb_ps", "cb_ev"))
        comb_stored = sem("comb_stored")
        sq_ready, gate_exp, gneg = sem("sq_ready"), sem("gate_exp"), sem("gneg")
        f_w = [sem(f"f_w{s}") for s in range(2)]
        f_c = [sem(f"f_c{s}") for s in range(2)]
        h_ps, a_made, g_made, y_done, y_ev = (sem(n) for n in ("h_ps", "a_made", "g_made", "y_done", "y_ev"))
        att = [{n: sem(f"{n}{l}") for n in (
            "s_ld0", "s_ld1", "t_ld0", "t_ld1", "h_ld0", "h_ld1", "m_ld",
            "ring_full", "ring_free", "st_ps", "e_done", "av_done", "o_ev", "m_ready", "v_staged", "sum_in0", "sum_in1", "sum_inv", "rrow_in", "pj_ps", "pj_ev")}
            for l in range(2)]
        rw_in = [sem(f"rw_in{e}") for e in range(EXP)]
        x_made, x_used, x_ev, vt_ps, vt_ev = (sem(n) for n in ("x_made", "x_used", "x_ev", "vt_ps", "vt_ev"))
        s1_ps, s1_max, s1_exp, s1_p, pt_ps, pt_ev, o1_ps, o1_ev = (sem(n) for n in (
            "s1_ps", "s1_max", "s1_exp", "s1_p", "pt_ps", "pt_ev", "o1_ps", "o1_ev"))
        ox_made, ox_used, hs_ev = sem("ox_made"), sem("ox_used"), sem("hs_ev")
        i_ps, i_gelu, i_g, i_used, moe_ps, moe_ev = (sem(n) for n in ("i_ps", "i_gelu", "i_g", "i_used", "moe_ps", "moe_ev"))
        fin_silu, fin_x, fin_ps, fin_ev, stored = (sem(n) for n in ("fin_silu", "fin_x", "fin_ps", "fin_ev", "stored"))

        W_LOADS = 28
        NS = [len(t_steps(l)) for l in range(2)]

        UNITS = len(s_units(0)) + 1

        def ring_base(l, G):
            first = UNITS + AHEAD[l]
            if isinstance(G, int) and G == 0:
                return first
            last = AHEAD[l] if isinstance(G, int) and G == GROUPS - 1 else 0
            return (G - 1) * (UNITS + 2) + (first + UNITS + 1 - last)

        def ring_after_s(l, G):
            if isinstance(G, int) and G == 0:
                return UNITS + 2
            carry = not (isinstance(G, int) and G == 1)
            n = 0
            for what in (w for step in ring_plan(l, carry, 2) for w in step if w[0] != "Q"):
                n += 1
                if what[0] == "M":
                    break
            return ring_base(l, G - 1) + n

        def groups(eng, body, chain=None, per=0):
            body(0, 0, False, 2)
            with eng.Fori(0, 2) as it:
                if chain:
                    chain.enter(it, per)
                body(it * 2 + 1, 1, True, 2)
                body(it * 2 + 2, 0, True, 2)
            if chain:
                chain.leave(2)
            body(GROUPS - 3, 1, True, 2)
            body(GROUPS - 2, 0, True, 1)
            body(GROUPS - 1, 1, True, 0)

        block = ctx.enter_context(nc.Block())

        @block.sync
        def _(sp):
            x_v = a["L0_attn_x"].rearrange("b (t p) c -> p (b t) c", p=P)
            for c in range(NC):
                sp.dma_start(xtok[:, 4 * c:4 * c + 4, :], x_v[:, 4 * c:4 * c + 4, :]).then_inc(x_in[c], 16)
            n = 0
            sp.wait_ge(zero_done, 1)
            for l in range(2):
                for dst, src in ((wq, ("L0_attn_Wq", "L1_WQT")), (wk, ("L0_attn_Wk", "L1_WKT")), (wv, ("L0_attn_Wv", "L1_WVT"))):
                    sp.dma_start(dst[:, l, :], a[src[l]]).then_inc(w_in, 16)
                    n += 1
                w_v = a[("L0_attn_Wp", "L1_WOT")[l]].rearrange("(g j d) c -> j d g c", g=NG, j=HG)
                for j in range(HG):
                    sp.dma_start(wo[32 * j:32 * j + HD, l, :, :], w_v[j]).then_inc(w_in, 16)
                    n += 1
            for k, name in enumerate(("router_T", "L1_ffn_smha_sim", "L1_ffn_moe_sim")):
                sp.dma_start(router[:, k, :], a[name]).then_inc(w_in, 16)
                n += 1
            for k, name in enumerate(("L0_ffn_expert_bias", "L1_ffn_smha_gates", "L1_ffn_moe_gates")):
                sp.dma_start(erow[:, k, :], a[name].partition_broadcast(P)).then_inc(w_in, 16)
                n += 1
            for k, name in enumerate(("L0_attn_bq", "L0_attn_bk", "L0_attn_bp", "L1_ffn_ln1_w", "L1_ffn_ln1_b",
                                      "L1_ffn_ln2_w", "L1_ffn_ln2_b")):
                sp.dma_start(cols[:, k:k + 1], a[name].rearrange("(p a) -> p a", a=1)).then_inc(w_in, 16)
                n += 1
            sp.dma_start(temp, a["L0_attn_temperature"].partition_broadcast(P)).then_inc(w_in, 16)
            sp.dma_start(bvb[:, :], a["L0_attn_bv"].partition_broadcast(P)).then_inc(w_in, 16)
            n += 2
            assert n == W_LOADS + 1, n
            sp.dma_start(tblr[:, :], a["bias_rev_T"]).then_inc(tbl_in, 16)
            for s in range(2):
                sp.dma_start(fw0[:, s, 0:768], a["ffn_w"][s]).then_inc(f_w[s], 16)

            def store_qk(l, b):
                for which, sp32, dr, order in ((0, qsp, q_dram[l], (0, 1, 2, 0, 1)), (1, ksp, k_dram[l], (0, 1, 2))):
                    sp.wait_ge(split_done, 4 * l + 2 * b + which + 1)
                    for n_, part in enumerate(order):
                        dst = dr[b * NG:(b + 1) * NG, :, n_, :, :].rearrange("g j d t -> (g j) d t")
                        sp.dma_start(dst, sp32[:, part, b * SEQ:(b + 1) * SEQ]).then_inc(qk_stored[l][b], 16)

            def load_stack(l, which, G, parity):
                ld = att[l][f"{which.lower()}_ld{parity}"]
                for j in range(HG):
                    for name, dr, np_, step in (("q", q_dram[l], PARTS + 2, 1), ("k", k_dram[l], PARTS, 0)):
                        src = bass.AP(tensor=dr.tensor, offset=G * (HG * np_ * HD * SEQ) + j * np_ * HD * SEQ,
                                      ap=[[step * HD * SEQ, PARTS], [SEQ, PARTS * HD], [1, SEQ]])
                        sp.dma_start(stack[which + name][0:STACK, parity, j, :], src).then_inc(ld, 16)

            def load_bias(G, parity):
                for j in range(HG):
                    src = bass.AP(tensor=drev_dram.tensor, offset=G * (HG * PARTS * DREV) + j * PARTS * DREV,
                                  ap=[[1, P], [DREV, PARTS], [1, 256]])
                    sp.dma_start(Hst[:, parity, j, :, :], src).then_inc(att[0][f"h_ld{parity}"], 16)

            def load_max(l, G, parity):
                A = att[l]
                sp.wait_ge(A["m_ready"], G + 1)
                for part in range(PARTS):
                    dst = stack["Tq"][STACK + part:STACK + part + 1, parity, :, :].rearrange("p j (q t) -> p (j q) t", t=P)
                    sp.dma_start(dst, mrow[:, part, :]).then_inc(A["m_ld"], 16)

            def attention_loads(l, between=None):
                sp.wait_ge(ones_set, 1)
                sp.wait_ge(qk_stored[l][0], 16 * 8)
                if l == 0:
                    sp.wait_ge(drev_stored, 16 * PARTS * BATCH)
                load_stack(l, "S", 0, 0)
                if between:
                    between()
                if l == 0:
                    load_bias(0, 0)
                load_stack(l, "S", 1, 1)
                if l == 0:
                    load_bias(1, 1)
                load_stack(l, "T", 0, 0)
                if l == 1:
                    sp.wait_ge(z_ready, 12)
                load_stack(l, "T", 1, 1)

            def attention_feed(l, between=None):
                A = att[l]
                NSJ = NS[l] * HG

                def sums_back(G, half):
                    sp.wait_ge(A["sum_inv"], G * 2 + (half + 1))
                    sp.dma_start(Osb[HD:P:32, half, :].rearrange("j (c e) -> j c e", e=16), rsums[:, half, :]).then_inc(A["rrow_in"], 16)

                def feed(G, parity, first, s_next, t_next, between=None):
                    load_max(l, G, parity)
                    if s_next:
                        sp.wait_ge(A["ring_full"], ring_after_s(l, G))
                        load_stack(l, "S", G + 2, parity)
                    if l == 0 and not first and t_next:
                        sp.wait_ge(A["st_ps"], G * NSJ)
                        load_bias(G + 1, 1 - parity)
                    if not first:
                        sums_back(G - 1, 1)
                    if not first and t_next:
                        sp.wait_ge(A["st_ps"], G * NSJ)
                        load_stack(l, "T", G + 1, 1 - parity)
                    if between:
                        between()
                    sums_back(G, 0)

                feed(0, 0, True, True, False)
                with sp.Fori(0, 2) as it:
                    feed(it * 2 + 1, 1, False, True, True)
                    feed(it * 2 + 2, 0, False, True, True)
                feed(5, 1, False, True, True)
                feed(6, 0, False, False, True)
                feed(7, 1, False, False, False, between)
                sums_back(GROUPS - 1, 1)

            for b in range(BATCH):
                store_qk(0, b)
            sp.wait_ge(drev_ready, 1)
            for part in range(PARTS):
                for b in range(BATCH):
                    dst = drev_dram[b * NG:(b + 1) * NG, :, part, :].rearrange("g j n -> (g j) n")
                    sp.dma_start(dst, dpart[:, part, :]).then_inc(drev_stored, 16)
            sp.wait_ge(cb_ev, 1)
            sp.dma_start(comb_dram[0], combT[:, :]).then_inc(comb_stored, 16)
            sp.wait_ge(comb_stored, 16)
            for b in range(BATCH):
                sp.wait_ge(qk_stored[0][b], 16 * 8)
            comb_rows = comb_dram[0].rearrange("(e t) k -> e (t k)", e=EXP)

            def load_gate(e, slot):
                sp.dma_start(cwb[:, slot, :], comb_rows[e].partition_broadcast(P)).then_inc(f_c[slot], 16)

            load_gate(0, 1)

            def next_expert(n, slot, routed):
                sp.wait_ge(y_done, n * 8 + 8)
                sp.dma_start(fw0[:, slot, 0:768], a["ffn_w"][n + 2]).then_inc(f_w[slot], 16)
                if routed:
                    load_gate(n + 1, slot)

            with sp.Fori(0, 3) as it:
                next_expert(it * 2, 0, True)
                next_expert(it * 2 + 1, 1, True)
            next_expert(6, 0, True)
            next_expert(7, 1, False)
            attention_loads(0)
            attention_feed(0)
            sp.wait_ge(y_ev, NC)
            for n_, name in enumerate(("q_proj", "k_proj", "v_proj", "o_proj", "w1", "w2")):
                sp.dma_start(fw[:, n_ * 1024:(n_ + 1) * 1024].rearrange("p (e c) -> p e c", e=EXP),
                             a["L1_ffn_" + name].rearrange("e c h -> c e h")).then_inc(fw_in, 16)
            store_qk(1, 0)
            attention_loads(1, lambda: store_qk(1, 1))
            sp.wait_ge(cb_ev, 2)
            sp.dma_start(comb_dram[1], combT[:, :]).then_inc(comb_stored, 16)
            sp.wait_ge(qk_stored[1][1], 16 * 8)
            rows = [comb_dram[n].rearrange("(e t) k -> e (t k)", e=EXP) for n in (1, 2)]

            def load_rw(n, *experts):
                for e in experts:
                    sp.dma_start(rwb[:, e, :], rows[n][e].partition_broadcast(P)).then_inc(rw_in[e], 16)

            def load_first_rw():
                sp.wait_ge(comb_stored, 32)
                sp.wait_ge(att[1]["ring_full"], ring_after_s(1, GROUPS - 1))
                load_rw(0, 0, 1, 2)

            attention_feed(1, load_first_rw)
            sp.wait_ge(att[1]["st_ps"], (GROUPS - 1) * NS[1] * HG)
            load_rw(0, 3, 4, 6)
            sp.wait_ge(att[1]["st_ps"], GROUPS * NS[1] * HG)
            load_rw(0, 5, 7)
            sp.wait_ge(cb_ev, 3)
            sp.dma_start(comb_dram[2], combT[:, :]).then_inc(comb_stored, 16)
            sp.wait_ge(comb_stored, 48)
            load_rw(1, *range(EXP))
            o_v = out.rearrange("b (t p) c -> p (b t) c", p=P)
            for c in range(NC):
                sp.wait_ge(fin_ev, c + 1)
                sp.dma_start(o_v[:, 4 * c:4 * c + 4, :], otok[:, 4 * c:4 * c + 4, :]).then_inc(stored, 16)
            sp.wait_ge(stored, 16 * NC)

        @block.gpsimd
        def _(pool):
            own = Chain(pool, pool_own)
            g = nc.gpsimd
            g.memset(wo[:, :, :, :], 0.0).then_inc(zero_done, 1)
            for t_ in (ident, sel, identb, flip, mask_kq, mask_qk):
                g.memset(t_[:, :], 0.0)
            g.memset(ones[:, :], 1.0)
            own.link(g.memset(tri[:, :, :], 1.0))
            for t_, pattern, base, mult, op, fill in (
                    (ident, [[-1, P]], 0, 1, ALU.not_equal, 1.0),
                    (identb, [[-1, P]], 0, 1, ALU.not_equal, 1.0),
                    (flip, [[1, P]], -(P - 1), 1, ALU.not_equal, 1.0),
                    (mask_kq, [[1, P]], 0, -1, ALU.is_ge, NEG),
                    (mask_qk, [[-1, P]], 0, 1, ALU.is_ge, NEG)):
                g.affine_select(out=t_[:, :], in_=t_[:, :], compare_op=op, fill=fill, base=base,
                                pattern=pattern, channel_multiplier=mult)
            sel_v = sel[:, :].rearrange("p (j d) -> p j d", j=HG)
            g.affine_select(out=sel_v, in_=sel_v, compare_op=ALU.not_equal, fill=1.0, base=-HD,
                            pattern=[[-32, HG], [0, 32]], channel_multiplier=1)
            g.affine_select(out=tri[:, :, :], in_=tri[:, :, :], compare_op=ALU.is_gt, fill=0.0, base=0,
                            pattern=[[1, EXP], [-1, EXP]], channel_multiplier=0).then_inc(const_done, 1)

            def attention(l):
                A = att[l]
                pool.wait_ge(v_ev, 4 * (l + 1))

                def stage(G, parity):
                    src = V[:, G, :, :].rearrange("p k (j c) -> p k j c", j=HG)
                    g.tensor_copy(Vst[:, parity, :, :, 0:HD], src).then_inc(A["v_staged"], 1)

                def body(G, parity, carry, s_phase):
                    if s_phase:
                        if carry:
                            pool.wait_ge(A["av_done"], G * NS[l])
                        stage(G + 1, 1 - parity)

                stage(0, 0)
                groups(pool, body)

            pool.wait_ge(const_done, 1)
            g.memset(stack["Tk"][64:96, :, :, :], 1.0).then_inc(ones_set, 1)
            pool.wait_ge(ones_set, 1)
            own.link(g.memset(Vst[:, :, :, :, :], 0.0))
            own.link(g.memset(Vst[:, :, :, :, HD:HD + 1], 1.0))
            attention(0)
            attention(1)

        @block.scalar
        def _(act):
            s = nc.scalar

            def copies(first, dst, count_from):
                for c in range(NC):
                    act.wait_ge(tr_ps, count_from + c + 1)
                    s.activation(dst(c), bank(first + c), ACT.Copy).then_inc(tr_ev, 1)

            def split_hi(l, b):
                part = slice(b * SEQ, (b + 1) * SEQ)
                for n, (src, dst) in enumerate(((q32, qsp), (k32, ksp))):
                    act.wait_ge(q_ev if n == 0 else k_ev, 4 * l + 2 * b + 2)
                    s.activation(dst[:, 0, part], src[:, part], ACT.Copy).then_inc(hi_done, 1)
                for n, (src, dst) in enumerate(((q32, qsp), (k32, ksp))):
                    act.wait_ge(rest_done, 4 * l + 2 * b + n + 1)
                    s.activation(dst[:, 1, part], src[:, part], ACT.Copy).then_inc(mid_done, 1)

            def gate_exps(n):
                act.wait_ge(gx_ready, n)
                s.activation(gated[:, :, :], gated[:, :, :], ACT.Exp).then_inc(ge_ready, 1)

            def attention(l):
                A = att[l]
                steps = t_steps(l)
                n_exp = len(steps) * HG

                def evac(G, half):
                    if half == 0:
                        act.wait_ge(A["av_done"], G * len(steps) + sum(1 for x in steps if x[0] == 0))
                    else:
                        act.wait_ge(A["av_done"], (G + 1) * len(steps))
                    s.activation(Osb[:, half, :], bank(7), ACT.Copy).then_inc(A["o_ev"], 1)
                    act.wait_ge(A["o_ev"], G * 2 + (half + 1))
                    act.dma_start(sums[:, half, :], Osb[HD:P:32, half, :].rearrange("j (c e) -> j c e", e=16)).then_inc(A[f"sum_in{half}"], 16)

                def body(G, parity, carry, s_phase):
                    first_of_half1 = next(i for i, x in enumerate(steps) if x[0] == 1)
                    for i, (h, kt, off) in enumerate(steps):
                        for j in range(HG):
                            m = HG * i + j
                            act.wait_ge(A["st_ps"], G * n_exp + m + 1)
                            if i >= 2:
                                act.wait_ge(A["av_done"], G * len(steps) + i - 1)
                            elif carry:
                                act.wait_ge(A["av_done"], G * len(steps) + i - 1)
                            w = 512 - off
                            s.activation(Pr[:, m % 8, 0:w], bank(4 + m % 3, 0, w), ACT.Exp).then_inc(A["e_done"], 1)
                        if i == 0 and carry:
                            act.wait_ge(A["ring_free"], ring_base(l, G))
                            evac(G - 1, 1)
                        if i == first_of_half1:
                            if carry:
                                act.wait_ge(A["ring_free"], ring_base(l, G))
                            evac(G, 0)

                groups(act, body)
                act.wait_ge(A["ring_free"], ring_base(l, GROUPS - 1) + 2)
                evac(GROUPS - 1, 1)

            def root_var(n):
                act.wait_ge(var_ready, n)
                s.activation(small[:, 2, :], small[:, 1, :], ACT.Sqrt).then_inc(rstd_ready, 1)

            def root_squares(n):
                act.wait_ge(ss_ready, n)
                s.activation(gl[:, n, 128:152], gl[:, n, 128:152], ACT.Sqrt).then_inc(norm_ready, 1)

            act.wait_ge(const_done, 1)
            copies(4, lambda c: xT[:, 512 * c:512 * (c + 1)], 0)
            root_var(1)
            copies(0, lambda c: xnT[:, 512 * c:512 * (c + 1)], 4)
            act.wait_ge(w_in, 16 * (W_LOADS + 1))
            for b in range(BATCH):
                for c in (2 * b, 2 * b + 1):
                    act.wait_ge(k_ps, c + 1)
                    s.activation(k32[:, 512 * c:512 * (c + 1)], bank(c), ACT.Identity, bias=bk).then_inc(k_ev, 1)
                split_hi(0, b)
            gate_exps(1)
            s.activation(gl[:, 0, 0:2 * EXP], erow[:, 1:3, :].rearrange("p a e -> p (a e)"), ACT.Exp, scale=-1.0).then_inc(gate_exp, 1)

            def silu_units(n_term, base):
                for u in range(8):
                    act.wait_ge(h_ps, n_term + base + u + 1)
                    if not (isinstance(n_term, int) and base + u < 2):
                        act.wait_ge(g_made, n_term + base + u - 1)
                    s.activation(fa[:, u % 2, :], bank(2 * (u % 2)), ACT.Silu).then_inc(a_made, 1)

            silu_units(0, 0)
            with act.Fori(0, 4) as it:
                silu_units(it * 16, 8)
                silu_units(it * 16, 16)
            silu_units(0, 72)
            act.wait_ge(y_done, 8 * FFN_SEQ)
            for c in range(NC):
                s.activation(n1T[:, 512 * c:512 * (c + 1)], bank(4 + c), ACT.Silu).then_inc(y_ev, 1)
            attention(0)

            copies(4, lambda c: xtok[:, 4 * c:4 * c + 4, :].rearrange("p t c -> p (t c)"), 8)
            root_var(2)
            copies(0, lambda c: xnT[:, 512 * c:512 * (c + 1)], 12)
            for b in range(BATCH):
                for c in (2 * b, 2 * b + 1):
                    act.wait_ge(k_ps, 4 + c + 1)
                    s.activation(k32[:, 512 * c:512 * (c + 1)], bank(4 + c), ACT.Copy).then_inc(k_ev, 1)
                split_hi(1, b)
            root_var(3)
            for c in range(NC):
                act.wait_ge(tr_ps, 16 + c + 1)
                s.activation(n1T[:, 512 * c:512 * (c + 1)], bank(4 + c), ACT.Identity, bias=ln_b[0], scale=ln_w[0]).then_inc(tr_ev, 1)
            act.wait_ge(tr_ev, 20)
            s.activation(zz.rearrange("p t c -> p (t c)"), n1T[:, :], ACT.Square).then_inc(sq_ready, 1)
            root_squares(1)
            gate_exps(2)
            attention(1)
            for c in range(NC):
                act.wait_ge(att[1]["pj_ps"], c + 1)
                if c == 0:
                    act.wait_ge(att[1]["v_staged"], GROUPS)
                s.activation(sT1[:, 512 * c:512 * (c + 1)], bank(c), ACT.Copy).then_inc(att[1]["pj_ev"], 1)

            with act.Fori(0, BATCH) as b:
                act.wait_ge(x_used, b * EXP + EXP)
                for c in range(2):
                    s.activation(qT[:, 512 * c:512 * (c + 1)], bank(c), ACT.Copy, scale=1.0 / math.sqrt(C)).then_inc(x_ev, 1)
                for c in range(2):
                    s.activation(vT[:, 512 * c:512 * (c + 1)], bank(4 + c), ACT.Copy).then_inc(x_ev, 1)
                for qt in range(KT):
                    act.wait_ge(s1_max, b * KT + qt + 1)
                    if qt >= 2:
                        act.wait_ge(pt_ps, b * KT + qt - 1)
                    w = (qt + 1) * P
                    s.activation(P1[:, qt % 2, 0:w], PS[:, 1024 * (qt % 2):1024 * (qt % 2) + w], ACT.Exp,
                                 bias=small[:, 4, qt:qt + 1], accum_out=small[:, 5, qt:qt + 1]).then_inc(s1_exp, 1)
                    if qt in (4, 7):
                        half = 0 if qt == 4 else 1
                        act.wait_ge(o1_ps, b * 2 + half + 1)
                        s.activation(attnT[:, bass.ds(b * SEQ + 512 * half, 512)], bank(6 + half), ACT.Copy).then_inc(o1_ev, 1)
            copies(4, lambda c: xtok[:, 4 * c:4 * c + 4, :].rearrange("p t c -> p (t c)"), 20)
            root_var(4)
            for c in range(NC):
                act.wait_ge(tr_ps, 24 + c + 1)
                s.activation(xnT[:, 512 * c:512 * (c + 1)], bank(c), ACT.Identity, bias=ln_b[1], scale=ln_w[1]).then_inc(tr_ev, 1)
            act.wait_ge(tr_ev, 28)
            s.activation(zz.rearrange("p t c -> p (t c)"), xnT[:, :], ACT.Square).then_inc(sq_ready, 1)
            root_squares(2)
            gate_exps(3)
            with act.Fori(0, BATCH) as b:
                for u in range(2 * EXP):
                    act.wait_ge(i_ps, b * 16 + u + 1)
                    s.activation(ga[:, u % 4, :], bank(u % 4), ACT.Gelu).then_inc(i_gelu, 1)
            for c in range(NC):
                act.wait_ge(moe_ev, c + 1)
                s.activation(hsT[:, 512 * c:512 * (c + 1)], hsT[:, 512 * c:512 * (c + 1)], ACT.Silu).then_inc(fin_silu, 1)
            for c in range(NC):
                act.wait_ge(fin_ps, c + 1)
                s.activation(otok[:, 4 * c:4 * c + 4, :].rearrange("p t c -> p (t c)"), bank(c), ACT.Copy).then_inc(fin_ev, 1)

        @block.vector
        def _(dve):
            own = Chain(dve, dve_own)
            v = nc.vector
            mean, var, rs, dd = small[:, 0, :], small[:, 1, :], small[:, 2, :], small[:, 3, :]

            def layer_norm(n, src, dst, ready=None):
                for t in range(NT):
                    if ready and t % 4 == 0:
                        ready(t // 4)
                    ins = v.bn_stats(stats[:, t, :], src[:, t, :])
                own.link(ins)
                own.link(v.tensor_tensor(dd, stats[:, :, 1], stats[:, :, 4], ALU.add))
                own.link(v.tensor_scalar(mean, dd, 0.5, None, ALU.mult))
                own.link(v.tensor_tensor(dd, stats[:, :, 1], stats[:, :, 4], ALU.subtract))
                own.link(v.scalar_tensor_tensor(dd, dd, 0.25, dd, ALU.mult, ALU.mult))
                own.link(v.tensor_tensor(var, stats[:, :, 2], stats[:, :, 5], ALU.add))
                own.link(v.scalar_tensor_tensor(var, var, 1.0 / C, dd, ALU.mult, ALU.add))
                v.tensor_scalar(var, var, LN_EPS, None, ALU.add).then_inc(var_ready, 1)
                dve.wait_ge(rstd_ready, n)
                own.link(v.reciprocal(rs, rs))
                for t in range(NT):
                    ins = v.tensor_scalar(dst[:, t, :], src[:, t, :], mean[:, t:t + 1], rs[:, t:t + 1], ALU.subtract, ALU.mult)
                    if t % 4 == 3:
                        ins.then_inc(z_ready, 1)

            def split_rest(l, b):
                part = slice(b * SEQ, (b + 1) * SEQ)
                for n, (src, dst) in enumerate(((q32, qsp), (k32, ksp))):
                    dve.wait_ge(hi_done, 4 * l + 2 * b + n + 1)
                    v.tensor_tensor(src[:, part], src[:, part], dst[:, 0, part], ALU.subtract).then_inc(rest_done, 1)
                for n, (src, dst) in enumerate(((q32, qsp), (k32, ksp))):
                    dve.wait_ge(mid_done, 4 * l + 2 * b + n + 1)
                    v.tensor_tensor(dst[:, 2, part], src[:, part], dst[:, 1, part], ALU.subtract).then_inc(split_done, 1)

            def per_token(x):
                return x.unsqueeze(2).to_broadcast([P, NT, EXP])

            def per_expert(x):
                return x.unsqueeze(1).to_broadcast([P, NT, EXP])

            def gate(n):
                own.link(v.tensor_tensor(cmp_a, lg[:, :, :].unsqueeze(2).to_broadcast([P, NT, EXP, EXP]),
                                         lg[:, :, :].unsqueeze(3).to_broadcast([P, NT, EXP, EXP]), ALU.is_gt))
                own.link(v.tensor_tensor(cmp_b, lg[:, :, :].unsqueeze(2).to_broadcast([P, NT, EXP, EXP]),
                                         lg[:, :, :].unsqueeze(3).to_broadcast([P, NT, EXP, EXP]), ALU.is_equal))
                own.link(v.tensor_tensor(cmp_b, cmp_b, tri[:, :, :].unsqueeze(1).to_broadcast([P, NT, EXP, EXP]), ALU.mult))
                own.link(v.tensor_tensor(cmp_a, cmp_a, cmp_b, ALU.add))
                own.link(v.reduce_sum(top2[:, :, :], cmp_a, axis=AX.X))
                own.link(v.tensor_scalar(top2[:, :, :], top2[:, :, :], 1.5, None, ALU.is_lt))
                src = lg
                if n:
                    own.link(v.tensor_scalar(act_mask[:, :, :], lg[:, :, :], 0.0, None, ALU.is_gt))
                    own.link(v.reduce_max(small[:, 6, :], act_mask[:, :, :], axis=AX.X))
                    own.link(v.tensor_scalar(small[:, 6, :], small[:, 6, :], 0.5, None, ALU.is_lt))
                    own.link(v.tensor_tensor(top2[:, :, :], top2[:, :, :], per_token(small[:, 6, :]), ALU.mult))
                    own.link(v.tensor_tensor(top2[:, :, :], top2[:, :, :], act_mask[:, :, :], ALU.max))
                    own.link(v.tensor_scalar(lg[:, :, :], lg[:, :, :], 0.0, None, ALU.max))
                own.link(v.reduce_max(small[:, 7, :], src[:, :, :], axis=AX.X))
                v.tensor_tensor(gated[:, :, :], src[:, :, :], per_token(small[:, 7, :]), ALU.subtract).then_inc(gx_ready, 1)
                dve.wait_ge(ge_ready, n + 1)
                own.link(v.tensor_tensor(gated[:, :, :], gated[:, :, :], top2[:, :, :], ALU.mult))
                own.link(v.reduce_sum(small[:, 8, :], gated[:, :, :], axis=AX.X))
                own.link(v.reciprocal(small[:, 9, :], small[:, 8, :]))
                if n:
                    dve.wait_ge(comb_stored, 16 * n)
                v.tensor_tensor(comb[:, :, :].rearrange("p e t -> p t e"), gated[:, :, :], per_token(small[:, 9, :]),
                                ALU.mult).then_inc(comb_ready, 1)
                dve.wait_ge(cb_ps, n + 1)
                v.tensor_copy(combT[:, :], bank((1, 5, 5)[n], 0, P)).then_inc(cb_ev, 1)

            def gate_logits(n):
                dve.wait_ge(lg_ps, n + 1)
                v.tensor_copy(gl[:, n, 0:152], bank(4, 0, 152)).then_inc(ss_ready, 1)
                dve.wait_ge(norm_ready, n)
                own.link(v.tensor_scalar(gl[:, n, 128:152], gl[:, n, 128:152], 1e-12, None, ALU.max))
                own.link(v.reciprocal(gl[:, n, 128:152], gl[:, n, 128:152]))
                raw = gl[:, n, 0:128].rearrange("p (t e) -> p t e", e=EXP)
                own.link(v.tensor_tensor(lg[:, :, :], raw, per_token(gl[:, n, 128:144]), ALU.mult))
                own.link(v.tensor_tensor(lg[:, :, :], lg[:, :, :], per_expert(gl[:, n, 144:152]), ALU.mult))
                own.link(v.tensor_tensor(lg[:, :, :], lg[:, :, :], per_expert(erow[:, n, :]), ALU.subtract))

            def attention(l):
                A = att[l]

                def unit(U, parity, what, mpar):
                    dve.wait_ge(A["ring_full"], U + 1)
                    lo = 1024 * parity
                    if what[0] == "S":
                        j, q, w = what[2]
                        mpar = (mpar + what[1]) % 2
                        v.reduce_max(mx[:, mpar, j * KT + q:j * KT + q + 1], PS[:, lo:lo + w], axis=AX.X).then_inc(A["ring_free"], 1)
                    elif what[0] == "R":
                        G, half = what[1]
                        dst = OT[:, G, 512 * half:512 * (half + 1)]
                        v.tensor_tensor(dst, Osb[:, half, :], PS[:, lo:lo + 512], ALU.mult).then_inc(A["ring_free"], 1)
                    else:
                        G = what[1]
                        n = HG * KT
                        src = PS[0:n, lo:lo + P]
                        if not (isinstance(G, int) and G == 0):
                            dve.wait_ge(A["m_ld"], G * 48)
                        own.link(v.tensor_scalar(mrow[:, 0, :], src, -1.0, None, ALU.mult))
                        v.scalar_tensor_tensor(mres[:, :], src, -1.0, mrow[:, 0, :], ALU.mult, ALU.subtract).then_inc(A["ring_free"], 1)
                        dve.wait_ge(A["ring_free"], U + 1)
                        own.link(v.tensor_copy(mrow[:, 1, :], mres[:, :]))
                        v.tensor_tensor(mrow[:, 2, :], mres[:, :], mrow[:, 1, :], ALU.subtract).then_inc(A["m_ready"], 1)

                def invert(G, half):
                    dve.wait_ge(A[f"sum_in{half}"], G * 16 + 16)
                    v.reciprocal(rsums[:, half, :], sums[:, half, :]).then_inc(A["sum_inv"], 1)

                def units(G, U, parity, plan, mpar):
                    n = 0
                    for step in plan:
                        for what in step:
                            if what[0] == "Q":
                                invert(G - 1 if what[1] else G, what[1])
                                continue
                            if what[0] == "R":
                                what = ("R", (G - 1 if what[1] else G, what[1]))
                            if what[0] == "M":
                                what = ("M", G + 1)
                            unit(U + n, (parity + n) % 2, what, mpar)
                            n += 1

                def body(G, parity, carry, s_phase):
                    base = ring_base(l, G)
                    base_parity = (base if isinstance(G, int) else ring_base(l, 2 - parity)) % 2
                    units(G, base, base_parity, ring_plan(l, carry, s_phase), 1 - parity)

                units(-1, 0, 0, [s_sequence(l, True, True)], 0)
                groups(dve, body, own, 4)
                invert(GROUPS - 1, 1)
                last = ring_base(l, GROUPS - 1) + 2
                unit(last, last % 2, ("R", (GROUPS - 1, 1)), 0)

            def x_ready(c):
                dve.wait_ge(x_in[c], 16)

            layer_norm(1, xtok, ztok, x_ready)
            dve.wait_ge(w_in, 16 * (W_LOADS + 1))
            own.link(v.tensor_scalar(qscale, temp, 0.1, 10.0, ALU.max, ALU.min))
            own.link(v.tensor_scalar(qscale, qscale, math.sqrt(C), None, ALU.mult))
            own.link(v.reciprocal(qscale, qscale))

            def values(l, first):
                for c in range(NC):
                    dve.wait_ge(v_ps, 4 * l + c + 1)
                    b, k0 = c // 2, 4 * (c % 2)
                    dst = V[:, b * NG:(b + 1) * NG, k0:k0 + 4, :].rearrange("p g k c -> p k g c")
                    src = bank(first + c).rearrange("p (k g c) -> p k g c", k=4, g=NG)
                    if l == 0:
                        bias = bvb[:, :].rearrange("p (g c) -> p g c", g=NG).unsqueeze(1).to_broadcast([P, 4, NG, 32])
                        v.tensor_tensor(dst, src, bias, ALU.add).then_inc(v_ev, 1)
                    else:
                        v.tensor_copy(dst, src).then_inc(v_ev, 1)

            for b in range(BATCH):
                for c in (2 * b, 2 * b + 1):
                    dve.wait_ge(q_ps, c + 1)
                    v.tensor_scalar(q32[:, 512 * c:512 * (c + 1)], bank(4 + c), bq, qscale, ALU.add, ALU.mult).then_inc(q_ev, 1)
                split_rest(0, b)
            values(0, 4)
            dve.wait_ge(tbl_in, 16)
            own.link(v.memset(dfull[:, :], 0.0))
            own.link(v.tensor_scalar(dfull[:, DREV - 1 - REL:DREV - 1], tblr[:, :], tblr[:, 0:1], qscale[0:HEADS, :],
                                     ALU.subtract, ALU.mult))
            own.link(v.tensor_copy(dpart[:, 0, :], dfull[:, :]))
            own.link(v.tensor_tensor(dfull[:, :], dfull[:, :], dpart[:, 0, :], ALU.subtract))
            own.link(v.tensor_copy(dpart[:, 1, :], dfull[:, :]))
            v.tensor_tensor(dpart[:, 2, :], dfull[:, :], dpart[:, 1, :], ALU.subtract).then_inc(drev_ready, 1)
            dve.wait_ge(lg_ps, 1)
            dve.wait_ge(const_done, 1)
            own.link(v.tensor_tensor(lg[:, :, :], bank(0, 0, 128).rearrange("p (t e) -> p t e", e=EXP),
                                     per_expert(erow[:, 0, :]), ALU.add))
            gate(0)
            dve.wait_ge(gate_exp, 1)
            own.link(v.tensor_scalar(gl[:, 0, 0:2 * EXP], gl[:, 0, 0:2 * EXP], 1.0, None, ALU.add))
            own.link(v.reciprocal(erow[:, 1:3, :].rearrange("p a e -> p (a e)"), gl[:, 0, 0:2 * EXP]))
            v.tensor_tensor(simsq[:, :, :], router[:, 1:3, :], router[:, 1:3, :], ALU.mult).then_inc(gneg, 1)

            def ffn_units(n_term, base, slot, routed):
                for u in range(8):
                    U = base + u
                    dve.wait_ge(a_made, n_term + U + 1)
                    if not (isinstance(n_term, int) and U < 4):
                        dve.wait_ge(y_done, n_term + U - 3)
                    g_ = fg[:, u % 4, :]
                    ins = v.tensor_tensor(g_, bank(2 * (u % 2) + 1), fa[:, u % 2, :], ALU.mult)
                    if routed is not None:
                        own.link(ins)
                        if u == 0:
                            dve.wait_ge(f_c[slot], routed)
                        ins = v.tensor_tensor(g_, g_, cwb[:, slot, 512 * (u // 2):512 * (u // 2 + 1)], ALU.mult)
                    ins.then_inc(g_made, 1)

            ffn_units(0, 0, 0, None)
            with dve.Fori(0, 4) as it:
                own.enter(it, 16)
                ffn_units(it * 16, 8, 1, it * 16 + 16)
                ffn_units(it * 16, 16, 0, it * 16 + 16)
            own.leave(4)
            ffn_units(0, 72, 1, None)
            attention(0)
            for c in range(NC):
                dve.wait_ge(att[0]["pj_ps"], c + 1)
                part = slice(512 * c, 512 * (c + 1))
                dve.wait_ge(y_ev, c + 1)
                own.link(v.scalar_tensor_tensor(n1T[:, part], bank(c), bp, n1T[:, part], ALU.add, ALU.mult))
                v.tensor_tensor(xT[:, part], xT[:, part], n1T[:, part], ALU.add).then_inc(att[0]["pj_ev"], 1)

            layer_norm(2, xtok, ztok, lambda c: dve.wait_ge(tr_ev, 8 + c + 1))
            for b in range(BATCH):
                for c in (2 * b, 2 * b + 1):
                    dve.wait_ge(q_ps, 4 + c + 1)
                    v.tensor_scalar(q32[:, 512 * c:512 * (c + 1)], bank(c), 1.0 / math.sqrt(HD), None, ALU.mult).then_inc(q_ev, 1)
                split_rest(1, b)
            values(1, 0)
            dve.wait_ge(z_ready, 8)
            layer_norm(3, ztok, zz)
            gate_logits(1)
            gate(1)
            attention(1)

            dve.wait_ge(att[1]["pj_ev"], NC)
            with dve.Fori(0, BATCH) as b:
                own.enter(b, 16)
                tok = bass.ds(b * SEQ, SEQ)
                for e in range(EXP):
                    if e >= 2:
                        dve.wait_ge(x_used, b * EXP + e - 1)
                    dve.wait_ge(rw_in[e], 16)
                    v.tensor_tensor(Xe[:, e % 2, :], n1T[:, tok], rwb[:, e, tok], ALU.mult).then_inc(x_made, 1)
                dve.wait_ge(x_used, b * EXP + EXP)
                for c in range(2):
                    v.tensor_copy(kT[:, 512 * c:512 * (c + 1)], bank(2 + c)).then_inc(vt_ev, 1)
                for c in range(2):
                    dve.wait_ge(vt_ps, b * 2 + c + 1)
                    v.tensor_copy(vtok[:, 4 * c:4 * c + 4, :].rearrange("p k c -> p (k c)"), bank(6 + c)).then_inc(vt_ev, 1)
                for i in range(KT + 1):
                    if i < KT:
                        w = (i + 1) * P
                        dve.wait_ge(s1_ps, b * KT + i + 1)
                        own.link(v.reduce_max(small[:, 3, i:i + 1], PS[:, 1024 * (i % 2):1024 * (i % 2) + w], axis=AX.X))
                        v.tensor_scalar(small[:, 4, i:i + 1], small[:, 3, i:i + 1], -1.0, None, ALU.mult).then_inc(s1_max, 1)
                        dve.wait_ge(s1_exp, b * KT + i + 1)
                        own.link(v.reciprocal(small[:, 6, i:i + 1], small[:, 5, i:i + 1]))
                        v.tensor_scalar(P1[:, i % 2, 0:w], P1[:, i % 2, 0:w], small[:, 6, i:i + 1], None, ALU.mult).then_inc(s1_p, 1)
                    if i >= 1:
                        q = i - 1
                        dve.wait_ge(pt_ps, b * KT + q + 1)
                        if q == 4:
                            dve.wait_ge(o1_ps, b * 2 + 1)
                        src = PS[:, 2048:2048 + (q + 1) * P].rearrange("p (k q) -> p k q", q=P)
                        v.tensor_copy(PT[:, 0:q + 1, (q % 4) * P:(q % 4 + 1) * P], src).then_inc(pt_ev, 1)
                for e in range(EXP):
                    if e == 0:
                        dve.wait_ge(o1_ev, b * 2 + 2)
                    if e >= 2:
                        dve.wait_ge(ox_used, b * EXP + e - 1)
                    v.tensor_tensor(Xe[:, e % 2, :], attnT[:, tok], rwb[:, e, tok], ALU.mult).then_inc(ox_made, 1)
                dve.wait_ge(ox_used, b * EXP + EXP)
                for c in range(2):
                    sl = bass.ds(b * SEQ + 512 * c, 512)
                    v.tensor_tensor(hsT[:, sl], bank(c), xnT[:, sl], ALU.add).then_inc(hs_ev, 1)
            own.leave(2)
            layer_norm(4, xtok, ztok, lambda c: dve.wait_ge(tr_ev, 20 + c + 1))
            gate_logits(2)
            gate(2)
            with dve.Fori(0, BATCH) as b:
                for u in range(2 * EXP):
                    e, c = u // 2, u % 2
                    dve.wait_ge(i_gelu, b * 16 + u + 1)
                    if u >= 4:
                        dve.wait_ge(i_used, b * 16 + u - 3)
                    dve.wait_ge(rw_in[e], 32)
                    v.tensor_tensor(gg[:, u % 4, :], ga[:, u % 4, :], rwb[:, e, bass.ds(b * SEQ + 512 * c, 512)], ALU.mult).then_inc(i_g, 1)
                dve.wait_ge(i_used, b * 16 + 16)
                for c in range(2):
                    sl = bass.ds(b * SEQ + 512 * c, 512)
                    v.tensor_tensor(hsT[:, sl], bank(4 + c), hsT[:, sl], ALU.add).then_inc(moe_ev, 1)
            for c in range(NC):
                part = slice(512 * c, 512 * (c + 1))
                dve.wait_ge(fin_silu, c + 1)
                own.link(v.tensor_tensor(hsT[:, part], hsT[:, part], sT1[:, part], ALU.mult))
                v.tensor_tensor(hsT[:, part], hsT[:, part], xT[:, part], ALU.add).then_inc(fin_x, 1)

        @block.tensor
        def _(pe):
            def mm(out_, lhsT, rhs, start=True, stop=True):
                return nc.tensor.matmul(out_, lhsT, rhs, start=start, stop=stop)

            def transposes(src, first, ready):
                for c in range(NC):
                    ready(c)
                    for k in range(4):
                        ins = nc.tensor.transpose(bank(first + c, P * k, P * (k + 1)), src(4 * c + k), ident[:, :])
                    ins.then_inc(tr_ps, 1)

            def project_qk(l, q_first, k_first, ready):
                for b in range(BATCH):
                    for w, first, done in ((wq, q_first, q_ps), (wk, k_first, k_ps)):
                        for c in (2 * b, 2 * b + 1):
                            ready(c)
                            mm(bank(first + c), w[:, l, :], xnT[:, 512 * c:512 * (c + 1)]).then_inc(done, 1)

            def project_v(l, first, ready):
                for c in range(NC):
                    ready(c)
                    for k in range(4):
                        t = 4 * c + k
                        ins = mm(bank(first + c, P * k, P * (k + 1)), xnT[:, t * P:(t + 1) * P], wv[:, l, :])
                    ins.then_inc(v_ps, 1)

            def comb_T(n, b_):
                pe.wait_ge(comb_ready, n + 1)
                nc.tensor.transpose(bank(b_, 0, P), comb[:, :, :].rearrange("p e t -> p (e t)"), ident[:, :]).then_inc(cb_ps, 1)

            def gate_products(n, srcT):
                pe.wait_ge(sq_ready, n)
                pe.wait_ge(gneg, 1)
                sq = zz.rearrange("p t c -> p (t c)")
                for t in range(NT):
                    mm(bank(4, 8 * t, 8 * t + 8), srcT[:, t * P:(t + 1) * P], router[:, n, :])
                    mm(bank(4, 128 + t, 129 + t), sq[:, t * P:(t + 1) * P], ones[:, 0:1])
                mm(bank(4, 144, 152), ones[:, :], simsq[:, n - 1, :]).then_inc(lg_ps, 1)

            def attention(l):
                A = att[l]
                steps = t_steps(l)
                n_st = len(steps) * HG
                half0 = sum(1 for x in steps if x[0] == 0)

                def s_unit(U, parity, j, q, w, slot):
                    lo = 1024 * parity
                    queries = stack["Sq"][0:STACK, slot, j, q * P:(q + 1) * P]
                    for k0 in range(0, w, 512):
                        k1 = min(w, k0 + 512)
                        extra = []
                        if l == 0 and q < 2 and k0 == 512:
                            h0 = 256 if q == 0 else 384
                            extra = [(h0, flip[:, :], Hst[:, slot, j, part, 0:512 - h0]) for part in range(PARTS)]
                        if l == 1 and k1 == w:
                            extra = [(k1 - k0 - P, identb[:, :], mask_qk[:, :])]
                        ins = mm(PS[:, lo + k0:lo + k1], queries, stack["Sk"][0:STACK, slot, j, k0:k1], stop=not extra)
                        for n, (c0, lhsT, rhs) in enumerate(extra):
                            ins = mm(PS[:, lo + k0 + c0:lo + k1], lhsT, rhs, start=False, stop=n == len(extra) - 1)
                    ins.then_inc(A["ring_full"], 1)

                def unit(U, parity, what, slot, last_m=False):
                    if not (isinstance(U, int) and U < 2):
                        pe.wait_ge(A["ring_free"], U - 1)
                    if what[0] == "S":
                        s_unit(U, parity, *what[2], (slot + what[1]) % 2)
                    elif what[0] == "R":
                        G, half = what[1]
                        pe.wait_ge(A["rrow_in"], G * 32 + 16 * half + 16)
                        mm(PS[:, 1024 * parity:1024 * parity + 512], sel[:, :], Osb[:, half, :]).then_inc(A["ring_full"], 1)
                    else:
                        pe.wait_ge(A["ring_free"], U if last_m else U - 1)
                        nc.tensor.transpose(PS[0:HG * KT, 1024 * parity:1024 * parity + P], mx[:, slot, :], ident[:, :])\
                            .then_inc(A["ring_full"], 1)

                def st_step(G, i, parity, carry, heads):
                    h, kt, off = steps[i]
                    for j in heads:
                        m = HG * i + j
                        if m >= 3:
                            pe.wait_ge(A["e_done"], G * n_st + m - 2)
                        elif carry:
                            pe.wait_ge(A["e_done"], G * n_st)
                        w = 512 - off
                        q0 = 512 * h + off
                        dst = bank(4 + m % 3, 0, w)
                        extra = []
                        if l == 0 and h == 0 and kt == KT - 2:
                            extra = [(0, Hst[:, parity, j, part, 0:P], flip[:, :]) for part in range(PARTS)]
                        if l == 0 and h == 0 and kt == KT - 1:
                            extra = [(q * P, Hst[:, parity, j, part, P * (1 - q):P * (2 - q)], flip[:, :])
                                     for q in range(2) for part in range(PARTS)]
                        if l == 1 and kt * P == q0:
                            extra = [(0, identb[:, :], mask_kq[:, :])]
                        ins = mm(dst, stack["Tk"][0:STACK + PARTS, parity, j, kt * P:(kt + 1) * P],
                                 stack["Tq"][0:STACK + PARTS, parity, j, q0:q0 + w], stop=not extra)
                        for n, (c0, lhsT, rhs) in enumerate(extra):
                            ins = mm(bank(4 + m % 3, c0, c0 + P), lhsT, rhs, start=False, stop=n == len(extra) - 1)
                        ins.then_inc(A["st_ps"], 1)

                def av_step(G, i, parity):
                    h, kt, off = steps[i]
                    pe.wait_ge(A["e_done"], G * n_st + HG * (i + 1))
                    if i == 0:
                        pe.wait_ge(A["v_staged"], G + 1)
                        if not (isinstance(G, int) and G == 0):
                            pe.wait_ge(A["o_ev"], G * 2)
                    if i == half0:
                        pe.wait_ge(A["o_ev"], G * 2 + 1)
                    last = i + 1 == len(steps) or steps[i + 1][0] != h
                    for j in range(HG):
                        ins = mm(PS[32 * j:32 * (j + 1), 7 * 512 + off:8 * 512], Vst[:, parity, kt, j, :],
                                 Pr[:, (HG * i + j) % 8, 0:512 - off], start=kt == 0, stop=last)
                    ins.then_inc(A["av_done"], 1)

                def body(G, parity, carry, s_phase):
                    plan = ring_plan(l, carry, s_phase)
                    U = 0
                    base = ring_base(l, G)
                    base_parity = (base if isinstance(G, int) else ring_base(l, 2 - parity)) % 2
                    begun = biased = False
                    for i in range(len(steps)):
                        if i == 0:
                            wait_loads("t", G, parity)
                            pe.wait_ge(A["m_ld"], G * 48 + 48)
                        todo = [w for w in plan[i] if w[0] != "Q"]
                        for what in todo:
                            if what[0] == "S" and what[1] == 1 and not begun:
                                wait_loads("s", G + 2, parity)
                                begun = True
                            if l == 0 and what[0] == "S" and what[1] == 0 and what[2][1] < 2 and not biased:
                                wait_bias(G + 1, 1 - parity)
                                biased = True
                        for j in range(HG):
                            st_step(G, i, parity, carry, (j,))
                            if j == 1:
                                if i == 0 and carry:
                                    av_step(G - 1, len(steps) - 1, 1 - parity)
                                if i > 0:
                                    av_step(G, i - 1, parity)
                            now = len(todo) if j == HG - 1 else 0 if j == 1 and len(todo) < 3 else 1
                            for what in todo[:now]:
                                if what[0] == "R":
                                    what = ("R", (G - 1 if what[1] else G, what[1]))
                                unit(base + U, (base_parity + U) % 2, what, 1 - parity, s_phase == 1)
                                U += 1
                            todo = todo[now:]

                def wait_loads(which, G, parity):
                    pe.wait_ge(A[f"{which}_ld{parity}"], (G - parity) * 64 + 128)

                def wait_bias(G, parity):
                    pe.wait_ge(A[f"h_ld{parity}"], (G - parity) * 32 + 64)

                wait_loads("s", 0, 0)
                if l == 0:
                    wait_bias(0, 0)
                wait_loads("s", 1, 1)
                for U, what in enumerate(s_sequence(l, True, True)):
                    unit(U, U % 2, what, 0)
                groups(pe, body)
                av_step(GROUPS - 1, len(steps) - 1, 1)
                last = ring_base(l, GROUPS - 1) + 2
                unit(last, last % 2, ("R", (GROUPS - 1, 1)), 0)
                pe.wait_ge(A["ring_free"], last + 1)
                for c in range(NC):
                    for g in range(NG):
                        ins = mm(bank(c), wo[:, l, g, :], OT[:, (c // 2) * NG + g, 512 * (c % 2):512 * (c % 2 + 1)],
                                 start=g == 0, stop=g == NG - 1)
                    ins.then_inc(A["pj_ps"], 1)

            pe.wait_ge(const_done, 1)
            transposes(lambda t: xtok[:, t, :], 4, lambda c: pe.wait_ge(x_in[c], 16))
            transposes(lambda t: ztok[:, t, :], 0, lambda c: pe.wait_ge(z_ready, c + 1))
            pe.wait_ge(w_in, 16 * (W_LOADS + 1))
            project_qk(0, 4, 0, lambda c: pe.wait_ge(tr_ev, 4 + c + 1))
            project_v(0, 4, lambda c: pe.wait_ge(q_ev, c + 1))
            pe.wait_ge(k_ev, 1)
            for t in range(NT):
                ins = mm(bank(0, 8 * t, 8 * t + 8), xnT[:, t * P:(t + 1) * P], router[:, 0, :])
            ins.then_inc(lg_ps, 1)
            pe.wait_ge(k_ev, 4)

            def up(n_term, U, u, slot, ready):
                if u == 0:
                    pe.wait_ge(f_w[slot], ready)
                if not (isinstance(n_term, int) and U < 2):
                    pe.wait_ge(g_made, n_term + U - 1)
                x = xnT[:, 512 * (u // 2):512 * (u // 2 + 1)]
                w0 = 128 * (u % 2)
                mm(bank(2 * (u % 2)), fw0[:, slot, w0:w0 + 128], x)
                mm(bank(2 * (u % 2) + 1), fw0[:, slot, 256 + w0:256 + w0 + 128], x).then_inc(h_ps, 1)

            def down(n_term, U, u, slot, first, last):
                pe.wait_ge(g_made, n_term + U + 1)
                w0 = 512 + 128 * (u % 2)
                mm(bank(4 + u // 2), fw0[:, slot, w0:w0 + 128], fg[:, u % 4, :], start=first and u % 2 == 0,
                   stop=last and u % 2 == 1).then_inc(y_done, 1)

            def expert(n_term, base, slot, ready, first=False, last=False, carry=False, flush=True):
                for u in range(8):
                    if u >= 2:
                        down(n_term, base + u - 2, u - 2, slot, first, last)
                    elif carry:
                        down(n_term, base + u - 2, 6 + u, 1 - slot, False, False)
                    up(n_term, base + u, u, slot, ready)
                if flush:
                    down(n_term, base + 6, 6, slot, first, last)
                    down(n_term, base + 7, 7, slot, first, last)

            comb_T(0, 1)
            pe.wait_ge(cb_ev, 1)
            pe.wait_ge(v_ev, 4)
            expert(0, 0, 0, 16, first=True)
            with pe.Fori(0, 4) as it:
                expert(it * 16, 8, 1, it * 16 + 16, flush=False)
                expert(it * 16, 16, 0, it * 16 + 32, carry=True)
            expert(0, 72, 1, 16 * 5, last=True)
            pe.wait_ge(y_ev, NC)
            attention(0)

            transposes(lambda t: xT[:, t * P:(t + 1) * P], 4, lambda c: pe.wait_ge(att[0]["pj_ev"], c + 1))
            transposes(lambda t: ztok[:, t, :], 0, lambda c: pe.wait_ge(z_ready, 4 + c + 1))
            project_qk(1, 0, 4, lambda c: pe.wait_ge(tr_ev, 12 + c + 1))
            project_v(1, 0, lambda c: pe.wait_ge(q_ev, 4 + c + 1))
            pe.wait_ge(k_ev, 8)
            transposes(lambda t: zz[:, t, :], 4, lambda c: pe.wait_ge(z_ready, 8 + c + 1))
            pe.wait_ge(tr_ev, 20)
            gate_products(1, n1T)
            comb_T(1, 5)
            pe.wait_ge(v_ev, 8)
            pe.wait_ge(cb_ev, 2)
            attention(1)

            pe.wait_ge(fw_in, 16 * 6)
            pe.wait_ge(att[1]["pj_ev"], NC)
            with pe.Fori(0, BATCH) as b:
                for e in range(EXP):
                    pe.wait_ge(x_made, b * EXP + e + 1)
                    for n, w in enumerate((fwq, fwk, fwv)):
                        for c in range(2):
                            ins = mm(bank(2 * n + c), w[:, e, :], Xe[:, e % 2, 512 * c:512 * (c + 1)], start=e == 0, stop=e == EXP - 1)
                    ins.then_inc(x_used, 1)
                pe.wait_ge(x_ev, b * 4 + 4)
                for c in range(2):
                    for k in range(4):
                        ins = nc.tensor.transpose(bank(6 + c, P * k, P * (k + 1)), vT[:, (4 * c + k) * P:(4 * c + k + 1) * P], ident[:, :])
                    ins.then_inc(vt_ps, 1)
                pe.wait_ge(vt_ev, b * 4 + 4)

                def scores(qt):
                    w = (qt + 1) * P
                    if qt >= 2:
                        pe.wait_ge(s1_p, b * KT + qt - 1)
                    lo = 1024 * (qt % 2)
                    for k0 in range(0, w, 512):
                        k1 = min(w, k0 + 512)
                        ins = mm(PS[:, lo + k0:lo + k1], qT[:, qt * P:(qt + 1) * P], kT[:, k0:k1], stop=k1 != w)
                    ins = mm(PS[:, lo + w - P:lo + w], identb[:, :], mask_qk[:, :], start=False)
                    ins.then_inc(s1_ps, 1)

                def p_transposes(qt):
                    pe.wait_ge(s1_p, b * KT + qt + 1)
                    if qt:
                        pe.wait_ge(pt_ev, b * KT + qt)
                    for k in range(qt + 1):
                        ins = nc.tensor.transpose(PS[:, 2048 + k * P:2048 + (k + 1) * P], P1[:, qt % 2, k * P:(k + 1) * P], ident[:, :])
                    ins.then_inc(pt_ps, 1)

                def values(half):
                    pe.wait_ge(pt_ev, b * KT + 4 * half + 4)
                    for kt in range(4 * half + 4):
                        off = max(0, kt - 4 * half) * P
                        ins = mm(bank(6 + half, off, 512), vtok[:, kt, :], PT[:, kt, off:512], start=kt == 0, stop=kt == 4 * half + 3)
                    ins.then_inc(o1_ps, 1)

                for qt in range(KT):
                    scores(qt)
                    if qt >= 1:
                        p_transposes(qt - 1)
                    if qt == 4:
                        values(0)
                p_transposes(KT - 1)
                values(1)
                for e in range(EXP):
                    pe.wait_ge(ox_made, b * EXP + e + 1)
                    for c in range(2):
                        ins = mm(bank(c), fwo[:, e, :], Xe[:, e % 2, 512 * c:512 * (c + 1)], start=e == 0, stop=e == EXP - 1)
                    ins.then_inc(ox_used, 1)
            pe.wait_ge(hs_ev, 4)
            transposes(lambda t: hsT[:, t * P:(t + 1) * P], 4, lambda c: None)
            transposes(lambda t: ztok[:, t, :], 0, lambda c: pe.wait_ge(z_ready, 12 + c + 1))
            pe.wait_ge(tr_ev, 28)
            gate_products(2, xnT)
            comb_T(2, 5)
            pe.wait_ge(cb_ev, 3)
            with pe.Fori(0, BATCH) as b:
                for u in range(2 * EXP + 2):
                    if u < 2 * EXP:
                        e, c = u // 2, u % 2
                        if u >= 4:
                            pe.wait_ge(i_gelu, b * 16 + u - 3)
                        mm(bank(u % 4), fw1[:, e, :], xnT[:, bass.ds(b * SEQ + 512 * c, 512)]).then_inc(i_ps, 1)
                    if u >= 2:
                        e, c = (u - 2) // 2, u % 2
                        pe.wait_ge(i_g, b * 16 + u - 1)
                        mm(bank(4 + c), fw2[:, e, :], gg[:, (u - 2) % 4, :], start=e == 0, stop=e == EXP - 1).then_inc(i_used, 1)
            for c in range(NC):
                pe.wait_ge(fin_x, c + 1)
                for k in range(4):
                    t = 4 * c + k
                    ins = nc.tensor.transpose(bank(c, P * k, P * (k + 1)), hsT[:, t * P:(t + 1) * P], ident[:, :])
                ins.then_inc(fin_ps, 1)


_NAMES = ["L0_attn_x", "L0_attn_Wq", "L0_attn_bq", "L0_attn_Wk", "L0_attn_bk", "L0_attn_Wv", "L0_attn_bv", "L0_attn_Wp",
          "L0_attn_bp", "L0_attn_temperature", "L0_ffn_expert_bias", "L1_ffn_ln1_w", "L1_ffn_ln1_b", "L1_ffn_ln2_w",
          "L1_ffn_ln2_b", "L1_ffn_smha_sim", "L1_ffn_smha_gates", "L1_ffn_q_proj", "L1_ffn_k_proj", "L1_ffn_v_proj",
          "L1_ffn_o_proj", "L1_ffn_moe_sim", "L1_ffn_moe_gates", "L1_ffn_w1", "L1_ffn_w2"]


def kernel(**inputs):
    import numpy as np
    import concourse.bacc as bacc
    from concourse.bass_utils import run_bass_kernel_spmd

    x = {k: np.asarray(v) for k, v in inputs.items()}
    laid = {n: x[n] for n in _NAMES}
    laid["L1_WQT"], laid["L1_WKT"] = x["L1_attn_W_Q"].T, x["L1_attn_W_K"].T
    laid["L1_WVT"], laid["L1_WOT"] = x["L1_attn_W_V"].T, x["L1_attn_W_O"].T
    laid["router_T"] = x["L0_ffn_router_w"].T
    laid["bias_rev_T"] = x["L0_attn_bias_table"][::-1].T

    def experts(w1, w3, w2):
        down = w2.transpose(0, 2, 1).reshape(w2.shape[0], 2, 128, 128).transpose(0, 2, 1, 3).reshape(w2.shape[0], 128, 256)
        return np.concatenate([w1.transpose(0, 2, 1), w3.transpose(0, 2, 1), down], axis=2)

    shared = experts(x["L0_ffn_sw1"], x["L0_ffn_sw3"], x["L0_ffn_sw2"])
    routed = experts(x["L0_ffn_w1"], x["L0_ffn_w3"], x["L0_ffn_w2"])
    laid["ffn_w"] = np.concatenate([shared[0:1], routed, shared[1:2]], axis=0)

    nc = bacc.Bacc("TRN2", target_bir_lowering=False, num_devices=1)
    arrays, args = {}, {}
    for name, value in laid.items():
        value = np.ascontiguousarray(value)
        arrays["in_" + name] = value
        args[name] = nc.dram_tensor("in_" + name, value.shape, mybir.dt.from_np(value.dtype), kind="ExternalInput").ap()
    out = nc.dram_tensor("out_x", (BATCH, SEQ, C), F32, kind="ExternalOutput").ap()
    block_net(nc, args, out)
    r = run_bass_kernel_spmd(nc, [arrays], core_ids=[0])
    return r.results[0]["out_x"]
```

```python
import math
from contextlib import ExitStack

import concourse.bass as bass
from concourse import mybir

F32 = mybir.dt.float32
BF16 = mybir.dt.bfloat16
F32R = mybir.dt.float32r
ALU = mybir.AluOpType
ACT = mybir.ActivationFunctionType
AX = mybir.AxisListType

P = 128
C = 128
BATCH, SEQ = 2, 1024
TOK = BATCH * SEQ
NT = TOK // P
NC = TOK // 512
HEADS, HD = 16, 8
HG = 4
NG = HEADS // HG
GROUPS = BATCH * NG
KT = SEQ // P
PARTS = 3
STACK = PARTS * PARTS * HD
EXP = 8
FFN_SEQ = EXP + 2
REL = 249
DREV = 384
NEG = -1.0e30
LN_EPS = 1e-5


class Chain:

    def __init__(self, eng, sem):
        self.eng, self.sem, self.n, self.term = eng, sem, 0, 0

    def link(self, ins):
        self.n += 1
        ins.then_inc(self.sem, 1)
        self.eng.wait_ge(self.sem, self.term + self.n)

    def enter(self, it, per):
        self.start, self.per, self.term = self.n, per, it * per

    def leave(self, iters):
        assert self.n - self.start == self.per, (self.n - self.start, self.per)
        self.n, self.term = self.start + self.per * iters, 0


def t_steps(layer):
    if layer == 0:
        return [(h, k, 0) for h in range(2) for k in range(KT)]
    return [(h, k, max(0, k - 4 * h) * P) for h in range(2) for k in range(4 * h + 4)]


def s_units(layer):
    order = list(range(2, KT)) + [0, 1]
    return [(j, q, SEQ if layer == 0 else (q + 1) * P) for q in order for j in range(HG)]


AHEAD = (8, 12)


def s_sequence(layer, first):
    units = s_units(layer)
    ahead = AHEAD[layer]
    return ([("S", 0, u) for u in units[(0 if first else ahead):]] + [("S", 1, u) for u in units[:2]] +
            [("M",)] + [("S", 1, u) for u in units[2:ahead]])


def ring_plan(layer, carry, s_phase):
    steps = t_steps(layer)
    n = len(steps)
    plan = [[] for _ in range(n)]
    first_of_half1 = next(i for i, s in enumerate(steps) if s[0] == 1)
    if carry:
        plan[3].append(("Q", 1))
        plan[5].append(("R", 1))
    plan[first_of_half1 + 3].append(("Q", 0))
    plan[first_of_half1 + 5].append(("R", 0))
    if not s_phase and layer == 1:
        plan[0].append(("G", 0))
        plan[5].append(("G", 1))
        plan[7].append(("C",))
    if s_phase:
        seq = s_sequence(layer, False)
        total, done, at = sum(w[2][2] for w in seq if w[0] == "S"), 0, 0
        t_total = sum(512 - s[2] for s in steps)
        for what in seq:
            while at < n - 1 and done * t_total >= total * sum(512 - s[2] for s in steps[:at + 1]):
                at += 1
            if what[0] == "M":
                plan[at].append(what)
                continue
            done += what[2][2]
            if what[1] == 0 or s_phase == 2:
                plan[at].append(what)
    return plan


def block_net(nc, a, out):
    ctx = ExitStack()
    with ctx:
        def sb(name, shape, dt=F32):
            return ctx.enter_context(nc.sbuf_tensor(name, shape, dt))

        def sem(name):
            return ctx.enter_context(nc.semaphore(name))

        def dram(name, shape, dt):
            return nc.dram_tensor(name, shape, dt).ap()

        q_dram = [dram(f"q_dram{l}", (GROUPS, HG, PARTS + 2, HD, SEQ), BF16) for l in range(2)]
        k_dram = [dram(f"k_dram{l}", (GROUPS, HG, PARTS, HD, SEQ), BF16) for l in range(2)]
        drev_dram = dram("drev_dram", (GROUPS, HG, PARTS, DREV), BF16)
        comb_dram = [dram(f"comb_dram{n}", (P, P), F32) for n in range(3)]

        PS = ctx.enter_context(nc.psum_tensor("PS", [P, 8 * 512], F32))

        def bank(n, lo=0, hi=512):
            return PS[:, n * 512 + lo:n * 512 + hi]

        xT = sb("xT", [P, TOK])
        xnT = sb("xnT", [P, TOK])
        n1T = sb("n1T", [P, TOK])
        ident = sb("ident", [P, P])
        ones = sb("ones", [P, P])
        sel = sb("sel", [P, P])
        identb = sb("identb", [P, P], BF16)
        flip = sb("flip", [P, P], BF16)
        mask_kq = sb("mask_kq", [P, P], BF16)
        mask_qk = sb("mask_qk", [P, P], BF16)
        sum_col = sb("sum_col", [P, 32])
        prefer = sb("prefer", [P, EXP])
        wq = sb("wq", [P, 2, C])
        wk = sb("wk", [P, 2, C])
        wv = sb("wv", [P, 2, C])
        wo = sb("wo", [P, 2, NG, C])
        router = sb("router", [P, 3, 32])
        simsq = sb("simsq", [P, 2, EXP])
        cols = sb("cols", [P, 10])
        bvb = sb("bvb", [P, C])
        erow = sb("erow", [P, 3, EXP])
        small = sb("small", [P, 10, NT])
        gl = sb("gl", [P, 3, 160])
        combT = sb("combT", [P, P])
        mx = sb("mx", [P, 2, HG * KT])
        sums = sb("sums", [P, 2, 16])
        rsums = sb("rsums", [P, 2, 16])
        mres = sb("mres", [HG * KT, P])
        mrow = sb("mrow", [HG * KT, PARTS, P], BF16)
        with ExitStack() as over:
            def part(name, kib, dt=F32R):
                return over.enter_context(nc.sbuf_tensor(name, [P, kib * 256], dt))

            part("below_x_hi", 8, F32)
            x_hi = part("x_hi", 8)
            part("below_x_lo", 8, F32)
            x_lo = part("x_lo", 8)
            part("below_e", 48, F32)
            e_hi_lo = part("e_hi_lo", 16)
            m_hi = part("m_hi", 8)
            w12_hi = part("w12_hi", 8)
            part("below_g", 4, F32)
            g_hi_lo = part("g_hi_lo", 16)
            w_hi_lo = part("w_hi_lo", 12)
            fw_lo = part("fw_lo", 24)
        arena = sb("arena", [P, 144 * 256])
        fw = sb("fw", [P, 6 * 1024])

        def at(kib, size):
            return arena[:, kib * 256:(kib + size) * 256]

        def bf(kib, size):
            return at(kib, size).bitcast(BF16)

        stack = {n: bf(k, 16).rearrange("p (s j t) -> p s j t", s=2, j=HG)
                 for n, k in (("Sq", 0), ("Sk", 16), ("Tq", 32), ("Tk", 48))}
        V = at(64, 8).rearrange("p (g k c) -> p g k c", g=GROUPS, k=KT)
        sT1 = at(64, 8)
        Vst = at(72, 8).rearrange("p (s k j c) -> p s k j c", s=2, k=KT, j=HG)
        Pr = at(80, 16).rearrange("p (s q) -> p s q", s=8)
        Osb = at(96, 4).rearrange("p (s q) -> p s q", s=2)
        OT = at(100, 32).rearrange("p (g q) -> p g q", g=GROUPS)
        Hst = bf(132, 12).rearrange("p (s j a c) -> p s j a c", s=2, j=HG, a=PARTS)
        xtok = at(32, 8).rearrange("p (t c) -> p t c", t=NT)
        ztok = at(40, 8).rearrange("p (t c) -> p t c", t=NT)
        zz = at(132, 8).rearrange("p (t c) -> p t c", t=NT)
        lrow = at(140, 2)
        q32, k32 = at(80, 8), at(88, 8)
        qsp = bf(100, 12).rearrange("p (a t) -> p a t", a=PARTS)
        ksp = bf(112, 12).rearrange("p (a t) -> p a t", a=PARTS)
        gate_tmp = at(129, 3)
        gate1_tmp = at(29, 3)

        def gate_bufs(n):
            tmp = gate1_tmp if n == 1 else gate_tmp
            return [tmp[:, k * 128:(k + 1) * 128].rearrange("p (t e) -> p t e", e=EXP) for k in range(4)] + [
                tmp[:, 512:640].rearrange("p (e t) -> p e t", e=EXP)]

        stats = gate_tmp[:, 640:736].rearrange("p (t n) -> p t n", t=NT)
        tblr = at(124, 5)[0:HEADS, 0:REL]
        dfull = at(124, 5)[0:HEADS, 256:256 + DREV]
        dpart = at(124, 5)[0:HEADS, 640:1216].bitcast(BF16).rearrange("h (a n) -> h a n", a=PARTS)
        cwb = at(100, 16).rearrange("p (s t) -> p s t", s=2)
        fw0 = fw[:, 0:1536].rearrange("p (s n) -> p s n", s=2)
        fa = fw[:, 2048:3072].rearrange("p (s n) -> p s n", s=2)
        fg = fw[:, 3072:5120].rearrange("p (s n) -> p s n", s=4)
        x_r = [x_hi, x_lo]
        g_r = [g_hi_lo[:, 2048 * h:2048 * (h + 1)].rearrange("p (s n) -> p s n", s=4) for h in range(2)]
        w_r = w_hi_lo[:, :].rearrange("p (s h n) -> p s h n", s=2, h=2)
        fwo = fw[:, 3 * 1024:4 * 1024].rearrange("p (e c) -> p e c", e=EXP)
        w_e_hi = [w_hi_lo[:, n * 1024:(n + 1) * 1024].rearrange("p (e c) -> p e c", e=EXP) for n in range(3)]
        w_e_hi += [None] + [w12_hi[:, n * 1024:(n + 1) * 1024].rearrange("p (e c) -> p e c", e=EXP) for n in range(2)]
        w_e_lo = [fw_lo[:, n * 1024:(n + 1) * 1024].rearrange("p (e c) -> p e c", e=EXP) for n in range(6)]
        rwb = at(0, 64).rearrange("p (e t) -> p e t", e=EXP)
        Xe = [at(96, 4), at(76, 4)]
        Xe_r = [e_hi_lo[:, h * TOK:(h + 1) * TOK].rearrange("p (s t) -> p s t", s=2) for h in range(2)]
        P1 = [at(128, 4), at(76, 4)]
        vtok = at(72, 4).rearrange("p (k c) -> p k c", k=KT)
        qT, kT, vT = at(100, 4), at(104, 4), at(108, 4)
        attnT = at(112, 8)
        hsT = at(120, 8)
        PT = at(80, 16).rearrange("p (k q) -> p k q", k=KT)
        n2_r = [e_hi_lo[:, h * TOK:(h + 1) * TOK] for h in range(2)]
        ga = at(112, 8).rearrange("p (s t) -> p s t", s=4)
        gg = at(72, 8).rearrange("p (s t) -> p s t", s=4)
        gg_r = [m_hi[:, :].rearrange("p (s t) -> p s t", s=4), w_hi_lo[:, 0:TOK].rearrange("p (s t) -> p s t", s=4)]
        otok = at(72, 8).rearrange("p (t c) -> p t c", t=NT)

        bq, bk, bp = cols[:, 0:1], cols[:, 1:2], cols[:, 2:3]
        ln_w = [cols[:, 3:4], cols[:, 5:6]]
        ln_b = [cols[:, 4:5], cols[:, 6:7]]
        temp, qscale = cols[:, 7:8], cols[:, 8:9]

        x_in = [sem(f"x_in{c}") for c in range(NC)]
        w_in, router_in, late_in, fw_in, tbl_in = (sem(n) for n in ("w_in", "router_in", "late_in", "fw_in", "tbl_in"))
        zero_done, const_done, ones_set = sem("zero_done"), sem("const_done"), sem("ones_set")
        dve_own, pool_own = sem("dve_own"), sem("pool_own")
        var_ready, rstd_ready = sem("var_ready"), sem("rstd_ready")
        z_ready = sem("z_ready")
        ss_ready, norm_ready = sem("ss_ready"), sem("norm_ready")
        tr_ps, tr_ev = sem("tr_ps"), sem("tr_ev")
        q_ps, k_ps, v_ps = sem("q_ps"), sem("k_ps"), sem("v_ps")
        q_ev, k_ev, v_ev = sem("q_ev"), sem("k_ev"), sem("v_ev")
        hi_done, rest_done, mid_done, split_done = sem("hi_done"), sem("rest_done"), sem("mid_done"), sem("split_done")
        qk_stored = [[sem(f"qk_stored{l}{b}") for b in range(BATCH)] for l in range(2)]
        drev_ready, drev_stored = sem("drev_ready"), sem("drev_stored")
        lg_ps, gx_ready, ge_ready, comb_ready, cb_ps, cb_ev = (sem(n) for n in (
            "lg_ps", "gx_ready", "ge_ready", "comb_ready", "cb_ps", "cb_ev"))
        comb_stored = sem("comb_stored")
        rows_ps, rows_ev = sem("rows_ps"), sem("rows_ev")
        sq_ready, gate_exp, gneg = sem("sq_ready"), sem("gate_exp"), sem("gneg")
        f_w = [sem(f"f_w{s}") for s in range(2)]
        f_c = [sem(f"f_c{s}") for s in range(2)]
        h_ps, a_made, g_made, gw_made, y_done, y_ev = (sem(n) for n in ("h_ps", "a_made", "g_made", "gw_made", "y_done", "y_ev"))
        xhi_made, xlo_made, whi_made, wlo_made, ghi_made, glo_made = (sem(n) for n in (
            "xhi_made", "xlo_made", "whi_made", "wlo_made", "ghi_made", "glo_made"))
        att = [{n: sem(f"{n}{l}") for n in (
            "s_ld0", "s_ld1", "t_ld0", "t_ld1", "h_ld0", "h_ld1", "m_ld",
            "ring_full", "ring_free", "half_out", "st_ps", "e_done", "av_done", "o_ev", "m_ready", "v_staged",
            "sum_in0", "sum_in1", "sum_inv", "rrow_in", "pj_ps", "pj_ev")}
            for l in range(2)]
        rw_in = [sem(f"rw_in{e}") for e in range(EXP)]
        x_made, x_used, x_ev, vt_ps, vt_ev = (sem(n) for n in ("x_made", "x_used", "x_ev", "vt_ps", "vt_ev"))
        s1_ps, s1_max, s1_exp, s1_p, pt_ps, pt_ev, o1_ps, o1_ev = (sem(n) for n in (
            "s1_ps", "s1_max", "s1_exp", "s1_p", "pt_ps", "pt_ev", "o1_ps", "o1_ev"))
        ew_split, ehi_made, elo_made, n2hi_made, n2lo_made, mw_hi, mw_split, mhi_made, mlo_made = (sem(n) for n in (
            "ew_split", "ehi_made", "elo_made", "n2hi_made", "n2lo_made", "mw_hi", "mw_split", "mhi_made", "mlo_made"))
        ox_made, ox_used, hs_ev = sem("ox_made"), sem("ox_used"), sem("hs_ev")
        i_ps, i_gelu, i_g, i_used, moe_ev = (sem(n) for n in ("i_ps", "i_gelu", "i_g", "i_used", "moe_ev"))
        fin_silu, fin_x, fin_ps, fin_ev, stored = (sem(n) for n in ("fin_silu", "fin_x", "fin_ps", "fin_ev", "stored"))

        FIRST_LOADS, LATE_LOADS = 8, 20
        NS = [len(t_steps(l)) for l in range(2)]

        UNITS = len(s_units(0)) + 1

        def ring_base(l, G):
            first = UNITS + AHEAD[l]
            if isinstance(G, int) and G == 0:
                return first
            last = AHEAD[l] if isinstance(G, int) and G == GROUPS - 1 else 0
            return (G - 1) * (UNITS + 2) + (first + UNITS + 1 - last)

        def last_unit(l):
            return ring_base(l, GROUPS - 1) + sum(1 for step in ring_plan(l, True, 0) for w in step if w[0] not in "QG")

        def ring_after_s(l, G):
            if isinstance(G, int) and G == 0:
                return UNITS + 2
            carry = not (isinstance(G, int) and G == 1)
            n = 0
            for what in (w for step in ring_plan(l, carry, 2) for w in step if w[0] not in "QG"):
                n += 1
                if what[0] == "M":
                    break
            return ring_base(l, G - 1) + n

        def groups(eng, body, chain=None, per=0):
            body(0, 0, False, 2)
            with eng.Fori(0, 2) as it:
                if chain:
                    chain.enter(it, per)
                body(it * 2 + 1, 1, True, 2)
                body(it * 2 + 2, 0, True, 2)
            if chain:
                chain.leave(2)
            body(GROUPS - 3, 1, True, 2)
            body(GROUPS - 2, 0, True, 1)
            body(GROUPS - 1, 1, True, 0)

        def ffn_experts(eng, expert, chain=None, per=0):
            expert(0, 0, 0, 0, 0)
            expert(1, 0, 8, 1, 1)
            with eng.Fori(0, 3) as it:
                if chain:
                    chain.enter(it, per)
                expert(it * 2 + 2, it * 16, 16, 0, 2)
                expert(it * 2 + 3, it * 16, 24, 1, 2)
            if chain:
                chain.leave(3)
            expert(8, 0, 64, 0, 2)
            expert(9, 0, 72, 1, 3)

        block = ctx.enter_context(nc.Block())

        @block.sync
        def _(sp):
            x_v = a["L0_attn_x"].rearrange("b (t p) c -> p (b t) c", p=P)
            for c in range(NC):
                sp.dma_start(xtok[:, 4 * c:4 * c + 4, :], x_v[:, 4 * c:4 * c + 4, :]).then_inc(x_in[c], 16)
            first = [(dst[:, 0, :], a[name]) for dst, name in ((wq, "L0_attn_Wq"), (wk, "L0_attn_Wk"), (wv, "L0_attn_Wv"))]
            first += [(cols[:, k:k + 1], a[name].rearrange("(p a) -> p a", a=1)) for k, name in enumerate(("L0_attn_bq", "L0_attn_bk"))]
            first += [(temp, a["L0_attn_temperature"].partition_broadcast(P)), (bvb[:, :], a["L0_attn_bv"].partition_broadcast(P)),
                      (erow[:, 0, :], a["L0_ffn_expert_bias"].partition_broadcast(P))]
            assert len(first) == FIRST_LOADS
            for dst, src in first:
                sp.dma_start(dst, src).then_inc(w_in, 16)
            sp.wait_ge(zero_done, 2)
            sp.dma_start(router[:, 0, 0:EXP], a["router_T"]).then_inc(router_in, 16)
            sp.dma_start(tblr[:, :], a["bias_rev_T"]).then_inc(tbl_in, 16)
            for s in range(2):
                sp.dma_start(fw0[:, s, 0:768], a["ffn_w"][s]).then_inc(f_w[s], 16)
            late = [(router[:, k, 0:EXP], a[name]) for k, name in ((1, "L1_ffn_smha_sim"), (2, "L1_ffn_moe_sim"))]
            late += [(erow[:, k, :], a[name].partition_broadcast(P)) for k, name in ((1, "L1_ffn_smha_gates"), (2, "L1_ffn_moe_gates"))]
            late += [(cols[:, k:k + 1], a[name].rearrange("(p a) -> p a", a=1)) for k, name in enumerate((
                "L0_attn_bp", "L1_ffn_ln1_w", "L1_ffn_ln1_b", "L1_ffn_ln2_w", "L1_ffn_ln2_b"), 2)]
            late += [(dst[:, 1, :], a[name]) for dst, name in ((wq, "L1_WQT"), (wk, "L1_WKT"), (wv, "L1_WVT"))]
            for l, name in enumerate(("L0_attn_Wp", "L1_WOT")):
                w_v = a[name].rearrange("(g j d) c -> j d g c", g=NG, j=HG)
                late += [(wo[32 * j:32 * j + HD, l, :, :], w_v[j]) for j in range(HG)]
            assert len(late) == LATE_LOADS
            for dst, src in late:
                sp.dma_start(dst, src).then_inc(late_in, 16)

            def store_qk(l, b):
                for which, sp32, dr, order in ((0, qsp, q_dram[l], (0, 1, 2, 0, 1)), (1, ksp, k_dram[l], (0, 1, 2))):
                    sp.wait_ge(split_done, 4 * l + 2 * b + which + 1)
                    for n_, part in enumerate(order):
                        dst = dr[b * NG:(b + 1) * NG, :, n_, :, :].rearrange("g j d t -> (g j) d t")
                        sp.dma_start(dst, sp32[:, part, b * SEQ:(b + 1) * SEQ]).then_inc(qk_stored[l][b], 16)

            def load_stack(l, which, G, parity):
                ld = att[l][f"{which.lower()}_ld{parity}"]
                for j in range(HG):
                    for name, dr, np_, step in (("q", q_dram[l], PARTS + 2, 1), ("k", k_dram[l], PARTS, 0)):
                        src = bass.AP(tensor=dr.tensor, offset=G * (HG * np_ * HD * SEQ) + j * np_ * HD * SEQ,
                                      ap=[[step * HD * SEQ, PARTS], [SEQ, PARTS * HD], [1, SEQ]])
                        sp.dma_start(stack[which + name][0:STACK, parity, j, :], src).then_inc(ld, 16)

            def load_bias(G, parity):
                for j in range(HG):
                    src = bass.AP(tensor=drev_dram.tensor, offset=G * (HG * PARTS * DREV) + j * PARTS * DREV,
                                  ap=[[1, P], [DREV, PARTS], [1, 256]])
                    sp.dma_start(Hst[:, parity, j, :, :], src).then_inc(att[0][f"h_ld{parity}"], 16)

            def load_max(l, G, parity):
                A = att[l]
                sp.wait_ge(A["m_ready"], G + 1)
                for part in range(PARTS):
                    dst = stack["Tq"][STACK + part:STACK + part + 1, parity, :, :].rearrange("p j (q t) -> p (j q) t", t=P)
                    sp.dma_start(dst, mrow[:, part, :]).then_inc(A["m_ld"], 16)

            def attention_loads(l, between=None):
                sp.wait_ge(ones_set, 1)
                sp.wait_ge(qk_stored[l][0], 16 * 8)
                if l == 0:
                    sp.wait_ge(drev_stored, 16 * PARTS * BATCH)
                load_stack(l, "S", 0, 0)
                if between:
                    between()
                if l == 0:
                    sp.wait_ge(y_done, 8 * FFN_SEQ)
                    load_bias(0, 0)
                load_stack(l, "S", 1, 1)
                if l == 0:
                    load_bias(1, 1)
                load_stack(l, "T", 0, 0)
                if l == 1:
                    sp.wait_ge(z_ready, 12)
                load_stack(l, "T", 1, 1)

            def attention_feed(l, between=None):
                A = att[l]
                NSJ = NS[l] * HG

                def sums_back(G, half):
                    sp.wait_ge(A["sum_inv"], G * 2 + (half + 1))
                    sp.dma_start(Osb[HD:P:32, half, :].rearrange("j (c e) -> j c e", e=16), rsums[:, half, :]).then_inc(A["rrow_in"], 16)

                def feed(G, parity, first, s_next, t_next, between=None):
                    load_max(l, G, parity)
                    if s_next:
                        sp.wait_ge(A["ring_full"], ring_after_s(l, G))
                        load_stack(l, "S", G + 2, parity)
                    if l == 0 and not first and t_next:
                        sp.wait_ge(A["st_ps"], G * NSJ)
                        load_bias(G + 1, 1 - parity)
                    if not first:
                        sums_back(G - 1, 1)
                    if not first and t_next:
                        sp.wait_ge(A["st_ps"], G * NSJ)
                        load_stack(l, "T", G + 1, 1 - parity)
                    sums_back(G, 0)
                    if between:
                        between()

                feed(0, 0, True, True, False)
                with sp.Fori(0, 2) as it:
                    feed(it * 2 + 1, 1, False, True, True)
                    feed(it * 2 + 2, 0, False, True, True)
                feed(5, 1, False, True, True)
                feed(6, 0, False, False, True)
                feed(7, 1, False, False, False, between)
                sums_back(GROUPS - 1, 1)

            for b in range(BATCH):
                store_qk(0, b)
            sp.wait_ge(drev_ready, 1)
            for part in range(PARTS):
                for b in range(BATCH):
                    dst = drev_dram[b * NG:(b + 1) * NG, :, part, :].rearrange("g j n -> (g j) n")
                    sp.dma_start(dst, dpart[:, part, :]).then_inc(drev_stored, 16)
            sp.wait_ge(cb_ev, 1)
            sp.dma_start(comb_dram[0], combT[:, :]).then_inc(comb_stored, 16)
            sp.wait_ge(comb_stored, 16)
            for b in range(BATCH):
                sp.wait_ge(qk_stored[0][b], 16 * 8)
            comb_rows = comb_dram[0].rearrange("(e t) k -> e (t k)", e=EXP)

            def load_gate(e, slot):
                sp.dma_start(cwb[:, slot, :], comb_rows[e].partition_broadcast(P)).then_inc(f_c[slot], 16)

            load_gate(0, 1)

            def next_expert(n, slot, routed, first=False):
                sp.wait_ge(wlo_made, n + 1)
                sp.dma_start(fw0[:, slot, 0:768], a["ffn_w"][n + 2]).then_inc(f_w[slot], 16)
                if routed:
                    if not first:
                        sp.wait_ge(gw_made, n * 8)
                    load_gate(n + 1, slot)

            next_expert(0, 0, True, True)
            next_expert(1, 1, True)
            with sp.Fori(0, 2) as it:
                next_expert(it * 2 + 2, 0, True)
                next_expert(it * 2 + 3, 1, True)
            next_expert(6, 0, True)
            next_expert(7, 1, False)
            attention_loads(0)
            attention_feed(0)
            sp.wait_ge(y_ev, NC)
            for n_, name in enumerate(("q_proj", "k_proj", "v_proj", "o_proj", "w1", "w2")):
                sp.dma_start(fw[:, n_ * 1024:(n_ + 1) * 1024].rearrange("p (e c) -> p e c", e=EXP),
                             a["L1_ffn_" + name].rearrange("e c h -> c e h")).then_inc(fw_in, 16)
            store_qk(1, 0)
            attention_loads(1, lambda: store_qk(1, 1))
            sp.wait_ge(qk_stored[1][1], 16 * 8)
            rows = [comb_dram[n].rearrange("(e t) k -> e (t k)", e=EXP) for n in (1, 2)]

            def load_rw(n, *experts):
                for e in experts:
                    sp.dma_start(rwb[:, e, :], rows[n][e].partition_broadcast(P)).then_inc(rw_in[e], 16)

            def load_first_rw():
                sp.wait_ge(att[1]["ring_free"], ring_base(1, GROUPS - 1) + 2)
                sp.dma_start(comb_dram[1], combT[:, :]).then_inc(comb_stored, 16)
                sp.wait_ge(comb_stored, 32)
                sp.wait_ge(att[1]["ring_full"], ring_after_s(1, GROUPS - 1))
                load_rw(0, 0)

            attention_feed(1, load_first_rw)
            load_rw(0, 1, 2)
            sp.wait_ge(att[1]["st_ps"], (GROUPS - 1) * NS[1] * HG)
            load_rw(0, 3, 4, 6)
            sp.wait_ge(att[1]["st_ps"], GROUPS * NS[1] * HG)
            load_rw(0, 5, 7)
            sp.wait_ge(cb_ev, 2)
            sp.dma_start(comb_dram[2], combT[:, :]).then_inc(comb_stored, 16)
            sp.wait_ge(comb_stored, 48)
            load_rw(1, *range(EXP))
            o_v = out.rearrange("b (t p) c -> p (b t) c", p=P)
            for c in range(NC):
                sp.wait_ge(fin_ev, c + 1)
                sp.dma_start(o_v[:, 4 * c:4 * c + 4, :], otok[:, 4 * c:4 * c + 4, :]).then_inc(stored, 16)
            sp.wait_ge(stored, 16 * NC)

        @block.gpsimd
        def _(pool):
            own = Chain(pool, pool_own)
            g = nc.gpsimd
            g.memset(wo[:, :, :, :], 0.0).then_inc(zero_done, 1)
            g.memset(router[:, :, :], 0.0).then_inc(zero_done, 1)
            for e in range(EXP):
                g.memset(prefer[:, e:e + 1], float(EXP - e))
            own.link(g.memset(sum_col[:, :], 0.0))
            g.memset(sum_col[:, EXP:EXP + 1], 1.0)
            for t_ in (ident, sel, identb, flip, mask_kq, mask_qk):
                g.memset(t_[:, :], 0.0)
            own.link(g.memset(ones[:, :], 1.0))
            for t_, pattern, base, mult, op, fill in (
                    (ident, [[-1, P]], 0, 1, ALU.not_equal, 1.0),
                    (identb, [[-1, P]], 0, 1, ALU.not_equal, 1.0),
                    (flip, [[1, P]], -(P - 1), 1, ALU.not_equal, 1.0),
                    (mask_kq, [[1, P]], 0, -1, ALU.is_ge, NEG),
                    (mask_qk, [[-1, P]], 0, 1, ALU.is_ge, NEG)):
                g.affine_select(out=t_[:, :], in_=t_[:, :], compare_op=op, fill=fill, base=base,
                                pattern=pattern, channel_multiplier=mult)
            sel_v = sel[:, :].rearrange("p (j d) -> p j d", j=HG)
            g.affine_select(out=sel_v, in_=sel_v, compare_op=ALU.not_equal, fill=1.0, base=-HD,
                            pattern=[[-32, HG], [0, 32]], channel_multiplier=1).then_inc(const_done, 1)

            def attention(l):
                A = att[l]
                pool.wait_ge(v_ev, 4 * (l + 1))

                def stage(G, parity):
                    src = V[:, G, :, :].rearrange("p k (j c) -> p k j c", j=HG)
                    g.tensor_copy(Vst[:, parity, :, :, 0:HD], src).then_inc(A["v_staged"], 1)

                def body(G, parity, carry, s_phase):
                    if s_phase:
                        if carry:
                            pool.wait_ge(A["av_done"], G * NS[l])
                        stage(G + 1, 1 - parity)

                stage(0, 0)
                groups(pool, body)

            pool.wait_ge(const_done, 1)
            g.memset(stack["Tk"][64:96, :, :, :], 1.0).then_inc(ones_set, 1)
            pool.wait_ge(ones_set, 1)
            own.link(g.memset(Vst[:, :, :, :, :], 0.0))
            own.link(g.memset(Vst[:, :, :, :, HD:HD + 1], 1.0))
            for c in range(NC):
                part = slice(512 * c, 512 * (c + 1))
                pool.wait_ge(xhi_made, c + 1)
                g.tensor_tensor(x_r[1][:, part], xnT[:, part], x_r[0][:, part], ALU.subtract).then_inc(xlo_made, 1)

            def gate_units(n, n_term, base, slot, kind):
                if kind in (0, 3):
                    return
                pool.wait_ge(f_c[slot], (n_term + base - (8 if slot else 16)) + 16)
                for u in range(8):
                    pool.wait_ge(g_made, n_term + base + u + 1)
                    g_ = fg[:, u % 4, :]
                    g.tensor_tensor(g_, g_, cwb[:, slot, 512 * (u // 2):512 * (u // 2 + 1)], ALU.mult).then_inc(gw_made, 1)

            ffn_experts(pool, gate_units)
            attention(0)
            attention(1)

            pool.wait_ge(fw_in, 16 * 6)
            pool.wait_ge(lg_ps, 2)
            for n in range(3):
                w = fw[:, n * 1024:(n + 1) * 1024].rearrange("p (e c) -> p e c", e=EXP)
                own.link(g.tensor_copy(w_e_hi[n], w))
                g.tensor_tensor(w_e_lo[n], w, w_e_hi[n], ALU.subtract).then_inc(ew_split, 1)
            pool.wait_ge(mw_hi, 1)
            for n in (4, 5):
                w = fw[:, n * 1024:(n + 1) * 1024].rearrange("p (e c) -> p e c", e=EXP)
                g.tensor_tensor(w_e_lo[n], w, w_e_hi[n], ALU.subtract).then_inc(mw_split, 1)
            for c in range(NC):
                part = slice(512 * c, 512 * (c + 1))
                pool.wait_ge(n2hi_made, c + 1)
                g.tensor_tensor(n2_r[1][:, part], xnT[:, part], n2_r[0][:, part], ALU.subtract).then_inc(n2lo_made, 1)

        @block.scalar
        def _(act):
            s = nc.scalar

            def copies(first, dst, count_from):
                for c in range(NC):
                    act.wait_ge(tr_ps, count_from + c + 1)
                    s.activation(dst(c), bank(first + c), ACT.Copy).then_inc(tr_ev, 1)

            def split_hi(l, b):
                part = slice(b * SEQ, (b + 1) * SEQ)
                for n, (src, dst) in enumerate(((q32, qsp), (k32, ksp))):
                    act.wait_ge(q_ev if n == 0 else k_ev, 4 * l + 2 * b + 2)
                    s.activation(dst[:, 0, part], src[:, part], ACT.Copy).then_inc(hi_done, 1)
                for n, (src, dst) in enumerate(((q32, qsp), (k32, ksp))):
                    act.wait_ge(rest_done, 4 * l + 2 * b + n + 1)
                    s.activation(dst[:, 1, part], src[:, part], ACT.Copy).then_inc(mid_done, 1)

            def rows_out(n, b_rows):
                act.wait_ge(rows_ps, n + 1)
                s.activation(lrow, bank(b_rows), ACT.Copy).then_inc(rows_ev, 1)

            def gate_exps(n):
                act.wait_ge(gx_ready, n)
                gated = gate_bufs(n - 1)[3]
                s.activation(gated[:, :, :], gated[:, :, :], ACT.Exp).then_inc(ge_ready, 1)

            def attention(l):
                A = att[l]
                steps = t_steps(l)
                n_exp = len(steps) * HG

                def evac(G, half):
                    if half == 0:
                        act.wait_ge(A["av_done"], G * len(steps) + sum(1 for x in steps if x[0] == 0))
                    else:
                        act.wait_ge(A["av_done"], (G + 1) * len(steps))
                    s.activation(Osb[:, half, :], bank(7), ACT.Copy).then_inc(A["o_ev"], 1)
                    act.wait_ge(A["o_ev"], G * 2 + (half + 1))
                    act.dma_start(sums[:, half, :], Osb[HD:P:32, half, :].rearrange("j (c e) -> j c e", e=16)).then_inc(A[f"sum_in{half}"], 16)

                def body(G, parity, carry, s_phase):
                    first_of_half1 = next(i for i, x in enumerate(steps) if x[0] == 1)
                    for i, (h, kt, off) in enumerate(steps):
                        for j in range(HG):
                            m = HG * i + j
                            act.wait_ge(A["st_ps"], G * n_exp + m + 1)
                            if i >= 2:
                                act.wait_ge(A["av_done"], G * len(steps) + i - 1)
                            elif carry:
                                act.wait_ge(A["av_done"], G * len(steps) + i - 1)
                            w = 512 - off
                            s.activation(Pr[:, m % 8, 0:w], bank(4 + m % 3, 0, w), ACT.Exp).then_inc(A["e_done"], 1)
                        if i == 0 and carry:
                            act.wait_ge(A["ring_free"], ring_base(l, G))
                            evac(G - 1, 1)
                        if l == 1 and not s_phase and i == 4:
                            gate_exps(2)
                        if i == first_of_half1:
                            if carry:
                                act.wait_ge(A["ring_free"], ring_base(l, G))
                            evac(G, 0)

                for U, what in enumerate(s_sequence(l, True)):
                    if what[0] == "S":
                        act.wait_ge(A["ring_full"], U + 1)
                        w, lo = what[2][2], 1024 * (U % 4)
                        s.activation(Pr[:, U % 8, 0:w // 2], PS[:, lo + w // 2:lo + w], ACT.Copy).then_inc(A["half_out"], 1)
                groups(act, body)
                act.wait_ge(A["ring_free"], ring_base(l, GROUPS - 1) + 2)
                evac(GROUPS - 1, 1)

            def root_var(n):
                act.wait_ge(var_ready, n)
                s.activation(small[:, 2, :], small[:, 1, :], ACT.Sqrt).then_inc(rstd_ready, 1)

            def root_squares(n):
                act.wait_ge(ss_ready, n)
                s.activation(gl[:, n, 128:152], gl[:, n, 128:152], ACT.Sqrt).then_inc(norm_ready, 1)

            act.wait_ge(const_done, 1)
            root_var(1)
            copies(4, lambda c: xT[:, 512 * c:512 * (c + 1)], 0)
            copies(0, lambda c: xnT[:, 512 * c:512 * (c + 1)], 4)
            act.wait_ge(w_in, 16 * FIRST_LOADS)
            for b in range(BATCH):
                for c in (2 * b, 2 * b + 1):
                    act.wait_ge(k_ps, c + 1)
                    s.activation(k32[:, 512 * c:512 * (c + 1)], bank(c), ACT.Identity, bias=bk).then_inc(k_ev, 1)
                split_hi(0, b)
            rows_out(0, 0)
            act.wait_ge(f_w[0], 16)
            s.activation(w_r[:, 0, 0, :], fw0[:, 0, 0:768], ACT.Copy).then_inc(whi_made, 1)
            for c in range(NC):
                part = slice(512 * c, 512 * (c + 1))
                s.activation(x_r[0][:, part], xnT[:, part], ACT.Copy).then_inc(xhi_made, 1)
            gate_exps(1)
            act.wait_ge(late_in, 16 * LATE_LOADS)
            s.activation(gl[:, 0, 0:2 * EXP], erow[:, 1:3, :].rearrange("p a e -> p (a e)"), ACT.Exp, scale=-1.0).then_inc(gate_exp, 1)

            def g_hi(base, u, gated):
                U = base + u
                if gated:
                    act.wait_ge(gw_made, U - 7)
                else:
                    act.wait_ge(g_made, U + 1)
                if not (isinstance(U, int) and U < 4):
                    act.wait_ge(y_done, U - 3)
                s.activation(g_r[0][:, u % 4, :], fg[:, u % 4, :], ACT.Copy).then_inc(ghi_made, 1)

            def silu_units(n, n_term, base, slot, kind):
                start = n_term + base
                for u in range(8):
                    act.wait_ge(h_ps, start + u + 1)
                    if not (isinstance(start, int) and base + u < 2):
                        act.wait_ge(g_made, start + u - 1)
                    s.activation(fa[:, u % 2, :], bank(2 * (u % 2)), ACT.Silu).then_inc(a_made, 1)
                    if u >= 2:
                        g_hi(start, u - 2, kind in (1, 2))
                    elif not (isinstance(start, int) and start == 0):
                        g_hi(start - 8, u + 6, kind in (2, 3))
                    if u == 4 and not (isinstance(n, int) and n == FFN_SEQ - 1):
                        act.wait_ge(f_w[1 - slot], (start + 8 - (8 if slot == 0 else 0)) + 16)
                        if not (isinstance(start, int) and start == 0):
                            act.wait_ge(y_done, start)
                        s.activation(w_r[:, 1 - slot, 0, :], fw0[:, 1 - slot, 0:768], ACT.Copy).then_inc(whi_made, 1)

            act.wait_ge(cb_ev, 1)
            for b in range(BATCH):
                act.wait_ge(qk_stored[0][b], 16 * 8)
            ffn_experts(act, silu_units)
            for u in (6, 7):
                g_hi(72, u, False)
            act.wait_ge(y_done, 8 * FFN_SEQ)
            for c in range(NC):
                s.activation(n1T[:, 512 * c:512 * (c + 1)], bank(4 + c), ACT.Silu).then_inc(y_ev, 1)
            attention(0)

            copies(4, lambda c: xtok[:, 4 * c:4 * c + 4, :].rearrange("p t c -> p (t c)"), 8)
            root_var(2)
            copies(0, lambda c: xnT[:, 512 * c:512 * (c + 1)], 12)
            for b in range(BATCH):
                for c in (2 * b, 2 * b + 1):
                    act.wait_ge(k_ps, 4 + c + 1)
                    s.activation(k32[:, 512 * c:512 * (c + 1)], bank(4 + c), ACT.Copy).then_inc(k_ev, 1)
                split_hi(1, b)
            root_var(3)
            for c in range(NC):
                act.wait_ge(tr_ps, 16 + c + 1)
                s.activation(n1T[:, 512 * c:512 * (c + 1)], bank(4 + c), ACT.Identity, bias=ln_b[0], scale=ln_w[0]).then_inc(tr_ev, 1)
            act.wait_ge(tr_ev, 20)
            s.activation(zz.rearrange("p t c -> p (t c)"), n1T[:, :], ACT.Square).then_inc(sq_ready, 1)
            rows_out(1, 4)
            root_squares(1)
            attention(1)
            for c in range(NC):
                act.wait_ge(att[1]["pj_ps"], c + 1)
                if c == 0:
                    act.wait_ge(att[1]["v_staged"], GROUPS)
                s.activation(sT1[:, 512 * c:512 * (c + 1)], bank(c), ACT.Copy).then_inc(att[1]["pj_ev"], 1)

            with act.Fori(0, BATCH) as b:
                for e in range(EXP):
                    act.wait_ge(x_made, b * EXP + e + 1)
                    if e >= 2:
                        act.wait_ge(x_used, b * EXP + e - 1)
                    s.activation(Xe_r[0][:, e % 2, :], Xe[e % 2], ACT.Copy).then_inc(ehi_made, 1)
                act.wait_ge(x_used, b * EXP + EXP)
                for c in range(2):
                    s.activation(qT[:, 512 * c:512 * (c + 1)], bank(c), ACT.Copy, scale=1.0 / math.sqrt(C)).then_inc(x_ev, 1)
                for c in range(2):
                    s.activation(vT[:, 512 * c:512 * (c + 1)], bank(4 + c), ACT.Copy).then_inc(x_ev, 1)
                for qt in range(KT):
                    act.wait_ge(s1_max, b * KT + qt + 1)
                    if qt >= 2:
                        act.wait_ge(pt_ps, b * KT + qt - 1)
                    w = (qt + 1) * P
                    s.activation(P1[qt % 2][:, 0:w], PS[:, 1024 * (qt % 2):1024 * (qt % 2) + w], ACT.Exp,
                                 bias=small[:, 4, qt:qt + 1], accum_out=small[:, 5, qt:qt + 1]).then_inc(s1_exp, 1)
                    if qt in (6, 7):
                        half = qt - 6
                        act.wait_ge(o1_ps, b * 2 + half + 1)
                        s.activation(attnT[:, bass.ds(b * SEQ + 512 * half, 512)], bank(6 + half), ACT.Copy).then_inc(o1_ev, 1)
            copies(4, lambda c: xtok[:, 4 * c:4 * c + 4, :].rearrange("p t c -> p (t c)"), 20)
            root_var(4)
            for c in range(NC):
                act.wait_ge(tr_ps, 24 + c + 1)
                s.activation(xnT[:, 512 * c:512 * (c + 1)], bank(c), ACT.Identity, bias=ln_b[1], scale=ln_w[1]).then_inc(tr_ev, 1)
            act.wait_ge(tr_ev, 28)
            for n in (4, 5):
                w = fw[:, n * 1024:(n + 1) * 1024].rearrange("p (e c) -> p e c", e=EXP)
                ins = s.activation(w_e_hi[n], w, ACT.Copy)
            ins.then_inc(mw_hi, 1)
            s.activation(zz.rearrange("p t c -> p (t c)"), xnT[:, :], ACT.Square).then_inc(sq_ready, 1)
            rows_out(2, 4)
            for c in range(NC):
                part = slice(512 * c, 512 * (c + 1))
                s.activation(n2_r[0][:, part], xnT[:, part], ACT.Copy).then_inc(n2hi_made, 1)
            root_squares(2)
            gate_exps(3)
            with act.Fori(0, BATCH) as b:
                def expert_hi(u):
                    act.wait_ge(i_g, b * 16 + u + 1)
                    if u >= 4:
                        act.wait_ge(i_used, b * 16 + u - 3)
                    s.activation(gg_r[0][:, u % 4, :], gg[:, u % 4, :], ACT.Copy).then_inc(mhi_made, 1)

                for u in range(2 * EXP):
                    act.wait_ge(i_ps, b * 16 + u + 1)
                    s.activation(ga[:, u % 4, :], bank(u % 4), ACT.Gelu).then_inc(i_gelu, 1)
                    if u >= 1:
                        expert_hi(u - 1)
                expert_hi(2 * EXP - 1)
            for c in range(NC):
                act.wait_ge(moe_ev, c + 1)
                s.activation(hsT[:, 512 * c:512 * (c + 1)], hsT[:, 512 * c:512 * (c + 1)], ACT.Silu).then_inc(fin_silu, 1)
            for c in range(NC):
                act.wait_ge(fin_ps, c + 1)
                s.activation(otok[:, 4 * c:4 * c + 4, :].rearrange("p t c -> p (t c)"), bank(c), ACT.Copy).then_inc(fin_ev, 1)

        @block.vector
        def _(dve):
            own = Chain(dve, dve_own)
            v = nc.vector
            mean, var, rs, dd = small[:, 0, :], small[:, 1, :], small[:, 2, :], small[:, 3, :]

            def layer_norm(n, src, dst, ready=None):
                for t in range(NT):
                    if ready and t % 4 == 0:
                        ready(t // 4)
                    ins = v.bn_stats(stats[:, t, :], src[:, t, :])
                own.link(ins)
                own.link(v.tensor_tensor(dd, stats[:, :, 1], stats[:, :, 4], ALU.add))
                own.link(v.tensor_scalar(mean, dd, 0.5, None, ALU.mult))
                own.link(v.tensor_tensor(dd, stats[:, :, 1], stats[:, :, 4], ALU.subtract))
                own.link(v.scalar_tensor_tensor(dd, dd, 0.25, dd, ALU.mult, ALU.mult))
                own.link(v.tensor_tensor(var, stats[:, :, 2], stats[:, :, 5], ALU.add))
                own.link(v.scalar_tensor_tensor(var, var, 1.0 / C, dd, ALU.mult, ALU.add))
                v.tensor_scalar(var, var, LN_EPS, None, ALU.add).then_inc(var_ready, 1)
                dve.wait_ge(rstd_ready, n)
                own.link(v.reciprocal(rs, rs))
                for t in range(NT):
                    ins = v.tensor_scalar(dst[:, t, :], src[:, t, :], mean[:, t:t + 1], rs[:, t:t + 1], ALU.subtract, ALU.mult)
                    if t % 4 == 3:
                        ins.then_inc(z_ready, 1)

            def split_rest(l, b):
                part = slice(b * SEQ, (b + 1) * SEQ)
                for n, (src, dst) in enumerate(((q32, qsp), (k32, ksp))):
                    dve.wait_ge(hi_done, 4 * l + 2 * b + n + 1)
                    v.tensor_tensor(src[:, part], src[:, part], dst[:, 0, part], ALU.subtract).then_inc(rest_done, 1)
                for n, (src, dst) in enumerate(((q32, qsp), (k32, ksp))):
                    dve.wait_ge(mid_done, 4 * l + 2 * b + n + 1)
                    v.tensor_tensor(dst[:, 2, part], src[:, part], dst[:, 1, part], ALU.subtract).then_inc(split_done, 1)

            def per_token(x):
                return x.unsqueeze(2).to_broadcast([P, NT, EXP])

            def per_expert(x):
                return x.unsqueeze(1).to_broadcast([P, NT, EXP])

            def gate_choice(n):
                lg, top2, act_mask, gated, _ = gate_bufs(n)

                def top(dst, src):
                    own.link(v.reduce_max(small[:, 7, :], src[:, :, :], axis=AX.X))
                    own.link(v.tensor_tensor(dst[:, :, :], src[:, :, :], per_token(small[:, 7, :]), ALU.is_equal))
                    own.link(v.tensor_tensor(dst[:, :, :], dst[:, :, :], per_expert(prefer[:, :]), ALU.mult))
                    own.link(v.reduce_max(small[:, 6, :], dst[:, :, :], axis=AX.X))
                    own.link(v.tensor_tensor(dst[:, :, :], dst[:, :, :], per_token(small[:, 6, :]), ALU.is_equal))

                top(top2, lg)
                own.link(v.scalar_tensor_tensor(act_mask[:, :, :], top2[:, :, :], NEG, lg[:, :, :], ALU.mult, ALU.add))
                top(gated, act_mask)
                own.link(v.tensor_tensor(top2[:, :, :], top2[:, :, :], gated[:, :, :], ALU.add))
                src = lg
                if n:
                    own.link(v.tensor_scalar(act_mask[:, :, :], lg[:, :, :], 0.0, None, ALU.is_gt))
                    own.link(v.reduce_max(small[:, 6, :], act_mask[:, :, :], axis=AX.X))
                    own.link(v.tensor_scalar(small[:, 6, :], small[:, 6, :], 0.5, None, ALU.is_lt))
                    own.link(v.tensor_tensor(top2[:, :, :], top2[:, :, :], per_token(small[:, 6, :]), ALU.mult))
                    own.link(v.tensor_tensor(top2[:, :, :], top2[:, :, :], act_mask[:, :, :], ALU.max))
                    own.link(v.tensor_scalar(lg[:, :, :], lg[:, :, :], 0.0, None, ALU.max))
                own.link(v.reduce_max(small[:, 7, :], src[:, :, :], axis=AX.X))
                v.tensor_tensor(gated[:, :, :], src[:, :, :], per_token(small[:, 7, :]), ALU.subtract).then_inc(gx_ready, 1)

            def gate_weights(n):
                _, top2, _, gated, comb = gate_bufs(n)
                dve.wait_ge(ge_ready, n + 1)
                own.link(v.tensor_tensor(gated[:, :, :], gated[:, :, :], top2[:, :, :], ALU.mult))
                own.link(v.reduce_sum(small[:, 8, :], gated[:, :, :], axis=AX.X))
                own.link(v.reciprocal(small[:, 9, :], small[:, 8, :]))
                if n:
                    dve.wait_ge(comb_stored, 16 * n)
                v.tensor_tensor(comb[:, :, :].rearrange("p e t -> p t e"), gated[:, :, :], per_token(small[:, 9, :]),
                                ALU.mult).then_inc(comb_ready, 1)

            def gate_out(n):
                dve.wait_ge(cb_ps, 1 if n == 0 else 2)
                v.tensor_copy(combT[:, :], bank((1, None, 5)[n], 0, P)).then_inc(cb_ev, 1)

            def gate(n):
                gate_choice(n)
                gate_weights(n)
                gate_out(n)

            def by_tile(x):
                return x.rearrange("p (c k e) -> p c k e", c=NC, e=EXP)

            def logits_of(n):
                return bank(n).rearrange("p (k c e) -> p c k e", k=4, c=NC)

            def gate_raw(n):
                dve.wait_ge(lg_ps, n + 1)
                v.tensor_copy(by_tile(gl[:, n, 0:128]), logits_of(6)[:, :, :, 0:EXP])
                v.tensor_copy(gl[:, n, 128:144].rearrange("p (c k) -> p c k", c=NC), logits_of(6)[:, :, :, EXP])
                v.tensor_copy(gl[:, n, 144:152], bank(5, 0, EXP)).then_inc(ss_ready, 1)

            def gate_logits(n):
                lg = gate_bufs(n)[0]
                dve.wait_ge(norm_ready, n)
                own.link(v.tensor_scalar(gl[:, n, 128:152], gl[:, n, 128:152], 1e-12, None, ALU.max))
                own.link(v.reciprocal(gl[:, n, 128:152], gl[:, n, 128:152]))
                raw = gl[:, n, 0:128].rearrange("p (t e) -> p t e", e=EXP)
                own.link(v.tensor_tensor(lg[:, :, :], raw, per_token(gl[:, n, 128:144]), ALU.mult))
                own.link(v.tensor_tensor(lg[:, :, :], lg[:, :, :], per_expert(gl[:, n, 144:152]), ALU.mult))
                own.link(v.tensor_tensor(lg[:, :, :], lg[:, :, :], per_expert(erow[:, n, :]), ALU.subtract))

            def attention(l):
                A = att[l]

                def first_units():
                    def move():
                        U, (_, n, (j, q, w)) = pending.pop()
                        dve.wait_ge(own.sem, made[U])
                        v.tensor_copy(mx[:, n, j * KT + q:j * KT + q + 1], Pr[:, U % 8, w // 2 - 1:w // 2]).then_inc(A["ring_free"], 1)

                    pending, made, halves = [], {}, 0
                    for U, what in enumerate(s_sequence(l, True)):
                        if what[0] == "S":
                            w, lo = what[2][2], 1024 * (U % 4)
                            halves += 1
                            dve.wait_ge(A["half_out"], halves)
                            own.n += 1
                            made[U] = own.n
                            v.tensor_tensor_scan(Pr[:, U % 8, 0:w // 2], PS[:, lo:lo + w // 2], Pr[:, U % 8, 0:w // 2], -3.0e38,
                                                 ALU.max, ALU.max).then_inc(own.sem, 1)
                            if pending:
                                move()
                            pending.append((U, what))
                        else:
                            move()
                            unit(U, U % 4, ("M", 0), 0)
                    move()

                def unit(U, parity, what, mpar):
                    dve.wait_ge(A["ring_full"], U + 1)
                    lo = 1024 * parity
                    if what[0] == "S":
                        j, q, w = what[2]
                        mpar = (mpar + what[1]) % 2
                        v.reduce_max(mx[:, mpar, j * KT + q:j * KT + q + 1], PS[:, lo:lo + w], axis=AX.X).then_inc(A["ring_free"], 1)
                    elif what[0] == "R":
                        G, half = what[1]
                        dst = OT[:, G, 512 * half:512 * (half + 1)]
                        v.tensor_tensor(dst, Osb[:, half, :], PS[:, lo:lo + 512], ALU.mult).then_inc(A["ring_free"], 1)
                    elif what[0] == "C":
                        v.tensor_copy(combT[:, :], PS[:, lo:lo + P]).then_inc(A["ring_free"], 1)
                    else:
                        G = what[1]
                        n = HG * KT
                        src = PS[0:n, lo:lo + P]
                        if not (isinstance(G, int) and G == 0):
                            dve.wait_ge(A["m_ld"], G * 48)
                        own.link(v.tensor_scalar(mrow[:, 0, :], src, -1.0, None, ALU.mult))
                        v.scalar_tensor_tensor(mres[:, :], src, -1.0, mrow[:, 0, :], ALU.mult, ALU.subtract).then_inc(A["ring_free"], 1)
                        dve.wait_ge(A["ring_free"], U + 1)
                        own.link(v.tensor_copy(mrow[:, 1, :], mres[:, :]))
                        v.tensor_tensor(mrow[:, 2, :], mres[:, :], mrow[:, 1, :], ALU.subtract).then_inc(A["m_ready"], 1)

                def invert(G, half):
                    dve.wait_ge(A[f"sum_in{half}"], G * 16 + 16)
                    v.reciprocal(rsums[:, half, :], sums[:, half, :]).then_inc(A["sum_inv"], 1)

                def units(G, U, parity, plan, mpar):
                    n = 0
                    for step in plan:
                        for what in step:
                            if what[0] == "Q":
                                invert(G - 1 if what[1] else G, what[1])
                                continue
                            if what == ("G", 0):
                                gate_logits(1)
                                gate_choice(1)
                                continue
                            if what == ("G", 1):
                                gate_weights(1)
                                continue
                            if what[0] == "R":
                                what = ("R", (G - 1 if what[1] else G, what[1]))
                            if what[0] == "M":
                                what = ("M", G + 1)
                            unit(U + n, (parity + n) % 2, what, mpar)
                            n += 1

                def body(G, parity, carry, s_phase):
                    base = ring_base(l, G)
                    base_parity = (base if isinstance(G, int) else ring_base(l, 2 - parity)) % 2
                    units(G, base, base_parity, ring_plan(l, carry, s_phase), 1 - parity)

                first_units()
                groups(dve, body, own, 4)
                invert(GROUPS - 1, 1)
                last = last_unit(l)
                unit(last, last % 2, ("R", (GROUPS - 1, 1)), 0)

            def x_ready(c):
                dve.wait_ge(x_in[c], 16)

            layer_norm(1, xtok, ztok, x_ready)
            dve.wait_ge(w_in, 16 * FIRST_LOADS)
            own.link(v.tensor_scalar(qscale, temp, 0.1, 10.0, ALU.max, ALU.min))
            own.link(v.tensor_scalar(qscale, qscale, math.sqrt(C), None, ALU.mult))
            own.link(v.reciprocal(qscale, qscale))

            def values(l, first):
                for c in range(NC):
                    dve.wait_ge(v_ps, 4 * l + c + 1)
                    b, k0 = c // 2, 4 * (c % 2)
                    dst = V[:, b * NG:(b + 1) * NG, k0:k0 + 4, :].rearrange("p g k c -> p k g c")
                    src = bank(first + c).rearrange("p (k g c) -> p k g c", k=4, g=NG)
                    if l == 0:
                        bias = bvb[:, :].rearrange("p (g c) -> p g c", g=NG).unsqueeze(1).to_broadcast([P, 4, NG, 32])
                        v.tensor_tensor(dst, src, bias, ALU.add).then_inc(v_ev, 1)
                    else:
                        v.tensor_copy(dst, src).then_inc(v_ev, 1)

            for b in range(BATCH):
                for c in (2 * b, 2 * b + 1):
                    dve.wait_ge(q_ps, c + 1)
                    v.tensor_scalar(q32[:, 512 * c:512 * (c + 1)], bank(4 + c), bq, qscale, ALU.add, ALU.mult).then_inc(q_ev, 1)
                split_rest(0, b)
            values(0, 4)
            def weights_lo(n, slot):
                dve.wait_ge(whi_made, n + 1)
                v.tensor_tensor(w_r[:, slot, 1, :], fw0[:, slot, 0:768], w_r[:, slot, 0, :], ALU.subtract).then_inc(wlo_made, 1)

            weights_lo(0, 0)
            dve.wait_ge(tbl_in, 16)
            own.link(v.memset(dfull[:, :], 0.0))
            own.link(v.tensor_scalar(dfull[:, DREV - 1 - REL:DREV - 1], tblr[:, :], tblr[:, 0:1], qscale[0:HEADS, :],
                                     ALU.subtract, ALU.mult))
            own.link(v.tensor_copy(dpart[:, 0, :], dfull[:, :]))
            own.link(v.tensor_tensor(dfull[:, :], dfull[:, :], dpart[:, 0, :], ALU.subtract))
            own.link(v.tensor_copy(dpart[:, 1, :], dfull[:, :]))
            v.tensor_tensor(dpart[:, 2, :], dfull[:, :], dpart[:, 1, :], ALU.subtract).then_inc(drev_ready, 1)
            dve.wait_ge(lg_ps, 1)
            dve.wait_ge(const_done, 1)
            lg = gate_bufs(0)[0]
            own.link(v.tensor_copy(by_tile(lg[:, :, :].rearrange("p t e -> p (t e)")), logits_of(2)[:, :, :, 0:EXP]))
            own.link(v.tensor_tensor(lg[:, :, :], lg[:, :, :], per_expert(erow[:, 0, :]), ALU.add))
            gate(0)
            dve.wait_ge(gate_exp, 1)
            own.link(v.tensor_scalar(gl[:, 0, 0:2 * EXP], gl[:, 0, 0:2 * EXP], 1.0, None, ALU.add))
            own.link(v.reciprocal(erow[:, 1:3, :].rearrange("p a e -> p (a e)"), gl[:, 0, 0:2 * EXP]))
            v.tensor_tensor(simsq[:, :, :], router[:, 1:3, 0:EXP], router[:, 1:3, 0:EXP], ALU.mult).then_inc(gneg, 1)

            def g_lo(base, u):
                U = base + u
                dve.wait_ge(ghi_made, U + 1)
                v.tensor_tensor(g_r[1][:, u % 4, :], fg[:, u % 4, :], g_r[0][:, u % 4, :], ALU.subtract).then_inc(glo_made, 1)

            def ffn_units(n, n_term, base, slot, kind):
                start = n_term + base
                for u in range(8):
                    if u >= 2:
                        g_lo(start, u - 2)
                    elif not (isinstance(start, int) and start == 0):
                        g_lo(start - 8, u + 6)
                    dve.wait_ge(a_made, start + u + 1)
                    if not (isinstance(start, int) and start + u < 4):
                        dve.wait_ge(glo_made, start + u - 3)
                    v.tensor_tensor(fg[:, u % 4, :], bank(2 * (u % 2) + 1), fa[:, u % 2, :], ALU.mult).then_inc(g_made, 1)
                    if u == 4 and not (isinstance(n, int) and n == FFN_SEQ - 1):
                        weights_lo(n + 1, 1 - slot)

            dve.wait_ge(drev_stored, 16 * PARTS * BATCH)
            ffn_experts(dve, ffn_units)
            for u in (6, 7):
                g_lo(72, u)
            attention(0)
            for c in range(NC):
                dve.wait_ge(att[0]["pj_ps"], c + 1)
                part = slice(512 * c, 512 * (c + 1))
                dve.wait_ge(y_ev, c + 1)
                own.link(v.scalar_tensor_tensor(n1T[:, part], bank(c), bp, n1T[:, part], ALU.add, ALU.mult))
                v.tensor_tensor(xT[:, part], xT[:, part], n1T[:, part], ALU.add).then_inc(att[0]["pj_ev"], 1)

            layer_norm(2, xtok, ztok, lambda c: dve.wait_ge(tr_ev, 8 + c + 1))
            for b in range(BATCH):
                for c in (2 * b, 2 * b + 1):
                    dve.wait_ge(q_ps, 4 + c + 1)
                    v.tensor_scalar(q32[:, 512 * c:512 * (c + 1)], bank(c), 1.0 / math.sqrt(HD), None, ALU.mult).then_inc(q_ev, 1)
                split_rest(1, b)
            values(1, 0)
            dve.wait_ge(z_ready, 8)
            layer_norm(3, ztok, zz)
            gate_raw(1)
            attention(1)

            dve.wait_ge(att[1]["pj_ev"], NC)
            with dve.Fori(0, BATCH) as b:
                own.enter(b, 16)
                tok = bass.ds(b * SEQ, SEQ)
                for e in range(EXP + 1):
                    if e < EXP:
                        if e >= 2:
                            dve.wait_ge(elo_made, b * EXP + e - 1)
                        dve.wait_ge(rw_in[e], 16)
                        v.tensor_tensor(Xe[e % 2], n1T[:, tok], rwb[:, e, tok], ALU.mult).then_inc(x_made, 1)
                    if e >= 1:
                        dve.wait_ge(ehi_made, b * EXP + e)
                        v.tensor_tensor(Xe_r[1][:, (e - 1) % 2, :], Xe[(e - 1) % 2], Xe_r[0][:, (e - 1) % 2, :],
                                        ALU.subtract).then_inc(elo_made, 1)
                dve.wait_ge(x_used, b * EXP + EXP)
                for c in range(2):
                    v.tensor_copy(kT[:, 512 * c:512 * (c + 1)], bank(2 + c)).then_inc(vt_ev, 1)
                for c in range(2):
                    dve.wait_ge(vt_ps, b * 2 + c + 1)
                    v.tensor_copy(vtok[:, 4 * c:4 * c + 4, :].rearrange("p k c -> p (k c)"), bank(6 + c)).then_inc(vt_ev, 1)
                for i in range(KT + 2):
                    if i < KT:
                        w = (i + 1) * P
                        dve.wait_ge(s1_ps, b * KT + i + 1)
                        own.link(v.reduce_max(small[:, 3, i:i + 1], PS[:, 1024 * (i % 2):1024 * (i % 2) + w], axis=AX.X))
                        v.tensor_scalar(small[:, 4, i:i + 1], small[:, 3, i:i + 1], -1.0, None, ALU.mult).then_inc(s1_max, 1)
                    if 1 <= i <= KT:
                        q = i - 1
                        w = (q + 1) * P
                        dve.wait_ge(s1_exp, b * KT + q + 1)
                        own.link(v.reciprocal(small[:, 6, q:q + 1], small[:, 5, q:q + 1]))
                        v.tensor_scalar(P1[q % 2][:, 0:w], P1[q % 2][:, 0:w], small[:, 6, q:q + 1], None, ALU.mult).then_inc(s1_p, 1)
                    if i >= 2:
                        q = i - 2
                        dve.wait_ge(pt_ps, b * KT + q + 1)
                        if q == 4:
                            dve.wait_ge(o1_ps, b * 2 + 1)
                        src = PS[:, 2048:2048 + (q + 1) * P].rearrange("p (k q) -> p k q", q=P)
                        v.tensor_copy(PT[:, 0:q + 1, (q % 4) * P:(q % 4 + 1) * P], src).then_inc(pt_ev, 1)
                for e in range(EXP):
                    if e == 0:
                        dve.wait_ge(o1_ev, b * 2 + 2)
                    if e >= 2:
                        dve.wait_ge(ox_used, b * EXP + e - 1)
                    v.tensor_tensor(Xe[e % 2], attnT[:, tok], rwb[:, e, tok], ALU.mult).then_inc(ox_made, 1)
                dve.wait_ge(ox_used, b * EXP + EXP)
                for c in range(2):
                    sl = bass.ds(b * SEQ + 512 * c, 512)
                    v.tensor_tensor(hsT[:, sl], bank(c), xnT[:, sl], ALU.add).then_inc(hs_ev, 1)
            own.leave(2)
            layer_norm(4, xtok, ztok, lambda c: dve.wait_ge(tr_ev, 20 + c + 1))
            gate_raw(2)
            gate_logits(2)
            gate(2)
            with dve.Fori(0, BATCH) as b:
                for u in range(2 * EXP + 2):
                    if u >= 2:
                        dve.wait_ge(mhi_made, b * 16 + u - 1)
                        v.tensor_tensor(gg_r[1][:, (u - 2) % 4, :], gg[:, (u - 2) % 4, :], gg_r[0][:, (u - 2) % 4, :],
                                        ALU.subtract).then_inc(mlo_made, 1)
                    if u < 2 * EXP:
                        e, c = u // 2, u % 2
                        dve.wait_ge(i_gelu, b * 16 + u + 1)
                        if u >= 4:
                            dve.wait_ge(mlo_made, b * 16 + u - 3)
                        dve.wait_ge(rw_in[e], 32)
                        v.tensor_tensor(gg[:, u % 4, :], ga[:, u % 4, :], rwb[:, e, bass.ds(b * SEQ + 512 * c, 512)], ALU.mult).then_inc(i_g, 1)
                dve.wait_ge(i_used, b * 16 + 16)
                for c in range(2):
                    sl = bass.ds(b * SEQ + 512 * c, 512)
                    v.tensor_tensor(hsT[:, sl], bank(4 + c), hsT[:, sl], ALU.add).then_inc(moe_ev, 1)
            for c in range(NC):
                part = slice(512 * c, 512 * (c + 1))
                dve.wait_ge(fin_silu, c + 1)
                own.link(v.tensor_tensor(hsT[:, part], hsT[:, part], sT1[:, part], ALU.mult))
                v.tensor_tensor(hsT[:, part], hsT[:, part], xT[:, part], ALU.add).then_inc(fin_x, 1)

        @block.tensor
        def _(pe):
            def mm(out_, lhsT, rhs, start=True, stop=True):
                return nc.tensor.matmul(out_, lhsT, rhs, start=start, stop=stop)

            def split_mm(out_, w, x, start=True, stop=True):
                mm(out_, w[0], x[0], start=start, stop=False)
                mm(out_, w[0], x[1], start=False, stop=False)
                return mm(out_, w[1], x[0], start=False, stop=stop)

            def transposes(src, first, ready):
                for c in range(NC):
                    ready(c)
                    for k in range(4):
                        ins = nc.tensor.transpose(bank(first + c, P * k, P * (k + 1)), src(4 * c + k), ident[:, :])
                    ins.then_inc(tr_ps, 1)

            def project_qk(l, q_first, k_first, ready):
                for b in range(BATCH):
                    for w, first, done in ((wq, q_first, q_ps), (wk, k_first, k_ps)):
                        for c in (2 * b, 2 * b + 1):
                            ready(c)
                            mm(bank(first + c), w[:, l, :], xnT[:, 512 * c:512 * (c + 1)]).then_inc(done, 1)

            def project_v(l, first, ready):
                for c in range(NC):
                    ready(c)
                    for k in range(4):
                        t = 4 * c + k
                        ins = mm(bank(first + c, P * k, P * (k + 1)), xnT[:, t * P:(t + 1) * P], wv[:, l, :])
                    ins.then_inc(v_ps, 1)

            def comb_T(n, b_):
                pe.wait_ge(comb_ready, n + 1)
                nc.tensor.transpose(bank(b_, 0, P), gate_bufs(n)[4][:, :, :].rearrange("p e t -> p (e t)"), ident[:, :]).then_inc(cb_ps, 1)

            def gate_rows(n, srcT, b_rows, b_out):
                if n:
                    pe.wait_ge(sq_ready, n)
                sq = zz.rearrange("p t c -> p (t c)")
                for c in range(NC):
                    part = slice(512 * c, 512 * (c + 1))
                    dst = PS[32 * c:32 * (c + 1), 512 * b_rows:512 * (b_rows + 1)]
                    ins = mm(dst, router[:, n, :], srcT[:, part], stop=not n)
                    if n:
                        ins = mm(dst, sum_col[:, :], sq[:, part], start=False)
                ins.then_inc(rows_ps, 1)
                if n:
                    pe.wait_ge(gneg, 1)
                    mm(bank(5, 0, EXP), ones[:, :], simsq[:, n - 1, :])
                pe.wait_ge(rows_ev, n + 1)
                for k in range(4):
                    ins = nc.tensor.transpose(bank(b_out, P * k, P * (k + 1)), lrow[:, P * k:P * (k + 1)], ident[:, :])
                ins.then_inc(lg_ps, 1)

            def attention(l):
                A = att[l]
                steps = t_steps(l)
                n_st = len(steps) * HG
                half0 = sum(1 for x in steps if x[0] == 0)

                def s_unit(U, parity, j, q, w, slot):
                    lo = 1024 * parity
                    queries = stack["Sq"][0:STACK, slot, j, q * P:(q + 1) * P]
                    for k0 in range(0, w, 512):
                        k1 = min(w, k0 + 512)
                        extra = []
                        if l == 0 and q < 2 and k0 == 512:
                            h0 = 256 if q == 0 else 384
                            extra = [(h0, flip[:, :], Hst[:, slot, j, part, 0:512 - h0]) for part in range(PARTS)]
                        if l == 1 and k1 == w:
                            extra = [(k1 - k0 - P, identb[:, :], mask_qk[:, :])]
                        ins = mm(PS[:, lo + k0:lo + k1], queries, stack["Sk"][0:STACK, slot, j, k0:k1], stop=not extra)
                        for n, (c0, lhsT, rhs) in enumerate(extra):
                            ins = mm(PS[:, lo + k0 + c0:lo + k1], lhsT, rhs, start=False, stop=n == len(extra) - 1)
                    ins.then_inc(A["ring_full"], 1)

                def unit(U, parity, what, slot, last_m=False, first=False):
                    if not first:
                        pe.wait_ge(A["ring_free"], U - 1)
                    if what[0] == "S":
                        s_unit(U, parity, *what[2], (slot + what[1]) % 2)
                    elif what[0] == "R":
                        G, half = what[1]
                        pe.wait_ge(A["rrow_in"], G * 32 + 16 * half + 16)
                        mm(PS[:, 1024 * parity:1024 * parity + 512], sel[:, :], Osb[:, half, :]).then_inc(A["ring_full"], 1)
                    elif what[0] == "C":
                        pe.wait_ge(comb_ready, 2)
                        nc.tensor.transpose(PS[:, 1024 * parity:1024 * parity + P], gate_bufs(1)[4][:, :, :].rearrange("p e t -> p (e t)"),
                                            ident[:, :]).then_inc(A["ring_full"], 1)
                    else:
                        pe.wait_ge(A["ring_free"], U if last_m else U - 1)
                        nc.tensor.transpose(PS[0:HG * KT, 1024 * parity:1024 * parity + P], mx[:, slot, :], ident[:, :])\
                            .then_inc(A["ring_full"], 1)

                def st_step(G, i, parity, carry, heads):
                    h, kt, off = steps[i]
                    for j in heads:
                        m = HG * i + j
                        if m >= 3:
                            pe.wait_ge(A["e_done"], G * n_st + m - 2)
                        elif carry:
                            pe.wait_ge(A["e_done"], G * n_st)
                        w = 512 - off
                        q0 = 512 * h + off
                        dst = bank(4 + m % 3, 0, w)
                        extra = []
                        if l == 0 and h == 0 and kt == KT - 2:
                            extra = [(0, Hst[:, parity, j, part, 0:P], flip[:, :]) for part in range(PARTS)]
                        if l == 0 and h == 0 and kt == KT - 1:
                            extra = [(q * P, Hst[:, parity, j, part, P * (1 - q):P * (2 - q)], flip[:, :])
                                     for q in range(2) for part in range(PARTS)]
                        if l == 1 and kt * P == q0:
                            extra = [(0, identb[:, :], mask_kq[:, :])]
                        ins = mm(dst, stack["Tk"][0:STACK + PARTS, parity, j, kt * P:(kt + 1) * P],
                                 stack["Tq"][0:STACK + PARTS, parity, j, q0:q0 + w], stop=not extra)
                        for n, (c0, lhsT, rhs) in enumerate(extra):
                            ins = mm(bank(4 + m % 3, c0, c0 + P), lhsT, rhs, start=False, stop=n == len(extra) - 1)
                        ins.then_inc(A["st_ps"], 1)

                def av_step(G, i, parity):
                    h, kt, off = steps[i]
                    pe.wait_ge(A["e_done"], G * n_st + HG * (i + 1))
                    if i == 0:
                        pe.wait_ge(A["v_staged"], G + 1)
                        if not (isinstance(G, int) and G == 0):
                            pe.wait_ge(A["o_ev"], G * 2)
                    if i == half0:
                        pe.wait_ge(A["o_ev"], G * 2 + 1)
                    last = i + 1 == len(steps) or steps[i + 1][0] != h
                    for j in range(HG):
                        ins = mm(PS[32 * j:32 * (j + 1), 7 * 512 + off:8 * 512], Vst[:, parity, kt, j, :],
                                 Pr[:, (HG * i + j) % 8, 0:512 - off], start=kt == 0, stop=last)
                    ins.then_inc(A["av_done"], 1)

                def body(G, parity, carry, s_phase):
                    plan = ring_plan(l, carry, s_phase)
                    U = 0
                    base = ring_base(l, G)
                    base_parity = (base if isinstance(G, int) else ring_base(l, 2 - parity)) % 2
                    begun = biased = False
                    for i in range(len(steps)):
                        if i == 0:
                            wait_loads("t", G, parity)
                            pe.wait_ge(A["m_ld"], G * 48 + 48)
                        todo = [w for w in plan[i] if w[0] not in "QG"]
                        for what in todo:
                            if what[0] == "S" and what[1] == 1 and not begun:
                                wait_loads("s", G + 2, parity)
                                begun = True
                            if l == 0 and what[0] == "S" and what[1] == 0 and what[2][1] < 2 and not biased:
                                wait_bias(G + 1, 1 - parity)
                                biased = True
                        for j in range(HG):
                            st_step(G, i, parity, carry, (j,))
                            if j == 2:
                                if i == 0 and carry:
                                    av_step(G - 1, len(steps) - 1, 1 - parity)
                                if i > 0:
                                    av_step(G, i - 1, parity)
                            now = len(todo) if j == HG - 1 else 0 if j == 1 and len(todo) < 3 else 1
                            for what in todo[:now]:
                                if what[0] == "R":
                                    what = ("R", (G - 1 if what[1] else G, what[1]))
                                unit(base + U, (base_parity + U) % 2, what, 1 - parity, s_phase == 1)
                                U += 1
                            todo = todo[now:]

                def wait_loads(which, G, parity):
                    pe.wait_ge(A[f"{which}_ld{parity}"], (G - parity) * 64 + 128)

                def wait_bias(G, parity):
                    pe.wait_ge(A[f"h_ld{parity}"], (G - parity) * 32 + 64)

                wait_loads("s", 0, 0)
                begun = biased = False
                for U, what in enumerate(s_sequence(l, True)):
                    if what[0] == "S" and what[1] == 1 and not begun:
                        wait_loads("s", 1, 1)
                        begun = True
                    if l == 0 and what[0] == "S" and what[1] == 0 and what[2][1] < 2 and not biased:
                        wait_bias(0, 0)
                        biased = True
                    if l == 0 and U == 2:
                        pe.wait_ge(y_ev, NC)
                    if U >= 4:
                        pe.wait_ge(A["ring_free"], U - 3)
                    unit(U, U % 4, what, 0, first=True)
                pe.wait_ge(A["ring_free"], UNITS + AHEAD[l])
                groups(pe, body)
                av_step(GROUPS - 1, len(steps) - 1, 1)
                last = last_unit(l)
                unit(last, last % 2, ("R", (GROUPS - 1, 1)), 0)
                pe.wait_ge(A["ring_free"], last + 1)
                for c in range(NC):
                    for g in range(NG):
                        ins = mm(bank(c), wo[:, l, g, :], OT[:, (c // 2) * NG + g, 512 * (c % 2):512 * (c % 2 + 1)],
                                 start=g == 0, stop=g == NG - 1)
                    ins.then_inc(A["pj_ps"], 1)

            pe.wait_ge(const_done, 1)
            transposes(lambda t: xtok[:, t, :], 4, lambda c: pe.wait_ge(x_in[c], 16))
            transposes(lambda t: ztok[:, t, :], 0, lambda c: pe.wait_ge(z_ready, c + 1))
            pe.wait_ge(w_in, 16 * FIRST_LOADS)
            project_qk(0, 4, 0, lambda c: pe.wait_ge(tr_ev, 4 + c + 1))
            project_v(0, 4, lambda c: pe.wait_ge(q_ev, c + 1))
            pe.wait_ge(k_ev, 4)
            pe.wait_ge(router_in, 16)
            gate_rows(0, xnT, 0, 2)

            def up(start, u, slot):
                if not (isinstance(start, int) and start + u < 2):
                    pe.wait_ge(g_made, start + u - 1)
                x = [x_r[h][:, 512 * (u // 2):512 * (u // 2 + 1)] for h in range(2)]
                for n in range(2):
                    w0 = 256 * n + 128 * (u % 2)
                    ins = split_mm(bank(2 * (u % 2) + n), [w_r[:, slot, h, w0:w0 + 128] for h in range(2)], x)
                ins.then_inc(h_ps, 1)

            def down(start, u, slot, first, last):
                pe.wait_ge(glo_made, start + u + 1)
                w0 = 512 + 128 * (u % 2)
                split_mm(bank(4 + u // 2), [w_r[:, slot, h, w0:w0 + 128] for h in range(2)],
                         [g_r[h][:, u % 4, :] for h in range(2)], start=first and u % 2 == 0,
                         stop=last and u % 2 == 1).then_inc(y_done, 1)

            LAG = 3

            def ffn_expert(n, n_term, base, slot, kind):
                start = n_term + base
                here = isinstance(start, int)
                for u in range(8):
                    if u == 0:
                        pe.wait_ge(wlo_made, n + 1)
                    if here and start == 0 and u % 2 == 0:
                        pe.wait_ge(xlo_made, u // 2 + 1)
                    up(start, u, slot)
                    if u >= LAG:
                        down(start, u - LAG, slot, here and start == 0, here and base == 72)
                    elif not (here and start == 0):
                        down(start - 8, u + 8 - LAG, 1 - slot, here and start == 8, False)

            comb_T(0, 1)
            pe.wait_ge(cb_ev, 1)
            pe.wait_ge(v_ev, 4)
            ffn_experts(pe, ffn_expert)
            for u in range(8 - LAG, 8):
                down(72, u, 1, False, True)
            attention(0)

            transposes(lambda t: xT[:, t * P:(t + 1) * P], 4, lambda c: pe.wait_ge(att[0]["pj_ev"], c + 1))
            transposes(lambda t: ztok[:, t, :], 0, lambda c: pe.wait_ge(z_ready, 4 + c + 1))
            project_qk(1, 0, 4, lambda c: pe.wait_ge(tr_ev, 12 + c + 1))
            project_v(1, 0, lambda c: pe.wait_ge(q_ev, 4 + c + 1))
            pe.wait_ge(k_ev, 8)
            transposes(lambda t: zz[:, t, :], 4, lambda c: pe.wait_ge(z_ready, 8 + c + 1))
            pe.wait_ge(tr_ev, 20)
            gate_rows(1, n1T, 4, 6)
            pe.wait_ge(ss_ready, 1)
            pe.wait_ge(v_ev, 8)
            attention(1)

            pe.wait_ge(ew_split, 3)
            pe.wait_ge(att[1]["pj_ev"], NC)
            with pe.Fori(0, BATCH) as b:
                for e in range(EXP):
                    pe.wait_ge(elo_made, b * EXP + e + 1)
                    for n in range(3):
                        for c in range(2):
                            ins = split_mm(bank(2 * n + c), [w_e_hi[n][:, e, :], w_e_lo[n][:, e, :]],
                                           [Xe_r[h][:, e % 2, 512 * c:512 * (c + 1)] for h in range(2)], start=e == 0, stop=e == EXP - 1)
                    ins.then_inc(x_used, 1)
                pe.wait_ge(x_ev, b * 4 + 4)
                for c in range(2):
                    for k in range(4):
                        ins = nc.tensor.transpose(bank(6 + c, P * k, P * (k + 1)), vT[:, (4 * c + k) * P:(4 * c + k + 1) * P], ident[:, :])
                    ins.then_inc(vt_ps, 1)
                pe.wait_ge(vt_ev, b * 4 + 4)

                def scores(qt):
                    w = (qt + 1) * P
                    if qt >= 2:
                        pe.wait_ge(s1_exp, b * KT + qt - 1)
                    lo = 1024 * (qt % 2)
                    for k0 in range(0, w, 512):
                        k1 = min(w, k0 + 512)
                        ins = mm(PS[:, lo + k0:lo + k1], qT[:, qt * P:(qt + 1) * P], kT[:, k0:k1], stop=k1 != w)
                    ins = mm(PS[:, lo + w - P:lo + w], identb[:, :], mask_qk[:, :], start=False)
                    ins.then_inc(s1_ps, 1)

                def p_transposes(qt):
                    pe.wait_ge(s1_p, b * KT + qt + 1)
                    if qt:
                        pe.wait_ge(pt_ev, b * KT + qt)
                    for k in range(qt + 1):
                        ins = nc.tensor.transpose(PS[:, 2048 + k * P:2048 + (k + 1) * P], P1[qt % 2][:, k * P:(k + 1) * P], ident[:, :])
                    ins.then_inc(pt_ps, 1)

                def values(half):
                    pe.wait_ge(pt_ev, b * KT + 4 * half + 4)
                    for kt in range(4 * half + 4):
                        off = max(0, kt - 4 * half) * P
                        ins = mm(bank(6 + half, off, 512), vtok[:, kt, :], PT[:, kt, off:512], start=kt == 0, stop=kt == 4 * half + 3)
                    ins.then_inc(o1_ps, 1)

                for qt in range(KT):
                    scores(qt)
                    if qt == 6:
                        values(0)
                    if qt >= 2:
                        p_transposes(qt - 2)
                p_transposes(KT - 2)
                p_transposes(KT - 1)
                values(1)
                for e in range(EXP):
                    pe.wait_ge(ox_made, b * EXP + e + 1)
                    for c in range(2):
                        ins = mm(bank(c), fwo[:, e, :], Xe[e % 2][:, 512 * c:512 * (c + 1)], start=e == 0, stop=e == EXP - 1)
                    ins.then_inc(ox_used, 1)
            pe.wait_ge(hs_ev, 4)
            transposes(lambda t: hsT[:, t * P:(t + 1) * P], 4, lambda c: None)
            transposes(lambda t: ztok[:, t, :], 0, lambda c: pe.wait_ge(z_ready, 12 + c + 1))
            pe.wait_ge(tr_ev, 28)
            gate_rows(2, xnT, 4, 6)
            comb_T(2, 5)
            pe.wait_ge(cb_ev, 2)
            pe.wait_ge(mw_split, 2)
            pe.wait_ge(n2lo_made, NC)
            with pe.Fori(0, BATCH) as b:
                for u in range(2 * EXP + LAG):
                    if u < 2 * EXP:
                        e, c = u // 2, u % 2
                        if u >= 4:
                            pe.wait_ge(i_gelu, b * 16 + u - 3)
                        split_mm(bank(u % 4), [w_e_hi[4][:, e, :], w_e_lo[4][:, e, :]],
                                 [n2_r[h][:, bass.ds(b * SEQ + 512 * c, 512)] for h in range(2)]).then_inc(i_ps, 1)
                    if u >= LAG:
                        d = u - LAG
                        e, c = d // 2, d % 2
                        pe.wait_ge(mlo_made, b * 16 + d + 1)
                        split_mm(bank(4 + c), [w_e_hi[5][:, e, :], w_e_lo[5][:, e, :]],
                                 [gg_r[h][:, d % 4, :] for h in range(2)], start=e == 0, stop=e == EXP - 1).then_inc(i_used, 1)
            for c in range(NC):
                pe.wait_ge(fin_x, c + 1)
                for k in range(4):
                    t = 4 * c + k
                    ins = nc.tensor.transpose(bank(c, P * k, P * (k + 1)), hsT[:, t * P:(t + 1) * P], ident[:, :])
                ins.then_inc(fin_ps, 1)


_NAMES = ["L0_attn_x", "L0_attn_Wq", "L0_attn_bq", "L0_attn_Wk", "L0_attn_bk", "L0_attn_Wv", "L0_attn_bv", "L0_attn_Wp",
          "L0_attn_bp", "L0_attn_temperature", "L0_ffn_expert_bias", "L1_ffn_ln1_w", "L1_ffn_ln1_b", "L1_ffn_ln2_w",
          "L1_ffn_ln2_b", "L1_ffn_smha_sim", "L1_ffn_smha_gates", "L1_ffn_q_proj", "L1_ffn_k_proj", "L1_ffn_v_proj",
          "L1_ffn_o_proj", "L1_ffn_moe_sim", "L1_ffn_moe_gates", "L1_ffn_w1", "L1_ffn_w2"]


def kernel(**inputs):
    import numpy as np
    import concourse.bacc as bacc
    from concourse.bass_utils import run_bass_kernel_spmd

    x = {k: np.asarray(v) for k, v in inputs.items()}
    laid = {n: x[n] for n in _NAMES}
    laid["L1_WQT"], laid["L1_WKT"] = x["L1_attn_W_Q"].T, x["L1_attn_W_K"].T
    laid["L1_WVT"], laid["L1_WOT"] = x["L1_attn_W_V"].T, x["L1_attn_W_O"].T
    laid["router_T"] = x["L0_ffn_router_w"].T
    laid["bias_rev_T"] = x["L0_attn_bias_table"][::-1].T

    def experts(w1, w3, w2):
        down = w2.transpose(0, 2, 1).reshape(w2.shape[0], 2, 128, 128).transpose(0, 2, 1, 3).reshape(w2.shape[0], 128, 256)
        return np.concatenate([w1.transpose(0, 2, 1), w3.transpose(0, 2, 1), down], axis=2)

    shared = experts(x["L0_ffn_sw1"], x["L0_ffn_sw3"], x["L0_ffn_sw2"])
    routed = experts(x["L0_ffn_w1"], x["L0_ffn_w3"], x["L0_ffn_w2"])
    laid["ffn_w"] = np.concatenate([shared[0:1], routed, shared[1:2]], axis=0)

    nc = bacc.Bacc("TRN2", target_bir_lowering=False, num_devices=1)
    arrays, args = {}, {}
    for name, value in laid.items():
        value = np.ascontiguousarray(value)
        arrays["in_" + name] = value
        args[name] = nc.dram_tensor("in_" + name, value.shape, mybir.dt.from_np(value.dtype), kind="ExternalInput").ap()
    out = nc.dram_tensor("out_x", (BATCH, SEQ, C), F32, kind="ExternalOutput").ap()
    block_net(nc, args, out)
    r = run_bass_kernel_spmd(nc, [arrays], core_ids=[0])
    return r.results[0]["out_x"]
```
